# Optimizing a Trainium2 kernel written in Bass

```python
import numpy as np
import jax
import jax.numpy as jnp

def _softmax(x, axis=-1):
    return jax.nn.softmax(x, axis=axis)

def _gelu(x):
    return jax.nn.gelu(x, approximate=True)

def _silu(x):
    return jax.nn.silu(x)

def _sigmoid(x):
    return jax.nn.sigmoid(x)

def _layernorm(x, axis=-1, eps=1e-05):
    m = jnp.mean(x, axis=axis, keepdims=True)
    v = jnp.var(x, axis=axis, keepdims=True)
    return (x - m) / jnp.sqrt(v + eps)

def _scatter_add(tgt, idx, src, axis=0):
    return tgt.at[idx].add(src)

def _segment_sum(src, seg, n):
    return jax.ops.segment_sum(src, seg, n)
kernel_name = 'mk_gnn_preln_d2_gnn_r64_43e970'

def setup_inputs(seed: int=0):
    np.random.seed(seed)
    _w = jnp.asarray

    def _rec_inputs():
        import jax
        import jax.numpy as jnp
        _gk = jax.random.key(seed)
        x = -0.000202 + 1 * jax.random.normal(jax.random.fold_in(_gk, 1), (50000, 128), jnp.float32)
        src = jax.random.randint(jax.random.fold_in(_gk, 2), (12500,), 0, 50000, jnp.int32)
        dst = jnp.minimum((50000 * jax.random.uniform(jax.random.fold_in(_gk, 3), (12500,)) ** 2.0).astype(jnp.int32), 49999)
        _o = jnp.argsort(dst, stable=True)
        src = src[_o]
        dst = dst[_o]
        edge_attr_3 = -0.000451519 + 1.00018 * jax.random.normal(jax.random.fold_in(_gk, 12), (12500, 3), jnp.float32)
        edge_weight = jax.random.uniform(jax.random.fold_in(_gk, 14), (12500,), jnp.float32, 0.0, 0.999998)
        return (x, src, dst, edge_attr_3, edge_weight)
    x, src, dst, edge_attr_3, edge_weight = _rec_inputs()

    def _L0_gnn_setup():
        import jax, jax.numpy as jnp
        import numpy as np
        N = 50000
        C = 128
        E = 12500
        STEPS = 3

        def _gru_cell(inp, h, W_ih, W_hh, b_ih, b_hh):
            gi = inp @ W_ih.T + b_ih
            gh = h @ W_hh.T + b_hh
            i_r, i_z, i_n = jnp.split(gi, 3, axis=-1)
            h_r, h_z, h_n = jnp.split(gh, 3, axis=-1)
            r = jax.nn.sigmoid(i_r + h_r)
            z = jax.nn.sigmoid(i_z + h_z)
            n = jnp.tanh(i_n + r * h_n)
            return (1.0 - z) * n + z * h
        key = jax.random.key(seed)
        ks = jax.random.split(key, 8)
        x = jax.random.normal(ks[0], (N, C), dtype=jnp.float32)
        edge_index = jax.random.randint(ks[1], (2, E), 0, N, dtype=jnp.int64)
        s = 1.0 / np.sqrt(C)
        W_lin = jax.random.uniform(ks[2], (C, C), jnp.float32, -s, s)
        W_ih = jax.random.uniform(ks[3], (3 * C, C), jnp.float32, -s, s)
        W_hh = jax.random.uniform(ks[4], (3 * C, C), jnp.float32, -s, s)
        b_ih = jax.random.uniform(ks[5], (3 * C,), jnp.float32, -s, s)
        b_hh = jax.random.uniform(ks[6], (3 * C,), jnp.float32, -s, s)
        return {'x': x, 'edge_index': edge_index, 'W_lin': W_lin, 'W_ih': W_ih, 'W_hh': W_hh, 'b_ih': b_ih, 'b_hh': b_hh}
    _L0_gnn_all = _L0_gnn_setup()
    _L0_gnn_in = {k: v for k, v in _L0_gnn_all.items() if k in ('W_lin', 'W_ih', 'W_hh', 'b_ih', 'b_hh')}
    del _L0_gnn_all

    def _L1_gnn_setup():
        import jax, jax.numpy as jnp
        import numpy as np
        N = 50000
        E = 12500
        MUL = 32
        NB = 8
        R_MAX = 1.0
        AVG = 16.0
        SQ3 = 3.0 ** 0.5

        def _radial_embedding(r):
            x = jnp.clip(r / R_MAX, 0.0, 1.0)
            centers = jnp.arange(NB, dtype=jnp.float32) / (NB - 1)
            sigma = 1.0 / (NB - 1)
            emb = jnp.exp(-0.5 * ((x[:, None] - centers[None, :]) / sigma) ** 2)
            emb = emb * NB ** 0.5 * (r <= R_MAX).astype(jnp.float32)[:, None]
            return emb
        key = jax.random.key(seed)
        k = jax.random.split(key, 12)
        inp = {'node_feats': jax.random.normal(k[0], (N, 4 * MUL), dtype=jnp.float32), 'edge_vec': jax.random.normal(k[1], (E, 3), dtype=jnp.float32), 'edge_length': jax.random.uniform(k[2], (E,), dtype=jnp.float32), 'senders': jax.random.randint(k[3], (E,), 0, N, dtype=jnp.int32), 'receivers': jax.random.randint(k[4], (E,), 0, N, dtype=jnp.int32), 'num_nodes': N, 'W_up0': jax.random.normal(k[5], (MUL, MUL), dtype=jnp.float32), 'W_up1': jax.random.normal(k[6], (MUL, MUL), dtype=jnp.float32), 'mlp_w0': jax.random.normal(k[7], (NB, 64), dtype=jnp.float32) / NB ** 0.5, 'mlp_b0': jnp.zeros((64,), dtype=jnp.float32), 'mlp_w1': jax.random.normal(k[8], (64, 64), dtype=jnp.float32) / 8.0, 'mlp_b1': jnp.zeros((64,), dtype=jnp.float32), 'mlp_w2': jax.random.normal(k[9], (64, 4 * MUL), dtype=jnp.float32) / 8.0, 'mlp_b2': jnp.zeros((4 * MUL,), dtype=jnp.float32), 'W_out0': jax.random.normal(k[10], (2 * MUL, MUL), dtype=jnp.float32), 'W_out1': jax.random.normal(k[11], (2 * MUL, MUL), dtype=jnp.float32)}
        return inp
    _L1_gnn_all = _L1_gnn_setup()
    _L1_gnn_in = {k: v for k, v in _L1_gnn_all.items() if k in ('W_up0', 'W_up1', 'mlp_w0', 'mlp_b0', 'mlp_w1', 'mlp_b1', 'mlp_w2', 'mlp_b2', 'W_out0', 'W_out1')}
    del _L1_gnn_all
    return {'x': x, 'src': src, 'dst': dst, 'edge_attr_3': edge_attr_3, 'edge_weight': edge_weight, 'L0_gnn_W_lin': _L0_gnn_in['W_lin'], 'L0_gnn_W_ih': _L0_gnn_in['W_ih'], 'L0_gnn_W_hh': _L0_gnn_in['W_hh'], 'L0_gnn_b_ih': _L0_gnn_in['b_ih'], 'L0_gnn_b_hh': _L0_gnn_in['b_hh'], 'L1_gnn_W_up0': _L1_gnn_in['W_up0'], 'L1_gnn_W_up1': _L1_gnn_in['W_up1'], 'L1_gnn_mlp_w0': _L1_gnn_in['mlp_w0'], 'L1_gnn_mlp_b0': _L1_gnn_in['mlp_b0'], 'L1_gnn_mlp_w1': _L1_gnn_in['mlp_w1'], 'L1_gnn_mlp_b1': _L1_gnn_in['mlp_b1'], 'L1_gnn_mlp_w2': _L1_gnn_in['mlp_w2'], 'L1_gnn_mlp_b2': _L1_gnn_in['mlp_b2'], 'L1_gnn_W_out0': _L1_gnn_in['W_out0'], 'L1_gnn_W_out1': _L1_gnn_in['W_out1']}

def reference(x, src, dst, edge_attr_3, edge_weight, L0_gnn_W_lin, L0_gnn_W_ih, L0_gnn_W_hh, L0_gnn_b_ih, L0_gnn_b_hh, L1_gnn_W_up0, L1_gnn_W_up1, L1_gnn_mlp_w0, L1_gnn_mlp_b0, L1_gnn_mlp_w1, L1_gnn_mlp_b1, L1_gnn_mlp_w2, L1_gnn_mlp_b2, L1_gnn_W_out0, L1_gnn_W_out1):
    import jax
    import jax.numpy as jnp

    def _L0_gnn_ref(x, edge_index, W_lin, W_ih, W_hh, b_ih, b_hh):
        import jax, jax.numpy as jnp
        import numpy as np
        N = 50000
        C = 128
        E = 12500
        STEPS = 3

        def _gru_cell(inp, h, W_ih, W_hh, b_ih, b_hh):
            gi = inp @ W_ih.T + b_ih
            gh = h @ W_hh.T + b_hh
            i_r, i_z, i_n = jnp.split(gi, 3, axis=-1)
            h_r, h_z, h_n = jnp.split(gh, 3, axis=-1)
            r = jax.nn.sigmoid(i_r + h_r)
            z = jax.nn.sigmoid(i_z + h_z)
            n = jnp.tanh(i_n + r * h_n)
            return (1.0 - z) * n + z * h
        src = edge_index[0]
        dst = edge_index[1]
        state = x
        for _ in range(STEPS):
            m = state @ W_lin.T
            msgs = jnp.take(m, src, axis=0)
            propagated = jax.ops.segment_sum(msgs, dst, num_segments=N)
            state = _gru_cell(propagated, state, W_ih, W_hh, b_ih, b_hh)
        return state

    def _L1_gnn_ref(node_feats, edge_vec, edge_length, senders, receivers, num_nodes, W_up0, W_up1, mlp_w0, mlp_b0, mlp_w1, mlp_b1, mlp_w2, mlp_b2, W_out0, W_out1):
        import jax, jax.numpy as jnp
        import numpy as np
        N = 50000
        E = 12500
        MUL = 32
        NB = 8
        R_MAX = 1.0
        AVG = 16.0
        SQ3 = 3.0 ** 0.5

        def _radial_embedding(r):
            x = jnp.clip(r / R_MAX, 0.0, 1.0)
            centers = jnp.arange(NB, dtype=jnp.float32) / (NB - 1)
            sigma = 1.0 / (NB - 1)
            emb = jnp.exp(-0.5 * ((x[:, None] - centers[None, :]) / sigma) ** 2)
            emb = emb * NB ** 0.5 * (r <= R_MAX).astype(jnp.float32)[:, None]
            return emb
        f32 = jnp.float32
        rhat = edge_vec / (jnp.linalg.norm(edge_vec, axis=-1, keepdims=True) + 1e-12)
        Y1 = SQ3 * rhat
        emb = _radial_embedding(edge_length)
        h = jax.nn.silu(emb @ mlp_w0 + mlp_b0)
        h = jax.nn.silu(h @ mlp_w1 + mlp_b1)
        w = (h @ mlp_w2 + mlp_b2).reshape(-1, 4, MUL)
        s = node_feats[:, :MUL]
        v = node_feats[:, MUL:].reshape(-1, MUL, 3)
        xs = s @ W_up0 / f32(MUL) ** 0.5
        xv = jnp.einsum('nmc,mk->nkc', v, W_up1) / f32(MUL) ** 0.5
        ss = xs[senders]
        vv = xv[senders]
        m0 = w[:, 0] * ss
        m1 = w[:, 1][:, :, None] * ss[:, :, None] * Y1[:, None, :]
        m2 = w[:, 2][:, :, None] * vv
        m3 = w[:, 3] * (jnp.einsum('emc,ec->em', vv, Y1) / SQ3)
        mid_s = jnp.concatenate([m0, m3], axis=1)
        mid_v = jnp.concatenate([m1, m2], axis=1)
        msg_s = jax.ops.segment_sum(mid_s, receivers, num_segments=num_nodes)
        msg_v = jax.ops.segment_sum(mid_v, receivers, num_segments=num_nodes)
        out_s = msg_s @ W_out0 / f32(2 * MUL) ** 0.5
        out_v = jnp.einsum('nmc,mk->nkc', msg_v, W_out1) / f32(2 * MUL) ** 0.5
        out = jnp.concatenate([out_s, out_v.reshape(-1, 3 * MUL)], axis=1)
        return out / max(AVG, 1e-08)
    edge_index = jnp.stack([src, dst])
    h = jnp.maximum(_layernorm(x, axis=-1), 0.0)
    x = x + _L0_gnn_ref(h, edge_index, L0_gnn_W_lin, L0_gnn_W_ih, L0_gnn_W_hh, L0_gnn_b_ih, L0_gnn_b_hh)
    h = jnp.maximum(_layernorm(x, axis=-1), 0.0)
    x = x + _L1_gnn_ref(h, edge_attr_3, edge_weight, src, dst, 50000, L1_gnn_W_up0, L1_gnn_W_up1, L1_gnn_mlp_w0, L1_gnn_mlp_b0, L1_gnn_mlp_w1, L1_gnn_mlp_b1, L1_gnn_mlp_w2, L1_gnn_mlp_b2, L1_gnn_W_out0, L1_gnn_W_out1)
    return x

_drawn_inputs = setup_inputs


def setup_inputs(seed=0):
    import zlib

    import numpy as np

    out = dict(_drawn_inputs(seed))
    spreads = {'L1_gnn_mlp_b0': (0.0, 0.8), 'L1_gnn_mlp_b1': (0.0, 0.8), 'L1_gnn_mlp_b2': (0.0, 0.8)}
    factors = {'edge_attr_3': 8.0,
     'edge_weight': 8.0,
     'L1_gnn_W_up0': 8.0,
     'L1_gnn_W_up1': 8.0,
     'L1_gnn_mlp_w0': 7.972,
     'L1_gnn_mlp_w1': 6.991,
     'L1_gnn_mlp_w2': 6.571,
     'L1_gnn_W_out0': 8.0,
     'L1_gnn_W_out1': 8.0}
    for name, (base, spread) in spreads.items():
        noise = np.random.default_rng([zlib.crc32(name.encode()), seed]).standard_normal(out[name].shape)
        drawn = base * np.exp(spread * noise) if base else spread * noise
        out[name] = jnp.asarray(drawn.astype(out[name].dtype))
    for name, factor in factors.items():
        out[name] = (out[name] * factor).astype(out[name].dtype)
    return out
```

```python
from contextlib import ExitStack

import numpy as np

import concourse.bass as bass
from concourse import mybir

F32 = mybir.dt.float32
BF16 = mybir.dt.bfloat16
I32 = mybir.dt.int32
ALU = mybir.AluOpType
ACT = mybir.ActivationFunctionType
AX = mybir.AxisListType

C = 128
TP = 125
TG = 4
G = TP * TG
LANES = 5
STEPS = 3
TE = TP + 2
NONE = 1 << 20
NB = 8
MUL = 32
HID = 64
EPS = 1e-5
LAG = 3
SPLIT = 112


class Ledger:

    def __init__(self, phases, turns, per, start=0):
        self.start, self.per = {}, per
        at = start
        for p in phases:
            self.start[p] = at
            at += turns * per.get(p, 0)
        self.total = at

    def at(self, phase, i, k=0):
        return i * self.per.get(phase, 0) + (self.start[phase] + k)


def gnn_kernel(nc, x, src, dst, edge_attr, edge_weight, W_lin, W_ih, W_hh, b_ih, b_hh, W_up0, W_up1,
               mlp_w0, mlp_b0, mlp_w1, mlp_b1, mlp_w2, mlp_b2, W_out0, W_out1, out):
    N = x.shape[0]
    E = src.shape[0]
    NG, EG, ET = N // G, E // G, E // TP
    assert x.shape[1] == C and N % G == 0 and E % G == 0 and EG % LANES == 0
    TURNS = EG // LANES
    assert NG == 4 * TURNS * LANES
    ROUNDS = STEPS + 1
    PHASES = ["W", "S"] + [f"{a}{r}" for r in range(ROUNDS) for a in "MD"]
    CELLS = STEPS * LANES
    free = ["S"] + [f"M{r}" for r in range(ROUNDS)]
    slot = [f"D{r}" for r in range(STEPS)]

    def ledger(start=0, **per):
        return Ledger(PHASES, TURNS, per, start)

    cell = ledger(1, **{p: CELLS for p in free}, **{p: LANES for p in slot})
    tin_per = {"S": LANES, "D3": LANES, "M3": 3 * LANES}
    tin_per |= {f"M{r}": 2 * LANES for r in range(STEPS)} | {p: 3 * LANES for p in slot}
    tin = ledger(1, **tin_per)
    for r in range(ROUNDS):
        for p in PHASES[PHASES.index(f"D{r}"):]:
            tin.start[p] += 1
    tout = ledger(1, S=CELLS, **{f"M{r}": LANES for r in range(ROUNDS)}, **{p: LANES for p in slot}, D3=LANES)

    with ExitStack() as ctx:
        def sb(name, shape, dt=F32):
            return ctx.enter_context(nc.sbuf_tensor(name, shape, dt))

        def lanes(name, shape, dt=F32):
            return [sb(f"{name}{l}", shape, dt) for l in range(LANES)]

        def bank(name):
            return ctx.enter_context(nc.psum_tensor(name, [C, 512], F32))

        def sem(name):
            return ctx.enter_context(nc.semaphore(name))

        def sems(name):
            return [sem(f"{name}{l}") for l in range(LANES)]

        def dram(name, shape, dt=F32):
            return nc.dram_tensor(name, shape, dt).ap()

        src_s = dram("src_sorted", [E], I32)
        dst_pad = dram("dst_sorted", [E + 1], I32)
        dst_s = dst_pad[1:E + 1]
        weight_s = dram("weight_sorted", [E])
        attr_s = dram("attr_sorted", [E, 3])
        late_col = dram("late_col", [TP])
        ranks = dram("ranks", [2, TP, ET], I32)
        slot_of_node = dram("slot_of_node", [N, 1], I32)
        idx_src = dram("idx_src", [EG, TP, TG], I32)
        idx_dst = dram("idx_dst", [EG, TP, TG], I32)
        idx_first = dram("idx_first", [EG, TP, TG], I32)
        idx_slot = dram("idx_slot", [EG, TP, TG], I32)
        edge_id = dram("edge_id", [EG, TP, TG], I32)
        dst_col = dram("dst_col", [EG, TP, TG])
        dst_rows = dram("dst_rows", [EG, G])
        mask_keys = dram("mask_keys", [EG, TG * TE])
        tile_masks = dram("tile_masks", [EG, TP, TG * TE])
        key_masks = dram("key_masks", [EG, ET, 2 * G], BF16)
        emb_d = dram("emb", [NB, E])
        rhat_d = dram("rhat", [3, E])
        conv_d = dram("conv_factors", [EG, C, 3 * G])
        src_rows = [dram(f"src_rows{r}", [E, C]) for r in range(ROUNDS)]
        slot_rows = [None] + [dram(f"slot_rows{r}", [E, C]) for r in range(1, ROUNDS)]
        dst_x = dram("dst_x", [E, C])
        sums_d = dram("sums", [EG, C, TG * TE])

        x_dense = x.rearrange("(g p j) c -> g p j c", p=TP, j=TG)
        out_dense = out.rearrange("(g p j) c -> g p j c", p=TP, j=TG)

        def by_tile(rows):
            return rows.rearrange("(g j p) c -> g p j c", p=TP, j=TG)

        ident = sb("ident", [C, C])
        w_raw = sb("w_raw", [C, 6, C])
        w_lin = sb("w_lin", [C, C])
        w_ihT = sb("w_ihT", [C, 3, C])
        w_hT = sb("w_hT", [C, 3, C])
        w_pT = sb("w_pT", [C, 3, C])
        bias = sb("bias", [C, 9])
        up = sb("up", [C, C])
        upss = sb("upss", [C, 96])
        mw0 = sb("mw0", [NB, HID])
        mw1 = sb("mw1", [HID, C])
        mw2 = sb("mw2", [HID, 4 * MUL])
        mw2x = sb("mw2x", [HID, 3, C])
        mb = sb("mb", [HID, 2])
        mb2 = sb("mb2", [C, 3])
        sel3 = sb("sel3", [3, 96])
        wo = sb("wo", [C, 3, C])
        part = sb("part", [C, ET * 2])
        keys = sb("keys", [ET, 2])
        bsum = sb("bsum", [ET, 3, 2 * C], BF16)
        brest = sb("brest", [ET, 2 * C])
        xa_xn = sb("xa_xn", [TP, 2 * LANES, TG, C])
        mm_on = sb("mm_on", [TP, 2 * LANES, TG, C])
        xa, xn, mm, on = ([t[:, k * LANES + l] for l in range(LANES)] for t in (xa_xn, mm_on) for k in range(2))
        hT = lanes("hT", [C, G])
        rT = lanes("rT", [C, G])
        zT = lanes("zT", [C, G])
        nT = lanes("nT", [C, G])
        tT = lanes("tT", [C, G])
        pt = lanes("pt", [C, TG * TE])
        pf = lanes("pf", [C, G])
        mk = lanes("mk", [TP, TG * TE])
        rm = lanes("rm", [ET, 2 * G], BF16)
        cc = lanes("cc", [C, 3 * G])
        ix = lanes("ix", [TP, TG], I32)
        jx = lanes("jx", [TP, TG], I32)
        dc = lanes("dc", [TP, TG])
        stats = lanes("stats", [TP, TG, 6])
        mv = lanes("mv", [TP, TG, 2])
        veps = lanes("veps", [TP, TG])
        minus_half = sb("minus_half", [TP, TG])
        half = sb("half", [TP, ET])
        rstd = lanes("rstd", [TP, TG])

        NCH = 10
        CH = E // NCH
        assert E % NCH == 0 and NB * NCH <= C and CH <= 3 * G
        wbc, emb_t, etmp = (cc[k][0:NB * NCH, 0:CH] for k in range(3))
        ic = [sb(f"ic{k}", [TP, ET], I32) for k in range(3)]
        ifirst, eid = sb("ifirst", [TP, ET], I32), sb("eid", [TP, ET], I32)
        dcf, dpf, deq, dfi = (sb(n, [TP, ET]) for n in ("dcf", "dpf", "deq", "dfi"))
        drow_i = sb("drow_i", [ET, TP], I32)
        drow, eqf, eql = (sb(n, [ET, TP]) for n in ("drow", "eqf", "eql"))
        ext = sb("ext", [ET, TE])
        none_t = sb("none_t", [TP, N // TP], I32)
        minus1 = sb("minus1", [1, 1], I32)
        attr_t = sb("attr_t", [TP, 3 * ET])
        asq = sb("asq", [TP, 3 * ET])
        rh = sb("rh", [TP, 3, ET])
        nrm, inv = sb("nrm", [TP, ET]), sb("inv", [TP, ET])
        etmp2 = cc[3][0:NB * NCH, 0:CH]
        cen_i, cen = sb("cen_i", [NB * NCH, 1], I32), sb("cen", [NB * NCH, 1])
        seq_i = [sb(f"seq_i{k}", [TP, ET], I32) for k in range(2)]
        seq, late, edge_f, dst_f = (sb(n, [TP, ET]) for n in ("seq", "late", "edge_f", "dst_f"))
        late_p, late_row, late_any = sb("late_p", [TP, 1]), sb("late_row", [1, TP]), sb("late_any", [1, 1])
        late_i, rank_i = sb("late_i", [1, 1], I32), sb("rank_i", [TP, ET], I32)
        RCH = 50
        assert E % RCH == 0 and ET * RCH <= 2 * LANES * TG * C
        other_i, other, other_d = sb("other_i", [TP, RCH], I32), sb("other", [TP, RCH]), sb("other_d", [TP, RCH])
        compared, counted = (t[:, :, :, :].rearrange("p a j c -> p (a j c)")[:, 0:ET * RCH].rearrange(
            "p (t f) -> p t f", f=RCH) for t in (xa_xn, mm_on))
        move_rank = sb("move_rank", [TP, 2, TG], I32)
        move_src, move_dst = (sb(n, [TP, TG], I32) for n in ("move_src", "move_dst"))
        move_w, move_attr = sb("move_w", [TP, TG]), sb("move_attr", [TP, TG, 3])
        N_SET = 3 + 3 + 4 + 10 + 1 + 6 + 1 + 9
        N_IDX = 4 + NCH + 1
        N_TAB = 5 + 2 + 3 + NCH

        gate = [[bank(f"{g}{s}") for g in "rnz"] for s in range(2)]
        ti, to = bank("ti"), bank("to")

        s_settle = sem("settled")
        s_seq = sem("edge_order_loaded")
        s_late = sem("edge_order_moved")
        v_late = sem("edge_order_found")
        s_copied = sem("edges_copied")
        s_order = sem("edges_sorted")
        s_ranks = sem("ranks_stored")
        s_other, s_move, s_moved = sem("others_loaded"), sem("unsorted_loaded"), sem("edges_moved")
        s_set = sem("setup_loaded")
        s_id = sem("ident_steps")
        s_cst = sem("pool_constants")
        s_wt = sem("weights_transposed")
        s_wc = sem("weights_copied")
        s_idx = sem("index_steps_loaded")
        s_prep = sem("tables_ready")
        s_tab = sem("tables_stored")
        s_exp_a, s_exp = sem("exp_done"), sem("radial_ready")
        s_vs = sem("vector_setup")
        chain = sem("vector_chain")
        pchain = sem("pool_chain")
        g_r, g_n, g_z = sem("gate_r_summed"), sem("gate_n_summed"), sem("gate_z_summed")
        a_r, a_n, a_z = sem("r_ready"), sem("n_ready"), sem("z_ready")
        v_t, v_h = sem("t_ready"), sem("state_ready")
        s_ti, s_tif = sem("ti_full"), sem("ti_free")
        s_to, s_tof = sem("to_full"), sem("to_free")
        s_ln = sem("normed")
        v_var, p_rs = sem("variances"), sem("rstd_ready")
        v_sq, p_nrm = sem("edge_squares"), sem("edge_norms")
        s_h0 = sem("first_rows_ready")
        s_pf = sem("pf_ready")
        ld_x, ld_m, ld_k, ld_i, ld_j = sems("ld_x"), sems("ld_m"), sems("ld_k"), sems("ld_i"), sems("ld_j")
        ld_p, ld_r, ld_b, ld_c, ld_w = sems("ld_p"), sems("ld_r"), sems("ld_b"), sems("ld_c"), sems("ld_w")
        gx, gj, gm = sems("gather_x"), sems("gather_slot"), sems("gather_rows")
        st_o, st_j, st_p, st_x, st_w = sems("st_o"), sems("st_j"), sems("st_p"), sems("st_x"), sems("st_w")
        sc = sems("scattered")
        pA, pB, pC = sem("mlp1_summed"), sem("mlp2_summed"), sem("factors_summed")
        aA, aB, aC = sem("mlp1_sigmoid"), sem("mlp2_sigmoid"), sem("factors_copied")
        vA, vB, vC = sem("mlp1_ready"), sem("mlp2_ready"), sem("factors_ready")
        v_m = sem("masks_ready")
        s_bt, s_bh, s_br, s_bm, s_bl = (sem("bnd_T"), sem("bnd_hi"), sem("bnd_rest"), sem("bnd_mid"),
                                        sem("bnd_lo"))
        s_up = sem("conv_up")
        s_pr = sem("conv_products")
        s_cn = sem("conv_rows")
        s_cf = sem("conv_rows_copied")

        Ms = [f"M{r}" for r in range(ROUNDS)]
        Ds = [f"D{r}" for r in range(ROUNDS)]
        n_x = ledger(**{"S": 0}, **{p: 2 for p in Ms})
        n_m = ledger(**{p: 1 for p in Ms}, **{p: 1 for p in Ds[1:]})
        n_k = ledger(**{p: 1 for p in Ms})
        n_i = ledger(W=1, S=1, D0=1, D3=1)
        n_j = ledger(W=1, **{p: 1 for p in Ms[1:]})
        n_p = ledger(**{p: 1 for p in Ds})
        n_b = ledger(D2=1)
        n_c = ledger(M3=1)
        n_gx = ledger(S=TG, D0=TG)
        n_gj = ledger(S=TG)
        n_gm = ledger(**{p: TG for p in Ms[1:]})
        n_sto = ledger(W=1, S=4, **{p: 2 for p in Ms}, D0=1, D1=1, D2=1)
        n_stj = ledger(S=1)
        n_stp = ledger(**{p: 1 for p in Ms})
        n_ln = ledger(S=LANES, **{p: LANES for p in Ms[:3]}, M3=2 * LANES, D0=LANES)
        n_w = ledger(W=5)
        n_stw = ledger(W=2)
        n_lane = ledger(W=LANES)
        primed = ledger(1, W=LANES)
        n_pf = ledger(**{p: LANES for p in Ds})
        n_cv = ledger(M3=LANES)
        n_scat = ledger(W=TG, D3=TG)

        block = ctx.enter_context(nc.Block())

        def settle(eng):
            eng.sem_inc(s_settle, 1)

        def flat(rows):
            return rows[:, :, :].rearrange("p j c -> p (j c)")

        @block.sync
        def _(sp):
            def rows_in(buf, view, g, s):
                sp.dma_start(buf[0:SPLIT], view[g, 0:SPLIT]).then_inc(s, 16)
                sp.dma_start(buf[SPLIT:TP], view[g, SPLIT:TP]).then_inc(s, 16)

            with nc.allow_non_contiguous_dma(reason="short rows"):
                sp.dma_start(seq_i[0][:, :], dst.rearrange("(p q) -> p q", p=TP)).then_inc(s_seq, 16)
                sp.wait_ge(s_cst, 1)
                sp.dma_start(seq_i[1][0:TP - 1, :], dst[1:E - ET + 1].rearrange("(p q) -> p q", p=TP - 1)).then_inc(s_seq, 16)
                sp.dma_start(seq_i[1][TP - 1:TP, 0:ET - 1], dst[E - ET + 1:E].rearrange("(p q) -> p q", p=1)).then_inc(s_seq, 16)
            sp.dma_start(dst_pad[0:1].rearrange("(a b) -> a b", a=1), minus1[0:1, 0:1]).then_inc(s_copied, 16)
            sp.dma_start(dst_s, dst).then_inc(s_copied, 16)
            sp.dma_start(src_s, src).then_inc(s_copied, 16)
            sp.dma_start(weight_s, edge_weight).then_inc(s_copied, 16)
            sp.dma_start(attr_s, edge_attr).then_inc(s_copied, 16)
            sp.dma_start(slot_of_node.rearrange("(p q) o -> p (q o)", p=TP), none_t[:, :]).then_inc(s_copied, 16)

            sp.wait_ge(v_late, 1)
            with nc.allow_non_contiguous_dma(reason="a column"):
                sp.dma_start(late_col.rearrange("(p o) -> p o", o=1), late_p[:, :]).then_inc(s_late, 16)
            sp.wait_ge(s_late, 16)
            sp.dma_start(late_row[:, :], late_col.rearrange("(o p) -> o p", o=1)).then_inc(s_late, 16)

            for k, w in enumerate((W_ih, W_hh)):
                sp.dma_start(w_raw[:, 3 * k:3 * k + 3, :], w.rearrange("(g o) i -> o g i", g=3)).then_inc(s_set, 16)
            sp.dma_start(w_lin[:, :], W_lin).then_inc(s_set, 16)
            sp.dma_start(mw0[:, :], mlp_w0).then_inc(s_set, 16)
            sp.dma_start(mw2[:, :], mlp_w2).then_inc(s_set, 16)
            with nc.allow_non_contiguous_dma(reason="short columns"):
                for k, b in enumerate((b_ih, b_hh)):
                    sp.dma_start(bias[:, 3 * k:3 * k + 3], b.rearrange("(g p) -> p g", g=3)).then_inc(s_set, 16)
                for k, b in enumerate((mlp_b0, mlp_b1)):
                    sp.dma_start(mb[:, k:k + 1], b.rearrange("(p o) -> p o", o=1)).then_inc(s_set, 16)
                sp.wait_ge(s_cst, 1)
                for k, blocks in enumerate(((0, 2, 2, 2), (1, 1, 1), (3, 3, 3))):
                    for q, b in enumerate(blocks):
                        sp.dma_start(mb2[q * MUL:(q + 1) * MUL, k:k + 1],
                                     mlp_b2[b * MUL:(b + 1) * MUL].rearrange("(p o) -> p o", o=1)).then_inc(s_set, 16)
                sp.dma_start(mw1[:, 0:HID], mlp_w1).then_inc(s_set, 16)
                sp.dma_start(up[0:MUL, 0:MUL], W_up0).then_inc(s_set, 16)
                for c in range(3):
                    sp.dma_start(upss[0:MUL, c * MUL:(c + 1) * MUL], W_up0).then_inc(s_set, 16)
                    sp.dma_start(up[MUL + c:MUL + c + 3 * (MUL - 1) + 1:3, MUL + c * MUL:MUL + (c + 1) * MUL],
                                 W_up1).then_inc(s_set, 16)
                sp.dma_start(wo[0:MUL, 0, 0:MUL], W_out0[0:MUL, :]).then_inc(s_set, 16)
                for c in range(3):
                    cols = slice(MUL + c, MUL + c + 3 * (MUL - 1) + 1, 3)
                    sp.dma_start(wo[MUL + c * MUL:2 * MUL + c * MUL, 0, cols], W_out1[MUL:2 * MUL, :]).then_inc(s_set, 16)
                    sp.dma_start(wo[c * MUL:(c + 1) * MUL, 1, cols], W_out1[0:MUL, :]).then_inc(s_set, 16)
                    sp.dma_start(wo[c * MUL:(c + 1) * MUL, 2, 0:MUL], W_out0[MUL:2 * MUL, :]).then_inc(s_set, 16)

            sp.wait_ge(s_order, 1)
            with nc.allow_non_contiguous_dma(reason="index columns"):
                for k, a in enumerate((src_s, dst_s, dst_pad[0:E])):
                    sp.dma_start(ic[k][:, :], a.rearrange("(t p) -> p t", p=TP)).then_inc(s_idx, 16)
            sp.dma_start(drow_i[:, :], dst_s.rearrange("(t p) -> t p", p=TP)).then_inc(s_idx, 16)
            for q in range(NCH):
                sp.dma_start(wbc[q * NB:(q + 1) * NB, :],
                             weight_s[q * CH:(q + 1) * CH].partition_broadcast(NB)).then_inc(s_idx, 16)
            sp.dma_start(attr_t[:, :], attr_s.rearrange("(p q) c -> p (q c)", p=TP)).then_inc(s_idx, 16)

            sp.wait_ge(s_prep, 1)
            tabs = [(idx_src, ic[0]), (idx_dst, ic[1]), (idx_first, ifirst), (edge_id, eid), (dst_col, dcf)]
            with nc.allow_non_contiguous_dma(reason="index columns"):
                for d, s_ in tabs:
                    sp.dma_start(d.rearrange("g p j -> p g j"), s_[:, :].rearrange("p (g j) -> p g j", j=TG)).then_inc(s_tab, 16)
            sp.dma_start(dst_rows.rearrange("g (j p) -> (g j) p", p=TP), drow[:, :]).then_inc(s_tab, 16)
            sp.dma_start(mask_keys.rearrange("g (j e) -> (g j) e", e=TE), ext[:, :]).then_inc(s_tab, 16)
            for c in range(3):
                sp.dma_start(rhat_d[c].rearrange("(p q) -> p q", p=TP), rh[:, c, :]).then_inc(s_tab, 16)
            sp.wait_ge(s_exp, 1)
            for q in range(NCH):
                sp.dma_start(emb_d[:, q * CH:(q + 1) * CH], emb_t[q * NB:(q + 1) * NB, :]).then_inc(s_tab, 16)
            sp.wait_ge(s_tab, 16 * N_TAB)

            with sp.Fori(0, TURNS) as i:
                for l in range(LANES):
                    g = i * LANES + l
                    sp.dma_start(pt[l][0:TP, :], mask_keys[g].partition_broadcast(TP)).then_inc(ld_w[l], 16)
                    sp.dma_start(pf[l][0:ET, :], dst_rows[g].partition_broadcast(ET)).then_inc(ld_w[l], 16)
                    sp.dma_start(dc[l][:, :], dst_col[g]).then_inc(ld_w[l], 16)
                    sp.dma_start(tT[l][0:NB, :], emb_d[:, bass.ds(g * G, G)]).then_inc(ld_w[l], 16)
                    sp.dma_start(hT[l][0:3, :], rhat_d[:, bass.ds(g * G, G)]).then_inc(ld_w[l], 16)
                    sp.dma_start(ix[l][:, :], idx_first[g]).then_inc(ld_i[l], 16)
                    sp.dma_start(jx[l][:, :], edge_id[g]).then_inc(ld_j[l], 16)
                for l in range(LANES):
                    g = i * LANES + l
                    sp.wait_ge(v_m, n_lane.at("W", i, l + 1))
                    sp.dma_start(tile_masks[g], mk[l][:, :]).then_inc(st_w[l], 16)
                    sp.dma_start(key_masks[g], rm[l][:, :]).then_inc(st_w[l], 16)
                    sp.wait_ge(vC, primed.at("W", i, l + 1))
                    sp.wait_ge(aC, primed.at("W", i, l + 1))
                    sp.dma_start(conv_d[g], cc[l][:, :]).then_inc(st_o[l], 16)
                for l in range(LANES):
                    sp.wait_ge(st_w[l], 16 * n_stw.at("W", i, 2))
                    sp.wait_ge(st_o[l], 16 * n_sto.at("W", i, 1))
                    sp.wait_ge(sc[l], 16 * n_scat.at("W", i, TG))
                settle(sp)

            with sp.Fori(0, TURNS) as i:
                for l in range(LANES):
                    sp.dma_start(ix[l][:, :], idx_src[i * LANES + l]).then_inc(ld_i[l], 16)
                for l in range(LANES):
                    sp.wait_ge(gx[l], 16 * n_gx.at("S", i, TG))
                    sp.wait_ge(gj[l], 16 * n_gj.at("S", i, TG))
                    sp.dma_start(idx_slot[i * LANES + l], jx[l][:, :]).then_inc(st_j[l], 16)
                for l in range(LANES):
                    sp.wait_ge(s_h0, i * LANES + (l + 1))
                    sp.dma_start(by_tile(src_rows[0])[i * LANES + l], on[l][:, :, :]).then_inc(st_o[l], 16)
                for s in range(STEPS):
                    for l in range(LANES):
                        sp.wait_ge(s_tof, tout.at("S", i, s * LANES + l + 1))
                        sp.dma_start(by_tile(src_rows[s + 1])[i * LANES + l], on[l][:, :, :]).then_inc(st_o[l], 16)
                for l in range(LANES):
                    sp.wait_ge(st_j[l], 16 * n_stj.at("S", i, 1))
                settle(sp)
            for l in range(LANES):
                rows_in(xa[l], x_dense, l, ld_x[l])
                sp.wait_ge(st_o[l], 16 * n_sto.start["M0"])

            for r in range(ROUNDS):
                M, D = f"M{r}", f"D{r}"
                def dense_turn(i, last):
                    for l in range(LANES):
                        g = i * LANES + l
                        sp.wait_ge(s_tif, tin.at(M, i))
                        sp.dma_start(mm[l][:, :, :], by_tile(src_rows[r])[g]).then_inc(ld_m[l], 16)
                        sp.dma_start(mk[l][:, :], tile_masks[g]).then_inc(ld_k[l], 16)
                        if r:
                            sp.dma_start(jx[l][:, :], idx_slot[g]).then_inc(ld_j[l], 16)
                        if r == STEPS:
                            sp.dma_start(cc[l][:, :], conv_d[g]).then_inc(ld_c[l], 16)
                    for l in range(LANES):
                        w = sp.snap(i * LANES + (r * TURNS * LANES + l))
                        sp.wait_ge(s_tof, tout.at(M, i, l + 1))
                        settle(sp)
                        sp.dma_start(out_dense[w, 0:SPLIT], on[l][0:SPLIT]).then_inc(st_o[l], 16)
                        sp.dma_start(out_dense[w, SPLIT:TP], on[l][SPLIT:TP]).then_inc(st_o[l], 16)
                        if not last:
                            rows_in(xa[l], x_dense, w + LANES, ld_x[l])
                    for l in range(LANES):
                        sp.wait_ge(s_tif, tin.at(M, i, (2 * LANES if r == STEPS else LANES) + l + 1))
                        sp.dma_start(sums_d[i * LANES + l], pt[l][:, :]).then_inc(st_p[l], 16)
                    for l in range(LANES):
                        sp.wait_ge(st_p[l], 16 * n_stp.at(M, i, 1))
                    settle(sp)

                if r < STEPS:
                    with sp.Fori(0, TURNS) as i:
                        dense_turn(i, False)
                else:
                    with sp.Fori(0, TURNS - 1) as i:
                        dense_turn(i, False)
                    dense_turn(TURNS - 1, True)
                for l in range(LANES):
                    if r == STEPS:
                        sp.wait_ge(st_o[l], 16 * n_sto.at(M, TURNS))
                with sp.Fori(0, TURNS) as i:
                    for l in range(LANES):
                        g = i * LANES + l
                        if r < STEPS:
                            sp.wait_ge(v_h, cell.at(D, i))
                        else:
                            sp.wait_ge(s_tof, tout.at(D, i))
                            settle(sp)
                            sp.wait_ge(s_tif, tin.at(D, i))
                        sp.dma_start(pt[l][:, :], sums_d[g]).then_inc(ld_p[l], 16)
                        sp.dma_start(rm[l][:, :], key_masks[g]).then_inc(ld_r[l], 16)
                        if r == 0:
                            sp.dma_start(ix[l][:, :], idx_dst[g]).then_inc(ld_i[l], 16)
                        else:
                            sp.dma_start(mm[l][:, :, :], by_tile(slot_rows[r])[g]).then_inc(ld_m[l], 16)
                        if r == 2:
                            sp.dma_start(xn[l][:, :, :], by_tile(dst_x)[g]).then_inc(ld_b[l], 16)
                        if r == STEPS:
                            sp.dma_start(ix[l][:, :], idx_first[g]).then_inc(ld_i[l], 16)
                    if r == 0:
                        for l in range(LANES):
                            sp.wait_ge(gx[l], 16 * n_gx.at(D, i, TG))
                            sp.dma_start(by_tile(dst_x)[i * LANES + l], mm[l][:, :, :]).then_inc(st_x[l], 16)
                    if r < STEPS:
                        for l in range(LANES):
                            sp.wait_ge(s_tof, tout.at(D, i, l + 1))
                            sp.dma_start(by_tile(slot_rows[r + 1])[i * LANES + l], on[l][:, :, :]).then_inc(st_o[l], 16)
                    else:
                        for l in range(LANES):
                            sp.wait_ge(sc[l], 16 * n_scat.at(D, i, TG))
                        settle(sp)
                if r < STEPS:
                    for l in range(LANES):
                        sp.wait_ge(st_o[l], 16 * n_sto.at(D, TURNS))
                        if r == 0:
                            sp.wait_ge(st_x[l], 16 * TURNS)
            for l in range(LANES):
                sp.wait_ge(sc[l], 16 * n_scat.total)

        @block.gpsimd
        def _(pool):
            steps = [0]

            def link(ins):
                steps[0] += 1
                ins.then_inc(pchain, 1)
                pool.wait_ge(pchain, steps[0])

            pool.memset(seq_i[1][:, :], NONE)
            pool.memset(up[:, :], 0.0)
            pool.memset(mw1[:, :], 0.0)
            pool.memset(upss[:, :], 0.0)
            pool.memset(wo[:, :, :], 0.0)
            pool.memset(mb2[:, :], 0.0)
            pool.memset(minus1[:, :], -1)
            pool.memset(minus_half[:, :], -0.5)
            pool.memset(half[:, :], 0.5)
            pool.memset(none_t[:, :], NONE).then_inc(s_cst, 1)
            pool.iota(eid[:, :], pattern=[[TP, ET]], base=0, channel_multiplier=1).then_inc(s_id, 1)
            pool.iota(cen_i[:, :], pattern=[[1, 1]], base=0, channel_multiplier=1).then_inc(s_id, 1)
            link(pool.memset(ident[:, :], 0.0))
            pool.affine_select(out=ident[:, :], in_=ident[:, :], compare_op=ALU.not_equal, fill=1.0,
                               base=0, pattern=[[-1, C]], channel_multiplier=1).then_inc(s_id, 1)
            link(pool.memset(sel3[:, :], 1.0))
            link(pool.affine_select(out=sel3[:, :], in_=sel3[:, :], compare_op=ALU.is_ge, fill=0.0,
                                    base=0, pattern=[[1, 96]], channel_multiplier=-MUL))
            pool.affine_select(out=sel3[:, :], in_=sel3[:, :], compare_op=ALU.is_ge, fill=0.0,
                               base=MUL - 1, pattern=[[-1, 96]], channel_multiplier=MUL).then_inc(s_id, 1)

            last_node, last_slot = N - 1, E - 1

            def sort_edges():
                steps[0] = 0
                pool.sem_clear(pchain)
                link(pool.tensor_copy(dst_f[:, :], seq_i[0][:, :]))
                link(pool.tensor_tensor(dst_f[:, :], dst_f[:, :], dst_f[:, :], ALU.add))
                link(pool.iota(seq_i[1][:, :], pattern=[[1, ET]], base=0, channel_multiplier=ET))
                link(pool.tensor_copy(edge_f[:, :], seq_i[1][:, :]))
                link(pool.iota(other_i[:, :], pattern=[[1, RCH]], base=0, channel_multiplier=0))
                link(pool.tensor_copy(other[:, :], other_i[:, :]))
                link(pool.memset(counted, 0.0))
                whole = [TP, ET, RCH]
                by_edge = [t[:, :].unsqueeze(2).broadcast_to(whole) for t in (edge_f, dst_f)]
                by_other = [t[:, :].unsqueeze(1).broadcast_to(whole) for t in (other, other_d)]
                with pool.Fori(0, E // RCH) as q:
                    steps[0] = 0
                    pool.sem_clear(pchain)
                    pool.dma_start(other_i[:, :], dst[bass.ds(q * RCH, RCH)].partition_broadcast(TP)).then_inc(s_other, 16)
                    pool.wait_ge(s_other, 16 * (q + 1))
                    settle(pool)
                    link(pool.tensor_copy(other_d[:, :], other_i[:, :]))
                    link(pool.tensor_tensor(other_d[:, :], other_d[:, :], other_d[:, :], ALU.add))
                    link(pool.tensor_tensor(compared, by_edge[0], by_other[0], ALU.subtract))
                    link(pool.tensor_scalar(compared, compared, 0.0, 1.0, ALU.max, ALU.min))
                    link(pool.tensor_tensor(compared, by_other[1], compared, ALU.subtract))
                    link(pool.tensor_tensor(compared, by_edge[1], compared, ALU.subtract))
                    link(pool.tensor_scalar(compared, compared, 0.0, 1.0, ALU.max, ALU.min))
                    link(pool.tensor_tensor(counted, counted, compared, ALU.add))
                    link(pool.tensor_scalar(other[:, :], other[:, :], float(RCH), None, ALU.add))
                w = RCH
                while w > 1:
                    half_w = w // 2
                    link(pool.tensor_tensor(counted[:, :, 0:half_w], counted[:, :, 0:half_w],
                                            counted[:, :, w - half_w:w], ALU.add))
                    w -= half_w
                for k in range(2):
                    link(pool.tensor_scalar(seq[:, :], counted[:, :, 0], float(k), None, ALU.add))
                    link(pool.tensor_copy(rank_i[:, :], seq[:, :]))
                    pool.dma_start(ranks[k], rank_i[:, :]).then_inc(s_ranks, 16)
                    pool.wait_ge(s_ranks, 16 * (k + 1))
                with pool.Fori(0, EG) as g:
                    def part_of(a):
                        return a.rearrange("(p g j) -> g p j", p=TP, j=TG)[g]

                    for k in range(2):
                        pool.dma_start(move_rank[:, k, :], ranks[k].rearrange("p (g j) -> g p j", j=TG)[g]).then_inc(s_move, 16)
                    with nc.allow_non_contiguous_dma(reason="index columns"):
                        pool.dma_start(move_src[:, :], part_of(src)).then_inc(s_move, 16)
                        pool.dma_start(move_dst[:, :], part_of(dst)).then_inc(s_move, 16)
                        pool.dma_start(move_w[:, :], part_of(edge_weight)).then_inc(s_move, 16)
                        pool.dma_start(move_attr[:, :, :], edge_attr.rearrange("(p g j) c -> g p j c", p=TP, j=TG)[g]).then_inc(s_move, 16)
                    pool.wait_ge(s_move, 16 * 6 * (g + 1))
                    settle(pool)
                    for j in range(TG):
                        places = [move_rank[:, k, j:j + 1] for k in range(2)]
                        for sorted_, edges, k in ((src_s, move_src, 0), (dst_pad, move_dst, 1), (weight_s, move_w, 0)):
                            scatter(sorted_.rearrange("(e o) -> e o", o=1), edges[:, j:j + 1], places[k], s_moved,
                                    last_slot + k)
                        scatter(attr_s, move_attr[:, j, :], places[0], s_moved, last_slot)
                    pool.wait_ge(s_moved, 16 * 4 * TG * (g + 1))
                    settle(pool)

            def gather(rows, table, index, s, bound):
                pool.indirect_dma_start(
                    out=rows, out_offset=None, in_=table,
                    in_offset=bass.IndirectOffsetOnAxis(ap=index, axis=0),
                    bounds_check=bound, oob_is_err=False).then_inc(s, 16)

            def scatter(table, rows, index, s, bound):
                pool.indirect_dma_start(
                    out=table, out_offset=bass.IndirectOffsetOnAxis(ap=index, axis=0),
                    in_=rows, in_offset=None, bounds_check=bound, oob_is_err=False).then_inc(s, 16)

            pool.wait_ge(v_late, 2)
            pool.wait_ge(s_copied, 16 * 6)
            unsorted = pool.value_load(late_i[0:1, 0:1], min_val=0, max_val=1)
            with pool.If(unsorted != 0):
                sort_edges()
            pool.sem_inc(s_order, 1)

            pool.wait_ge(v_sq, 1)
            pool.tensor_tensor(nrm[:, :], nrm[:, :], half[:, :], ALU.pow).then_inc(p_nrm, 1)

            def rstds(ph, i, u, l):
                pool.wait_ge(v_var, n_ln.at(ph, i, u + 1))
                pool.tensor_tensor(rstd[l][:, :], veps[l][:, :], minus_half[:, :], ALU.pow).then_inc(p_rs, 1)

            with pool.Fori(0, TURNS) as i:
                for l in range(LANES):
                    pool.wait_ge(ld_i[l], 16 * n_i.at("W", i, 1))
                    pool.wait_ge(ld_j[l], 16 * n_j.at("W", i, 1))
                    settle(pool)
                    for j in range(TG):
                        scatter(slot_of_node, jx[l][:, j:j + 1], ix[l][:, j:j + 1], sc[l], last_node)

            with pool.Fori(0, TURNS) as i:
                for l in range(LANES):
                    pool.wait_ge(ld_i[l], 16 * n_i.at("S", i, 1))
                    pool.wait_ge(s_tof, tout.at("S", i))
                    settle(pool)
                    for j in range(TG):
                        gather(xa[l][:, j, :], x, ix[l][:, j:j + 1], gx[l], last_node)
                for l in range(LANES):
                    rstds("S", i, l, l)
                for l in range(LANES):
                    for j in range(TG):
                        gather(jx[l][:, j:j + 1], slot_of_node, ix[l][:, j:j + 1], gj[l], last_node)

            for r in range(ROUNDS):
                M, D = f"M{r}", f"D{r}"
                with pool.Fori(0, TURNS) as i:
                    for l in range(LANES):
                        rstds(M, i, l, l)
                    if r:
                        for l in range(LANES):
                            pool.wait_ge(ld_m[l], 16 * n_m.at(M, i, 1))
                            pool.wait_ge(ld_j[l], 16 * n_j.at(M, i, 1))
                            settle(pool)
                            for j in range(TG):
                                gather(mm[l][:, j, :], slot_rows[r], jx[l][:, j:j + 1], gm[l], last_slot)
                    if r == STEPS:
                        for l in range(LANES):
                            rstds(M, i, LANES + l, l)
                if r == 0:
                    with pool.Fori(0, TURNS) as i:
                        for l in range(LANES):
                            pool.wait_ge(ld_i[l], 16 * n_i.at(D, i, 1))
                            pool.wait_ge(v_h, cell.at(D, i))
                            settle(pool)
                            for j in range(TG):
                                gather(mm[l][:, j, :], x, ix[l][:, j:j + 1], gx[l], last_node)
                        for l in range(LANES):
                            rstds(D, i, l, l)
                        for l in range(LANES):
                            pool.wait_ge(st_x[l], 16 * (i + 1))
                        settle(pool)
                if r == STEPS:
                    with pool.Fori(0, TURNS) as i:
                        for l in range(LANES):
                            pool.wait_ge(ld_i[l], 16 * n_i.at(D, i, 1))
                            pool.wait_ge(s_tof, tout.at(D, i, l + 1))
                            settle(pool)
                            for j in range(TG):
                                scatter(out, on[l][:, j, :], ix[l][:, j:j + 1], sc[l], last_node)

        @block.scalar
        def _(act):
            act.sem_inc(a_r, 1)
            act.sem_inc(a_n, 1)
            act.sem_inc(a_z, 1)
            act.sem_inc(aC, 1)
            act.wait_ge(s_vs, 1)
            nc.scalar.activation(emb_t, etmp, ACT.Exp, scale=-0.5 * (NB - 1) ** 2).then_inc(s_exp_a, 1)

            with act.Fori(0, TURNS) as i:
                for q in range(LANES + 2):
                    if q < LANES:
                        act.wait_ge(pA, n_lane.at("W", i, q + 1))
                        nc.scalar.activation(rT[q][0:HID, :], gate[0][0][0:HID, 0:G], ACT.Sigmoid,
                                             bias=mb[:, 0:1]).then_inc(aA, 1)
                    l = q - 1
                    if 0 <= l < LANES:
                        act.wait_ge(pB, n_lane.at("W", i, l + 1))
                        nc.scalar.activation(flat(mm[l])[0:HID, 0:G], gate[0][1][0:HID, 0:G], ACT.Sigmoid,
                                             bias=mb[:, 1:2]).then_inc(aB, 1)
                    l = q - 2
                    if 0 <= l < LANES:
                        act.wait_ge(pC, n_lane.at("W", i, l + 1))
                        nc.scalar.activation(flat(xn[l])[0:96, 0:G], gate[1][2][0:96, 0:G], ACT.Copy)
                        nc.scalar.activation(cc[l][:, 0:G], gate[0][2][:, 0:G], ACT.Identity,
                                             bias=mb2[:, 0:1]).then_inc(aC, 1)

            def first_state(ph, i, l, u, func):
                act.wait_ge(s_ti, tin.at(ph, i, u + 1) - 1)
                nc.scalar.activation(hT[l][:, :], ti[:, 0:G], func).then_inc(s_tif, 1)

            def cell_r_z(ph, i, k, l):
                st = gate[k % 2]
                act.wait_ge(g_r, cell.at(ph, i, k + 1) - 1)
                nc.scalar.activation(rT[l][:, :], st[0][:, 0:G], ACT.Sigmoid, bias=bias[:, 6:7]).then_inc(a_r, 1)

            def cell_z(ph, i, k, l):
                st = gate[k % 2]
                act.wait_ge(g_z, cell.at(ph, i, k + 1) - 1)
                nc.scalar.activation(zT[l][:, :], st[2][:, 0:G], ACT.Sigmoid, bias=bias[:, 7:8]).then_inc(a_z, 1)

            def cell_n(ph, i, k, l):
                if ph in slot:
                    act.wait_ge(s_tif, tin.at(ph, i, 2 * LANES + k + 1))
                else:
                    act.wait_ge(v_t, cell.at(ph, i, k + 1))
                nc.scalar.activation(nT[l][:, :], tT[l][:, :], ACT.Tanh, bias=bias[:, 2:3]).then_inc(a_n, 1)

            def rows_copy(ph, i, u, l, stored):
                act.wait_ge(s_to, tout.at(ph, i, u + 1) - 1)
                act.wait_ge(st_o[l], 16 * stored)
                nc.scalar.activation(flat(on[l])[:, :], to[0:TP, :], ACT.Copy).then_inc(s_tof, 1)

            def sums_copy(ph, i, u, l):
                act.wait_ge(s_ti, tin.at(ph, i, u + 1) - 1)
                nc.scalar.activation(pt[l][:, :], ti[:, 0:TG * TE], ACT.Copy)
                nc.scalar.activation(part[:, bass.ds((i * LANES + l) * 2 * TG, 2 * TG)].rearrange("p (j b) -> p j b", b=2),
                                     ti[:, 0:TG * TE].rearrange("p (j e) -> p j e", e=TE)[:, :, TP:TE],
                                     ACT.Copy).then_inc(s_tif, 1)

            def cells(ph, i, steps, extra):
                n = steps * LANES
                for k in range(n + 1):
                    if k < n:
                        cell_r_z(ph, i, k, k % LANES)
                    if k:
                        cell_n(ph, i, k - 1, (k - 1) % LANES)
                    if k < n:
                        cell_z(ph, i, k, k % LANES)
                        extra(k)
                for k in range(n, n + LAG):
                    extra(k)

            with act.Fori(0, TURNS) as i:
                for l in range(LANES):
                    first_state("S", i, l, l, ACT.Relu)

                def extra(k):
                    c = k - LAG
                    if 0 <= c < CELLS - LANES:
                        l = c % LANES
                        rows_copy("S", i, c, l, n_sto.at("S", i, c // LANES + 1))

                cells("S", i, STEPS, extra)

            for r in range(ROUNDS):
                M, D = f"M{r}", f"D{r}"
                with act.Fori(0, TURNS) as i:
                    for l in range(LANES):
                        first_state(M, i, l, l, ACT.Relu)

                    def extra(k):
                        if r < STEPS and k < CELLS and k % STEPS == STEPS - 1:
                            sums_copy(M, i, LANES + k // STEPS, k // STEPS)

                    cells(M, i, STEPS, extra)
                    if r == STEPS:
                        act.wait_ge(v_h, cell.at(M, i, CELLS))
                        for q in range(LANES):
                            act.wait_ge(s_ti, tin.at(M, i, LANES + q + 1) - 1)
                            nc.scalar.activation(tT[q][:, :], ti[:, 0:G], ACT.Relu).then_inc(s_tif, 1)
                        for q in range(LANES + 2):
                            l = q - 1
                            if 0 <= l < LANES:
                                act.wait_ge(s_cn, n_cv.at(M, i, l + 1))
                                nc.scalar.activation(flat(mm[l])[:, :], gate[1][0][0:TP, :], ACT.Copy).then_inc(s_cf, 1)
                            l = q - 2
                            if 0 <= l < LANES:
                                sums_copy(M, i, 2 * LANES + l, l)
                act.wait_ge(s_ti, tin.at(D, 0) - 1)
                nc.scalar.activation(bsum[:, 0, :], ti[0:ET, 0:2 * C], ACT.Copy).then_inc(s_bh, 1)
                act.wait_ge(s_tif, tin.at(D, 0))
                nc.scalar.activation(bsum[:, 1, :], brest[:, :], ACT.Copy).then_inc(s_bm, 1)
                if r < STEPS:
                    with act.Fori(0, TURNS) as i:
                        for l in range(LANES):
                            first_state(D, i, l, 2 * l, ACT.Copy if r else ACT.Relu)

                        def extra(k):
                            c = k - LAG
                            if r < STEPS - 1 and 0 <= c < LANES:
                                rows_copy(D, i, c, c, n_sto.at(D, i))

                        cells(D, i, 1, extra)

        @block.vector
        def _(dve):
            steps = [0]

            def link(ins):
                steps[0] += 1
                ins.then_inc(chain, 1)
                dve.wait_ge(chain, steps[0])

            def new_chain():
                dve.sem_clear(chain)
                steps[0] = 0

            V = nc.vector
            dve.sem_inc(v_t, 1)
            dve.sem_inc(v_h, 1)
            dve.sem_inc(s_tif, 1)
            dve.sem_inc(s_tof, 1)
            for s_ in (vA, vB, vC):
                dve.sem_inc(s_, 1)
            dve.wait_ge(s_seq, 48)
            V.tensor_copy(late[:, :], seq_i[0][:, :])
            link(V.tensor_copy(seq[:, :], seq_i[1][:, :]))
            link(V.tensor_tensor(late[:, :], late[:, :], seq[:, :], ALU.is_gt))
            V.tensor_reduce(late_p[:, :], late[:, :], AX.X, ALU.max).then_inc(v_late, 1)
            dve.wait_ge(s_late, 32)
            link(V.tensor_reduce(late_any[:, :], late_row[:, :], AX.X, ALU.max))
            V.tensor_copy(late_i[:, :], late_any[:, :]).then_inc(v_late, 1)
            for l in range(LANES):
                V.memset(cc[l][96:C, G:3 * G], 0.0)
            dve.wait_ge(s_id, 4)
            dve.wait_ge(s_idx, 16 * N_IDX)
            link(V.tensor_scalar(cen_i[:, :], cen_i[:, :], NB - 1, None, ALU.bitwise_and))
            link(V.tensor_copy(cen[:, :], cen_i[:, :]))
            link(V.tensor_scalar(cen[:, :], cen[:, :], 1.0 / (NB - 1), None, ALU.mult))
            link(V.tensor_scalar(etmp, wbc, 0.0, 1.0, ALU.max, ALU.min))
            link(V.tensor_scalar(etmp, etmp, cen[:, 0:1], None, ALU.subtract))
            V.tensor_tensor(etmp, etmp, etmp, ALU.mult).then_inc(s_vs, 1)
            V.tensor_copy(dcf[:, :], ic[1][:, :])
            link(V.tensor_copy(dpf[:, :], ic[2][:, :]))
            V.tensor_tensor(deq[:, :], dcf[:, :], dpf[:, :], ALU.is_equal)
            link(V.tensor_scalar(dfi[:, :], dcf[:, :], -1.0, float(NONE), ALU.mult, ALU.add))
            link(V.tensor_tensor(dfi[:, :], dfi[:, :], deq[:, :], ALU.mult))
            link(V.tensor_tensor(dfi[:, :], dfi[:, :], dcf[:, :], ALU.add))
            V.tensor_copy(ifirst[:, :], dfi[:, :])
            link(V.tensor_copy(drow[:, :], drow_i[:, :]))
            V.tensor_scalar(eqf[:, :], drow[:, :], drow[:, 0:1], None, ALU.is_equal)
            link(V.tensor_scalar(eql[:, :], drow[:, :], drow[:, TP - 1:TP], None, ALU.is_equal))
            link(V.tensor_tensor(eql[:, :], eqf[:, :], eql[:, :], ALU.max))
            link(V.scalar_tensor_tensor(eql[:, :], drow[:, :], 1.0, eql[:, :], ALU.add, ALU.mult))
            V.tensor_tensor(ext[:, 0:TP], drow[:, :], eql[:, :], ALU.subtract)
            V.tensor_copy(ext[:, TP:TP + 1], drow[:, 0:1])
            link(V.scalar_tensor_tensor(ext[:, TP + 1:TE], drow[:, TP - 1:TP], 1.0, eqf[:, TP - 1:TP],
                                        ALU.add, ALU.mult))
            link(V.tensor_tensor(ext[:, TP + 1:TE], drow[:, TP - 1:TP], ext[:, TP + 1:TE], ALU.subtract))
            V.tensor_copy(keys[:, :], ext[:, TP:TE])
            link(V.tensor_tensor(asq[:, :], attr_t[:, :], attr_t[:, :], ALU.mult))
            V.tensor_reduce(nrm[:, :], asq[:, :].rearrange("p (q c) -> p q c", c=3), AX.X, ALU.add).then_inc(v_sq, 1)
            dve.wait_ge(p_nrm, 1)
            link(V.tensor_scalar(nrm[:, :], nrm[:, :], 1e-12, None, ALU.add))
            link(V.reciprocal(inv[:, :], nrm[:, :]))
            for c in range(3):
                last = V.tensor_tensor(rh[:, c, :], attr_t[:, :].rearrange("p (q c) -> p c q", c=3)[:, c, :],
                                       inv[:, :], ALU.mult)
            last.then_inc(s_prep, 1)
            link(V.tensor_scalar(etmp2, wbc, 1.0, float(NB) ** 0.5, ALU.is_le, ALU.mult))
            dve.wait_ge(s_exp_a, 1)
            V.tensor_tensor(emb_t, emb_t, etmp2, ALU.mult).then_inc(s_exp, 1)

            dve.wait_ge(s_set, 16 * N_SET)
            V.tensor_tensor(bias[:, 6:9], bias[:, 0:3], bias[:, 3:6], ALU.add)
            for k, blocks in enumerate(((0, 2, 2, 2), (1, 1, 1), (3, 3, 3))):
                for q, b in enumerate(blocks):
                    V.tensor_copy(mw2x[:, k, q * MUL:(q + 1) * MUL], mw2[:, b * MUL:(b + 1) * MUL])
            V.tensor_scalar(up[:, :], up[:, :], float(MUL) ** -0.5, None, ALU.mult)
            V.tensor_scalar(upss[:, :], upss[:, :], float(MUL) ** -0.5, None, ALU.mult)
            for k, f in enumerate((1.0, 3.0 ** 0.5, 1.0)):
                V.tensor_scalar(wo[:, k, :], wo[:, k, :], f / (float(2 * MUL) ** 0.5 * 16.0), None, ALU.mult)
            dve.wait_ge(s_wt, 1)
            V.tensor_copy(flat(w_ihT)[:, :], ti[:, 0:3 * C])
            V.tensor_copy(flat(w_hT)[:, :], to[:, 0:3 * C]).then_inc(s_wc, 1)
            dve.wait_ge(s_wt, 2)
            V.tensor_copy(flat(w_pT)[:, :], gate[0][0][:, 0:3 * C]).then_inc(s_wc, 1)

            with dve.Fori(0, TURNS) as i:
                for l in range(LANES):
                    dve.wait_ge(ld_w[l], 16 * n_w.at("W", i, 5))
                    for j in range(TG):
                        V.tensor_scalar(mk[l][:, j * TE:(j + 1) * TE], pt[l][0:TP, j * TE:(j + 1) * TE],
                                        dc[l][:, j:j + 1], None, ALU.is_equal)
                    for b in range(2):
                        last = V.tensor_scalar(rm[l][:, b * G:(b + 1) * G], pf[l][0:ET, :], keys[:, b:b + 1],
                                               None, ALU.is_equal)
                    last.then_inc(v_m, 1)
                for q in range(LANES + 2):
                    if q < LANES:
                        dve.wait_ge(aA, n_lane.at("W", i, q + 1))
                        V.scalar_tensor_tensor(nT[q][0:HID, :], gate[0][0][0:HID, 0:G], mb[:, 0:1], rT[q][0:HID, :],
                                               ALU.add, ALU.mult).then_inc(vA, 1)
                    l = q - 1
                    if 0 <= l < LANES:
                        dve.wait_ge(aB, n_lane.at("W", i, l + 1))
                        V.scalar_tensor_tensor(zT[l][0:HID, :], gate[0][1][0:HID, 0:G], mb[:, 1:2],
                                               flat(mm[l])[0:HID, 0:G], ALU.add, ALU.mult).then_inc(vB, 1)
                    l = q - 2
                    if 0 <= l < LANES:
                        dve.wait_ge(aC, primed.at("W", i, l + 1))
                        for k in range(2):
                            last = V.scalar_tensor_tensor(
                                cc[l][0:96, (k + 1) * G:(k + 2) * G], gate[1][k][0:96, 0:G], mb2[0:96, k + 1:k + 2],
                                flat(xn[l])[0:96, 0:G], ALU.add, ALU.mult)
                        last.then_inc(vC, 1)

            def variance(l, rows):
                for j in range(TG):
                    last = V.bn_stats(stats[l][:, j, :], rows[:, j, :])
                link(last)
                for j in range(TG):
                    last = V.bn_aggr(mv[l][:, j, :], stats[l][:, j, :])
                link(last)
                V.tensor_scalar(veps[l][:, :], mv[l][:, :, 1], EPS, None, ALU.add).then_inc(v_var, 1)

            def norm(ph, i, u, l, rows):
                dve.wait_ge(p_rs, n_ln.at(ph, i, u + 1))
                for j in range(TG):
                    last = V.tensor_scalar(xn[l][:, j, :], rows[:, j, :], mv[l][:, j, 0:1], rstd[l][:, j:j + 1],
                                           ALU.subtract, ALU.mult)
                last.then_inc(s_ln, 1)

            def cell_t(ph, i, k, l):
                dve.wait_ge(a_r, cell.at(ph, i, k + 1))
                dve.wait_ge(g_n, cell.at(ph, i, k + 1) - 1)
                V.scalar_tensor_tensor(tT[l][:, :], gate[k % 2][1][:, 0:G], bias[:, 5:6], rT[l][:, :],
                                       ALU.add, ALU.mult).then_inc(v_t, 1)
                if ph in slot:
                    dve.wait_ge(v_t, cell.at(ph, i, k + 1))
                    dve.wait_ge(s_ti, tin.at(ph, i, 2 * LANES + k + 1) - 1)
                    V.tensor_tensor(tT[l][:, :], tT[l][:, :], ti[:, 0:G], ALU.add).then_inc(s_tif, 1)

            def cell_h(ph, i, k, l):
                dve.wait_ge(a_n, cell.at(ph, i, k + 1))
                link(V.tensor_tensor(tT[l][:, :], hT[l][:, :], nT[l][:, :], ALU.subtract))
                dve.wait_ge(a_z, cell.at(ph, i, k + 1))
                link(V.tensor_tensor(tT[l][:, :], zT[l][:, :], tT[l][:, :], ALU.mult))
                V.tensor_tensor(hT[l][:, :], nT[l][:, :], tT[l][:, :], ALU.add).then_inc(v_h, 1)

            def cells(ph, i, steps, extra):
                n = steps * LANES
                for k in range(n + 1):
                    if k < n:
                        cell_t(ph, i, k, k % LANES)
                    if k:
                        cell_h(ph, i, k - 1, (k - 1) % LANES)
                    if k < n:
                        extra(k)
                for k in range(n, n + LAG):
                    extra(k)

            def rows_add(ph, i, u, l, rows, stored):
                dve.wait_ge(s_to, tout.at(ph, i, u + 1) - 1)
                dve.wait_ge(st_o[l], 16 * stored)
                V.tensor_tensor(flat(on[l])[:, :], to[0:TP, :], flat(rows)[:, :], ALU.add).then_inc(s_tof, 1)

            with dve.Fori(0, TURNS) as i:
                new_chain()
                for l in range(LANES):
                    dve.wait_ge(gx[l], 16 * n_gx.at("S", i, TG))
                    variance(l, xa[l])
                for l in range(LANES):
                    norm("S", i, l, l, xa[l])
                    dve.wait_ge(s_ln, n_ln.at("S", i, l + 1))
                    dve.wait_ge(st_o[l], 16 * n_sto.at("S", i))
                    V.tensor_scalar(flat(on[l])[:, :], flat(xn[l])[:, :], 0.0, None, ALU.max).then_inc(s_h0, 1)

                def extra(k):
                    c = k - LAG
                    if CELLS - LANES <= c < CELLS:
                        l = c % LANES
                        rows_add("S", i, c, l, xa[l], n_sto.at("S", i, STEPS))

                cells("S", i, STEPS, extra)

            for r in range(ROUNDS):
                M, D = f"M{r}", f"D{r}"
                with dve.Fori(0, TURNS) as i:
                    new_chain()
                    for l in range(LANES):
                        dve.wait_ge(ld_x[l], 16 * (n_x.at(M, i) + 2))
                        variance(l, xa[l])
                    for l in range(LANES):
                        norm(M, i, l, l, xa[l])

                    def extra(k):
                        c = k - LAG
                        if CELLS - LANES <= c < CELLS:
                            l = c % LANES
                            rows_add(M, i, l, l, xa[l], n_sto.at(M, i))

                    cells(M, i, STEPS, extra)
                    if r == STEPS:
                        for q in range(LANES):
                            dve.wait_ge(gm[q], 16 * n_gm.at(M, i, TG))
                            variance(q, mm[q])
                        for q in range(LANES):
                            norm(M, i, LANES + q, q, mm[q])
                        for q in range(LANES):
                            dve.wait_ge(s_up, n_cv.at(M, i, q + 1))
                            dve.wait_ge(ld_c[q], 16 * n_c.at(M, i, 1))
                            V.tensor_tensor(rT[q][:, :], gate[0][0][:, 0:G], cc[q][:, 0:G], ALU.mult)
                            V.tensor_tensor(zT[q][0:96, :], gate[0][1][0:96, 0:G], cc[q][0:96, G:2 * G], ALU.mult)
                            V.tensor_tensor(nT[q][0:96, :], gate[0][2][0:96, 0:G], cc[q][0:96, 2 * G:3 * G],
                                            ALU.mult).then_inc(s_pr, 1)
                dve.wait_ge(s_bh, r + 1)
                V.tensor_tensor(brest[:, :], ti[0:ET, 0:2 * C], bsum[:, 0, :], ALU.subtract).then_inc(s_tif, 1)
                dve.wait_ge(s_bm, r + 1)
                V.tensor_tensor(bsum[:, 2, :], brest[:, :], bsum[:, 1, :], ALU.subtract).then_inc(s_bl, 1)

                def whole_sums(i, u, l):
                    dve.wait_ge(s_ti, tin.at(D, i, u + 1) - 1)
                    dve.wait_ge(ld_p[l], 16 * n_p.at(D, i, 1))
                    V.tensor_tensor(pf[l][:, :].rearrange("p (j e) -> p j e", e=TP),
                                    ti[:, 0:G].rearrange("p (j e) -> p j e", e=TP),
                                    pt[l][:, :].rearrange("p (j e) -> p j e", e=TE)[:, :, 0:TP],
                                    ALU.add).then_inc(s_tif, 1)

                with dve.Fori(0, TURNS) as i:
                    new_chain()
                    if r == 0:
                        for l in range(LANES):
                            dve.wait_ge(gx[l], 16 * n_gx.at(D, i, TG))
                            variance(l, mm[l])
                    for l in range(LANES):
                        if r == 0:
                            norm(D, i, l, l, mm[l])
                        whole_sums(i, 2 * l + 1 if r < STEPS else l, l)
                        if r == STEPS:
                            dve.wait_ge(sc[l], 16 * n_scat.at(D, i))
                            dve.wait_ge(ld_m[l], 16 * n_m.at(D, i, 1))
                            rows_add(D, i, l, l, mm[l], n_sto.at(D, i))
                    if r < STEPS:
                        def extra(k):
                            c = k - LAG
                            if r == STEPS - 1 and 0 <= c < LANES:
                                if c == 0:
                                    for l in range(LANES):
                                        dve.wait_ge(ld_b[l], 16 * n_b.at(D, i, 1))
                                rows_add(D, i, c, c, xn[c], n_sto.at(D, i))

                        cells(D, i, 1, extra)

        @block.tensor
        def _(pe):
            T = nc.tensor
            pe.wait_ge(s_id, 4)
            pe.wait_ge(s_set, 16 * N_SET)
            for k in range(6):
                last = T.transpose((ti, to)[k // 3][:, (k % 3) * C:(k % 3 + 1) * C], w_raw[:, k, :], ident[:, :])
            last.then_inc(s_wt, 1)
            pe.wait_ge(s_wc, 1)
            T.matmul(gate[0][0][:, 0:3 * C], w_lin[:, :], flat(w_ihT)[:, :], start=True, stop=True).then_inc(s_wt, 1)
            pe.wait_ge(s_wc, 2)

            with pe.Fori(0, TURNS) as i:
                for q in range(LANES + 2):
                    if q < LANES:
                        pe.wait_ge(ld_w[q], 16 * n_w.at("W", i, 5))
                        pe.wait_ge(vA, primed.at("W", i, q))
                        T.matmul(gate[0][0][0:HID, 0:G], mw0[:, :], tT[q][0:NB, :], start=True, stop=True).then_inc(pA, 1)
                    l = q - 1
                    if 0 <= l < LANES:
                        pe.wait_ge(vA, primed.at("W", i, l + 1))
                        pe.wait_ge(vB, primed.at("W", i, l))
                        T.matmul(gate[0][1][:, 0:G], mw1[:, :], nT[l][0:HID, :], start=True, stop=True).then_inc(pB, 1)
                    l = q - 2
                    if 0 <= l < LANES:
                        pe.wait_ge(vB, primed.at("W", i, l + 1))
                        pe.wait_ge(vC, primed.at("W", i, l))
                        pe.wait_ge(aC, primed.at("W", i, l))
                        T.matmul(gate[0][2][:, 0:G], mw2x[:, 0, :], zT[l][0:HID, :], start=True, stop=True)
                        for k in range(2):
                            T.matmul(gate[1][k][0:96, 0:G], mw2x[:, k + 1, 0:96], zT[l][0:HID, :], start=True, stop=True)
                        T.matmul(gate[1][2][0:96, 0:G], sel3[:, :], hT[l][0:3, :], start=True, stop=True).then_inc(pC, 1)
            pe.wait_ge(vC, primed.total)
            pe.wait_ge(aC, primed.total)

            def rows_to_cols(ph, i, u, rows):
                pe.wait_ge(s_tif, tin.at(ph, i, u))
                for j in range(TG):
                    last = T.transpose(ti[:, j * TP:(j + 1) * TP], rows[:, j, :], ident[0:TP, 0:TP])
                last.then_inc(s_ti, 1)

            def cols_to_rows(ph, i, u, cols):
                pe.wait_ge(s_tof, tout.at(ph, i, u))
                for j in range(TG):
                    last = T.transpose(to[0:TP, j * C:(j + 1) * C], cols[:, j * TP:(j + 1) * TP], ident[:, :])
                last.then_inc(s_to, 1)

            def cell_gates(ph, i, k, l, ready):
                st = gate[k % 2]
                ready()
                before = cell.at(ph, i, max(k - 1, 0))
                for b, (w, full, read) in enumerate(((0, g_r, a_r), (2, g_n, v_t), (1, g_z, a_z))):
                    pe.wait_ge(read, before)
                    both = ph in slot and w != 2
                    last = T.matmul(st[b][:, 0:G], w_hT[:, w, :], hT[l][:, :], start=True, stop=not both)
                    if both:
                        last = T.matmul(st[b][:, 0:G], w_pT[:, w, :], pf[l][:, :], start=False, stop=True)
                    last.then_inc(full, 1)
                    if ph in slot and w == 2:
                        pe.wait_ge(s_tif, tin.at(ph, i, 2 * LANES + k))
                        T.matmul(ti[:, 0:G], w_pT[:, 2, :], pf[l][:, :], start=True, stop=True).then_inc(s_ti, 1)

            def cells(ph, i, steps, first, extra):
                n = steps * LANES
                for k in range(n):
                    l = k % LANES

                    def ready():
                        if k < LANES:
                            first(l)
                        else:
                            pe.wait_ge(v_h, cell.at(ph, i, k - LANES + 1))

                    cell_gates(ph, i, k, l, ready)
                    extra(k)
                for k in range(n, n + LAG):
                    extra(k)

            def sum_tiles(ph, i, u, l):
                pe.wait_ge(ld_k[l], 16 * n_k.at(ph, i, 1))
                pe.wait_ge(s_tif, tin.at(ph, i, u))
                for j in range(TG):
                    last = T.matmul(ti[:, j * TE:(j + 1) * TE], mm[l][:, j, :], mk[l][:, j * TE:(j + 1) * TE],
                                    start=True, stop=True)
                last.then_inc(s_ti, 1)

            with pe.Fori(0, TURNS) as i:
                for l in range(LANES):
                    pe.wait_ge(s_ln, n_ln.at("S", i, l + 1))
                    rows_to_cols("S", i, l, xn[l])

                def extra(k):
                    c = k - LAG
                    if 0 <= c < CELLS:
                        pe.wait_ge(v_h, cell.at("S", i, c + 1))
                        cols_to_rows("S", i, c, hT[c % LANES])

                cells("S", i, STEPS, lambda l: pe.wait_ge(s_tif, tin.at("S", i, l + 1)), extra)

            for r in range(ROUNDS):
                M, D = f"M{r}", f"D{r}"
                with pe.Fori(0, TURNS) as i:
                    for l in range(LANES):
                        pe.wait_ge(s_ln, n_ln.at(M, i, l + 1))
                        rows_to_cols(M, i, l, xn[l])

                    def extra(k):
                        if r < STEPS and k < CELLS and k % STEPS == STEPS - 1:
                            l = k // STEPS
                            if r:
                                pe.wait_ge(gm[l], 16 * n_gm.at(M, i, TG))
                            else:
                                pe.wait_ge(ld_m[l], 16 * n_m.at(M, i, 1))
                            sum_tiles(M, i, LANES + l, l)
                        c = k - LAG
                        if CELLS - LANES <= c < CELLS:
                            pe.wait_ge(v_h, cell.at(M, i, c + 1))
                            cols_to_rows(M, i, c % LANES, hT[c % LANES])

                    cells(M, i, STEPS, lambda l: pe.wait_ge(s_tif, tin.at(M, i, l + 1)), extra)
                    if r == STEPS:
                        for q in range(LANES):
                            pe.wait_ge(s_ln, n_ln.at(M, i, LANES + q + 1))
                            rows_to_cols(M, i, LANES + q, xn[q])
                        for read in (a_r, v_t, a_z):
                            pe.wait_ge(read, cell.at(M, i, CELLS))
                        for q in range(LANES + 2):
                            if q < LANES:
                                pe.wait_ge(s_tif, tin.at(M, i, LANES + q + 1))
                                if q:
                                    pe.wait_ge(s_pr, n_cv.at(M, i, q))
                                T.matmul(gate[0][0][:, 0:G], up[:, :], tT[q][:, :], start=True, stop=True)
                                T.matmul(gate[0][1][0:96, 0:G], upss[:, :], tT[q][:, :], start=True, stop=True)
                                T.matmul(gate[0][2][0:96, 0:G], up[:, MUL:C], tT[q][:, :], start=True,
                                         stop=True).then_inc(s_up, 1)
                            l = q - 1
                            if 0 <= l < LANES:
                                pe.wait_ge(s_pr, n_cv.at(M, i, l + 1))
                                if l:
                                    pe.wait_ge(s_cf, n_cv.at(M, i, l))
                                for j in range(TG):
                                    cols = slice(j * TP, (j + 1) * TP)
                                    o = gate[1][0][0:TP, j * C:(j + 1) * C]
                                    T.matmul(o, rT[l][:, cols], wo[:, 0, :], start=True, stop=False)
                                    T.matmul(o, zT[l][0:96, cols], wo[0:96, 1, :], start=False, stop=False)
                                    last = T.matmul(o, nT[l][0:96, cols], wo[0:96, 2, :], start=False, stop=True)
                                last.then_inc(s_cn, 1)
                            l = q - 2
                            if 0 <= l < LANES:
                                pe.wait_ge(s_cf, n_cv.at(M, i, l + 1))
                                sum_tiles(M, i, 2 * LANES + l, l)
                pe.wait_ge(s_tif, tin.at(M, TURNS))
                for b in range(2):
                    last = T.transpose(ti[0:ET, b * C:(b + 1) * C],
                                       part[:, :].rearrange("p (t b) -> p b t", b=2)[:, b, :], ident[:, :])
                last.then_inc(s_ti, 1)
                pe.wait_ge(s_bl, r + 1)

                def spread(i, u, l):
                    pe.wait_ge(ld_r[l], 16 * n_p.at(D, i, 1))
                    pe.wait_ge(s_tif, tin.at(D, i, u))
                    for b in range(2):
                        for m in range(3):
                            last = T.matmul(ti[:, 0:G], bsum[:, m, b * C:(b + 1) * C], rm[l][:, b * G:(b + 1) * G],
                                            start=b == m == 0, stop=b == 1 and m == 2)
                    last.then_inc(s_ti, 1)

                with pe.Fori(0, TURNS) as i:
                    for l in range(LANES):
                        if r < STEPS:
                            if r:
                                pe.wait_ge(ld_m[l], 16 * n_m.at(D, i, 1))
                            else:
                                pe.wait_ge(s_ln, n_ln.at(D, i, l + 1))
                            rows_to_cols(D, i, 2 * l, mm[l] if r else xn[l])
                            spread(i, 2 * l + 1, l)
                        else:
                            spread(i, l, l)
                            pe.wait_ge(s_tif, tin.at(D, i, l + 1))
                            cols_to_rows(D, i, l, pf[l])
                    if r < STEPS:
                        def extra(k):
                            c = k - LAG
                            if 0 <= c < LANES:
                                pe.wait_ge(v_h, cell.at(D, i, c + 1))
                                cols_to_rows(D, i, c, hT[c])

                        cells(D, i, 1, lambda l: pe.wait_ge(s_tif, tin.at(D, i, 2 * l + 2)), extra)


_INS = ["x", "src", "dst", "edge_attr_3", "edge_weight", "L0_gnn_W_lin", "L0_gnn_W_ih", "L0_gnn_W_hh",
        "L0_gnn_b_ih", "L0_gnn_b_hh", "L1_gnn_W_up0", "L1_gnn_W_up1", "L1_gnn_mlp_w0", "L1_gnn_mlp_b0",
        "L1_gnn_mlp_w1", "L1_gnn_mlp_b1", "L1_gnn_mlp_w2", "L1_gnn_mlp_b2", "L1_gnn_W_out0", "L1_gnn_W_out1"]


def kernel(**inputs):
    import numpy as _np
    import concourse.bacc as _bacc
    from concourse import mybir as _mybir
    from concourse.bass_utils import run_bass_kernel_spmd as _run

    nc = _bacc.Bacc("TRN2", target_bir_lowering=False, num_devices=1)
    arrays, args = {}, []
    for name in _INS:
        a = _np.ascontiguousarray(inputs[name])
        arrays[f"in_{name}"] = a
        args.append(nc.dram_tensor(f"in_{name}", a.shape, _mybir.dt.from_np(a.dtype), kind="ExternalInput").ap())
    shape = inputs["x"].shape
    args.append(nc.dram_tensor("out_0", shape, _mybir.dt.float32, kind="ExternalOutput").ap())
    gnn_kernel(nc, *args)
    r = _run(nc, [arrays], core_ids=[0])
    return r.results[0]["out_0"]
```

```python
from contextlib import ExitStack

import numpy as np

import concourse.bass as bass
from concourse import mybir

F32 = mybir.dt.float32
BF16 = mybir.dt.bfloat16
I32 = mybir.dt.int32
ALU = mybir.AluOpType
ACT = mybir.ActivationFunctionType
AX = mybir.AxisListType

C = 128
TP = 125
TG = 4
G = TP * TG
LANES = 5
STEPS = 3
TE = TP + 2
NONE = 1 << 20
NB = 8
MUL = 32
HID = 64
EPS = 1e-5
LAG = 3
SPLIT = 112


class Plan:

    def __init__(self, turns, period, steps, waves=None):
        self.turns, self.period, self.steps, self.waves = turns, period, steps, waves or {}

    def in_slot(self, g):
        for name, ahead, slots in self.steps:
            for part, slot in enumerate(slots):
                if (g - slot) % self.period == 0:
                    yield name, part, (g - slot) // self.period + ahead

    def exists(self, name, wave):
        return wave in self.waves.get(name, range(self.turns))

    def order(self, uses):
        place, at = {}, 0
        for g in range(-2 * self.period, (self.turns + 2) * self.period):
            for name, part, wave in self.in_slot(g):
                if name in uses and self.exists(name, wave):
                    place[name, part, wave] = at
                    at += uses[name]
        per = at // self.turns

        def at_step(name, wave, part=0):
            if isinstance(wave, int):
                return place[name, part, wave]
            return wave * per + (place[name, part, 2] - 2 * per)

        return at_step

    def run(self, eng, does, head=None):
        def slots(first, last, turn=None):
            for g in range(first, last):
                for name, part, wave in self.in_slot(g):
                    if name not in does:
                        continue
                    if turn is not None:
                        does[name](turn + wave if wave else turn, part)
                    elif self.exists(name, wave):
                        does[name](wave, part)

        if head:
            head()
        slots(-2 * self.period, self.period)
        with eng.Fori(1, self.turns - 1) as i:
            if head:
                head()
            slots(0, self.period, i)
        if head:
            head()
        slots((self.turns - 1) * self.period, (self.turns + 2) * self.period)


class Ledger:

    def __init__(self, phases, turns, per, start=0):
        self.start, self.per = {}, per
        at = start
        for p in phases:
            self.start[p] = at
            at += turns * per.get(p, 0)
        self.total = at

    def at(self, phase, i, k=0):
        return i * self.per.get(phase, 0) + (self.start[phase] + k)


def gnn_kernel(nc, x, src, dst, edge_attr, edge_weight, W_lin, W_ih, W_hh, b_ih, b_hh, W_up0, W_up1,
               mlp_w0, mlp_b0, mlp_w1, mlp_b1, mlp_w2, mlp_b2, W_out0, W_out1, out):
    N = x.shape[0]
    E = src.shape[0]
    NG, EG, ET = N // G, E // G, E // TP
    assert x.shape[1] == C and N % G == 0 and E % G == 0 and EG % LANES == 0
    TURNS = EG // LANES
    assert NG == 4 * TURNS * LANES
    ROUNDS = STEPS + 1
    PHASES = ["W", "S"] + [f"{a}{r}" for r in range(ROUNDS) for a in "MD"]
    CELLS = STEPS * LANES
    free = ["S"] + [f"M{r}" for r in range(ROUNDS)]
    slot = [f"D{r}" for r in range(STEPS)]

    def ledger(start=0, **per):
        return Ledger(PHASES, TURNS, per, start)

    cell = ledger(1, **{p: CELLS for p in free}, **{p: LANES for p in slot})
    tin_per = {"S": LANES, "D3": LANES, "M3": 3 * LANES}
    tin_per |= {f"M{r}": 2 * LANES for r in range(STEPS)} | {p: 3 * LANES for p in slot}
    tin = ledger(1, **tin_per)
    for r in range(ROUNDS):
        for p in PHASES[PHASES.index(f"D{r}"):]:
            tin.start[p] += 1
    tout = ledger(1, S=CELLS, **{f"M{r}": LANES for r in range(ROUNDS)}, **{p: LANES for p in slot}, D3=LANES)

    LN = (4, 6, 8, 10, 11)
    BACK = CELLS - LANES + LAG
    cell_steps = [("cell", 0, range(CELLS)), ("late", 0, range(1, CELLS + 1)), ("z", 0, range(CELLS))]
    plans = {"S": Plan(TURNS, CELLS, [
        *cell_steps,
        ("back", 0, range(LAG, CELLS + LAG)),
        ("first", 1, range(BACK, BACK + LANES)),
        ("rows0", 1, range(BACK + 2, BACK + 2 + LANES)),
        ("load_i", 1, range(LANES)),
        ("gather_x", 1, range(LANES)),
        ("variance", 1, LN),
        ("gather_j", 1, LN),
        ("norm", 1, [k + 2 for k in LN]),
        ("store_j", 1, [k + 4 for k in LN])])}
    for r in range(ROUNDS):
        conv = r == STEPS
        plans[f"M{r}"] = Plan(TURNS, CELLS + LAG + 1 if conv else CELLS, [
            *cell_steps,
            *([] if conv else [("sum", 0, [k + 3 for k in LN])]),
            ("back", 0, range(BACK, BACK + LANES)),
            ("first", 1, range(BACK, BACK + LANES)),
            ("copy_x", 1, range(BACK + 1, BACK + 1 + LANES)),
            ("load_x", 1, range(1, LANES + 1)),
            ("load_m", 0, range(LANES)),
            ("variance", 1, LN),
            ("gather_m", 0, LN),
            ("norm", 1, [k + 2 for k in LN]),
            *([("conv", 0, [CELLS + LAG])] if conv else []),
            ("store_sum", 0, [CELLS + LAG] * LANES if conv else [k + 4 for k in LN])],
            waves={"load_x": range(1, TURNS if conv else TURNS + 1)})
    for r in range(STEPS):
        d = LAG if r else LAG + 1
        plans[f"D{r}"] = Plan(TURNS, LANES, [
            ("spread", 1, range(d, d + LANES)),
            ("cell", 0, range(LANES)), ("late", 0, range(1, LANES + 1)), ("z", 0, range(LANES)),
            ("back", 0, range(LAG, LANES + LAG)),
            ("first", 1, range(d, d + LANES)),
            ("load", 1, range(LANES)),
            *([("load_x", 0, range(LANES))] if r == STEPS - 1 else []),
            *([] if r else [
                ("gather_x", 1, range(LANES)),
                ("store_x", 1, range(1, LANES + 1)),
                ("variance", 1, range(2, LANES + 2)),
                ("norm", 1, range(3, LANES + 3))])])
    ti_use, norm_use = {}, {}
    for ph, plan in plans.items():
        uses = {"first": 1, "sum": 1, "spread": 1, "conv": 2 * LANES} | ({"cell": 1} if ph in slot else {})
        ti_use[ph] = plan.order(uses)
        norm_use[ph] = plan.order({"norm": 1, "conv": LANES})

    with ExitStack() as ctx:
        def sb(name, shape, dt=F32):
            return ctx.enter_context(nc.sbuf_tensor(name, shape, dt))

        def lanes(name, shape, dt=F32):
            return [sb(f"{name}{l}", shape, dt) for l in range(LANES)]

        def bank(name):
            return ctx.enter_context(nc.psum_tensor(name, [C, 512], F32))

        def sem(name):
            return ctx.enter_context(nc.semaphore(name))

        def sems(name):
            return [sem(f"{name}{l}") for l in range(LANES)]

        def dram(name, shape, dt=F32):
            return nc.dram_tensor(name, shape, dt).ap()

        src_s = dram("src_sorted", [E], I32)
        dst_pad = dram("dst_sorted", [E + 1], I32)
        dst_s = dst_pad[1:E + 1]
        weight_s = dram("weight_sorted", [E])
        attr_s = dram("attr_sorted", [E, 3])
        late_col = dram("late_col", [TP])
        ranks = dram("ranks", [2, TP, ET], I32)
        slot_of_node = dram("slot_of_node", [N, 1], I32)
        idx_src = dram("idx_src", [EG, TP, TG], I32)
        idx_dst = dram("idx_dst", [EG, TP, TG], I32)
        idx_first = dram("idx_first", [EG, TP, TG], I32)
        idx_slot = dram("idx_slot", [EG, TP, TG], I32)
        edge_id = dram("edge_id", [EG, TP, TG], I32)
        dst_col = dram("dst_col", [EG, TP, TG])
        dst_rows = dram("dst_rows", [EG, G])
        mask_keys = dram("mask_keys", [EG, TG * TE])
        tile_masks = dram("tile_masks", [EG, TP, TG * TE])
        key_masks = dram("key_masks", [EG, ET, 2 * G], BF16)
        emb_d = dram("emb", [NB, E])
        rhat_d = dram("rhat", [3, E])
        conv_d = dram("conv_factors", [EG, C, 3 * G])
        src_rows = [dram(f"src_rows{r}", [E, C]) for r in range(ROUNDS)]
        slot_rows = [None] + [dram(f"slot_rows{r}", [E, C]) for r in range(1, ROUNDS)]
        dst_x = dram("dst_x", [E, C])
        sums_d = dram("sums", [EG, C, TG * TE])

        x_dense = x.rearrange("(g p j) c -> g p j c", p=TP, j=TG)
        out_dense = out.rearrange("(g p j) c -> g p j c", p=TP, j=TG)

        def by_tile(rows):
            return rows.rearrange("(g j p) c -> g p j c", p=TP, j=TG)

        ident = sb("ident", [C, C])
        w_raw = sb("w_raw", [C, 6, C])
        w_lin = sb("w_lin", [C, C])
        w_ihT = sb("w_ihT", [C, 3, C])
        w_hT = sb("w_hT", [C, 3, C])
        w_pT = sb("w_pT", [C, 3, C])
        bias = sb("bias", [C, 9])
        up = sb("up", [C, C])
        upss = sb("upss", [C, 96])
        mw0 = sb("mw0", [NB, HID])
        mw1 = sb("mw1", [HID, C])
        mw2 = sb("mw2", [HID, 4 * MUL])
        mw2x = sb("mw2x", [HID, 3, C])
        mb = sb("mb", [HID, 2])
        mb2 = sb("mb2", [C, 3])
        sel3 = sb("sel3", [3, 96])
        wo = sb("wo", [C, 3, C])
        part = sb("part", [C, ET * 2])
        keys = sb("keys", [ET, 2])
        bsum = sb("bsum", [ET, 3, 2 * C], BF16)
        brest = sb("brest", [ET, 2 * C])
        xa_xn = sb("xa_xn", [TP, 2 * LANES, TG, C])
        mm_on = sb("mm_on", [TP, 2 * LANES, TG, C])
        xa, xn, mm, on = ([t[:, k * LANES + l] for l in range(LANES)] for t in (xa_xn, mm_on) for k in range(2))
        hT = lanes("hT", [C, G])
        rT = lanes("rT", [C, G])
        zT = lanes("zT", [C, G])
        nT = lanes("nT", [C, G])
        tT = lanes("tT", [C, G])
        pt = lanes("pt", [C, TG * TE])
        pf = lanes("pf", [C, G])
        mk = lanes("mk", [TP, TG * TE])
        rm = lanes("rm", [ET, 2 * G], BF16)
        cc = lanes("cc", [C, 3 * G])
        ix = lanes("ix", [TP, TG], I32)
        jx = lanes("jx", [TP, TG], I32)
        dc = lanes("dc", [TP, TG])
        stats = lanes("stats", [TP, TG, 6])
        mv = lanes("mv", [TP, TG, 2])
        veps = lanes("veps", [TP, TG])
        minus_half = sb("minus_half", [TP, TG])
        half = sb("half", [TP, ET])
        rstd = lanes("rstd", [TP, TG])

        NCH = 10
        CH = E // NCH
        assert E % NCH == 0 and NB * NCH <= C and CH <= 3 * G
        wbc, emb_t, etmp = (cc[k][0:NB * NCH, 0:CH] for k in range(3))
        ic = [sb(f"ic{k}", [TP, ET], I32) for k in range(3)]
        ifirst, eid = sb("ifirst", [TP, ET], I32), sb("eid", [TP, ET], I32)
        dcf, dpf, deq, dfi = (sb(n, [TP, ET]) for n in ("dcf", "dpf", "deq", "dfi"))
        drow_i = sb("drow_i", [ET, TP], I32)
        drow, eqf, eql = (sb(n, [ET, TP]) for n in ("drow", "eqf", "eql"))
        ext = sb("ext", [ET, TE])
        none_t = sb("none_t", [TP, N // TP], I32)
        minus1 = sb("minus1", [1, 1], I32)
        attr_t = sb("attr_t", [TP, 3 * ET])
        asq = sb("asq", [TP, 3 * ET])
        rh = sb("rh", [TP, 3, ET])
        nrm, inv = sb("nrm", [TP, ET]), sb("inv", [TP, ET])
        etmp2 = cc[3][0:NB * NCH, 0:CH]
        cen_i, cen = sb("cen_i", [NB * NCH, 1], I32), sb("cen", [NB * NCH, 1])
        seq_i = [sb(f"seq_i{k}", [TP, ET], I32) for k in range(2)]
        seq, late, edge_f, dst_f = (sb(n, [TP, ET]) for n in ("seq", "late", "edge_f", "dst_f"))
        late_p, late_row, late_any = sb("late_p", [TP, 1]), sb("late_row", [1, TP]), sb("late_any", [1, 1])
        late_i, rank_i = sb("late_i", [1, 1], I32), sb("rank_i", [TP, ET], I32)
        RCH = 50
        assert E % RCH == 0 and ET * RCH <= 2 * LANES * TG * C
        other_i, other, other_d = sb("other_i", [TP, RCH], I32), sb("other", [TP, RCH]), sb("other_d", [TP, RCH])
        compared, counted = (t[:, :, :, :].rearrange("p a j c -> p (a j c)")[:, 0:ET * RCH].rearrange(
            "p (t f) -> p t f", f=RCH) for t in (xa_xn, mm_on))
        move_rank = sb("move_rank", [TP, 2, TG], I32)
        move_src, move_dst = (sb(n, [TP, TG], I32) for n in ("move_src", "move_dst"))
        move_w, move_attr = sb("move_w", [TP, TG]), sb("move_attr", [TP, TG, 3])
        N_SET = 3 + 3 + 4 + 10 + 1 + 6 + 1 + 9
        N_IDX = 4 + NCH + 1
        N_TAB = 5 + 2 + 3 + NCH

        gate = [[bank(f"{g}{s}") for g in "rnz"] for s in range(2)]
        ti, to = bank("ti"), bank("to")

        s_settle = sem("settled")
        s_seq = sem("edge_order_loaded")
        s_late = sem("edge_order_moved")
        v_late = sem("edge_order_found")
        s_copied = sem("edges_copied")
        s_order = sem("edges_sorted")
        s_ranks = sem("ranks_stored")
        s_other, s_move, s_moved = sem("others_loaded"), sem("unsorted_loaded"), sem("edges_moved")
        s_set = sem("setup_loaded")
        s_id = sem("ident_steps")
        s_cst = sem("pool_constants")
        s_wt = sem("weights_transposed")
        s_wc = sem("weights_copied")
        s_idx = sem("index_steps_loaded")
        s_prep = sem("tables_ready")
        s_tab = sem("tables_stored")
        s_exp_a, s_exp = sem("exp_done"), sem("radial_ready")
        s_vs = sem("vector_setup")
        chain = sem("vector_chain")
        pchain = sem("pool_chain")
        g_r, g_n, g_z = sem("gate_r_summed"), sem("gate_n_summed"), sem("gate_z_summed")
        a_r, a_n, a_z = sem("r_ready"), sem("n_ready"), sem("z_ready")
        v_t, v_h = sem("t_ready"), sem("state_ready")
        s_ti, s_tif = sem("ti_full"), sem("ti_free")
        s_to, s_tof = sem("to_full"), sem("to_free")
        s_ln = sem("normed")
        v_var, p_rs = sem("variances"), sem("rstd_ready")
        v_sq, p_nrm = sem("edge_squares"), sem("edge_norms")
        s_h0 = sem("first_rows_ready")
        s_cp = sem("rows_kept")
        s_pf = sem("pf_ready")
        ld_x, ld_m, ld_k, ld_i, ld_j = sems("ld_x"), sems("ld_m"), sems("ld_k"), sems("ld_i"), sems("ld_j")
        ld_p, ld_r, ld_b, ld_c, ld_w = sems("ld_p"), sems("ld_r"), sems("ld_b"), sems("ld_c"), sems("ld_w")
        gx, gj, gm = sems("gather_x"), sems("gather_slot"), sems("gather_rows")
        st_o, st_j, st_p, st_x, st_w = sems("st_o"), sems("st_j"), sems("st_p"), sems("st_x"), sems("st_w")
        sc = sems("scattered")
        pA, pB, pC = sem("mlp1_summed"), sem("mlp2_summed"), sem("factors_summed")
        aA, aB, aC = sem("mlp1_sigmoid"), sem("mlp2_sigmoid"), sem("factors_copied")
        vA, vB, vC = sem("mlp1_ready"), sem("mlp2_ready"), sem("factors_ready")
        v_m = sem("masks_ready")
        s_bt, s_bh, s_br, s_bm, s_bl = (sem("bnd_T"), sem("bnd_hi"), sem("bnd_rest"), sem("bnd_mid"),
                                        sem("bnd_lo"))
        s_up = sem("conv_up")
        s_pr = sem("conv_products")
        s_cn = sem("conv_rows")
        s_cf = sem("conv_rows_copied")

        Ms = [f"M{r}" for r in range(ROUNDS)]
        Ds = [f"D{r}" for r in range(ROUNDS)]
        n_x = ledger(**{"S": 0}, **{p: 2 for p in Ms})
        n_m = ledger(**{p: 1 for p in Ms}, **{p: 1 for p in Ds[1:]})
        n_k = ledger(**{p: 1 for p in Ms})
        n_i = ledger(W=1, S=1, D0=1, D3=1)
        n_j = ledger(W=1, **{p: 1 for p in Ms[1:]})
        n_p = ledger(**{p: 1 for p in Ds})
        n_b = ledger(D2=1)
        n_c = ledger(M3=1)
        n_gx = ledger(S=TG, D0=TG)
        n_gj = ledger(S=TG)
        n_gm = ledger(**{p: TG for p in Ms[1:]})
        n_sto = ledger(W=1, S=4, **{p: 2 for p in Ms}, D0=1, D1=1, D2=1)
        n_stj = ledger(S=1)
        n_stp = ledger(**{p: 1 for p in Ms})
        n_ln = ledger(S=LANES, **{p: LANES for p in Ms[:3]}, M3=2 * LANES, D0=LANES)
        n_w = ledger(W=5)
        n_stw = ledger(W=2)
        n_lane = ledger(W=LANES)
        primed = ledger(1, W=LANES)
        n_pf = ledger(**{p: LANES for p in Ds})
        n_cv = ledger(M3=LANES)
        n_scat = ledger(W=TG, D3=TG)

        n_cp = ledger(S=LANES, **{p: LANES for p in Ms})

        def ti_at(ph, name, wave, part=0, more=0):
            return ti_use[ph](name, wave, part) + (tin.start[ph] + more)

        def norm_at(ph, name, wave, part=0, more=0):
            return norm_use[ph](name, wave, part) + (n_ln.start[ph] + more)

        def no_wave(wave):
            return isinstance(wave, int) and wave < 0

        block = ctx.enter_context(nc.Block())

        def settle(eng):
            eng.sem_inc(s_settle, 1)

        def flat(rows):
            return rows[:, :, :].rearrange("p j c -> p (j c)")

        @block.sync
        def _(sp):
            def rows_in(buf, view, g, s):
                sp.dma_start(buf[0:SPLIT], view[g, 0:SPLIT]).then_inc(s, 16)
                sp.dma_start(buf[SPLIT:TP], view[g, SPLIT:TP]).then_inc(s, 16)

            with nc.allow_non_contiguous_dma(reason="short rows"):
                sp.dma_start(seq_i[0][:, :], dst.rearrange("(p q) -> p q", p=TP)).then_inc(s_seq, 16)
                sp.wait_ge(s_cst, 1)
                sp.dma_start(seq_i[1][0:TP - 1, :], dst[1:E - ET + 1].rearrange("(p q) -> p q", p=TP - 1)).then_inc(s_seq, 16)
                sp.dma_start(seq_i[1][TP - 1:TP, 0:ET - 1], dst[E - ET + 1:E].rearrange("(p q) -> p q", p=1)).then_inc(s_seq, 16)
            sp.dma_start(dst_pad[0:1].rearrange("(a b) -> a b", a=1), minus1[0:1, 0:1]).then_inc(s_copied, 16)
            sp.dma_start(dst_s, dst).then_inc(s_copied, 16)
            sp.dma_start(src_s, src).then_inc(s_copied, 16)
            sp.dma_start(weight_s, edge_weight).then_inc(s_copied, 16)
            sp.dma_start(attr_s, edge_attr).then_inc(s_copied, 16)
            sp.dma_start(slot_of_node.rearrange("(p q) o -> p (q o)", p=TP), none_t[:, :]).then_inc(s_copied, 16)

            sp.wait_ge(v_late, 1)
            with nc.allow_non_contiguous_dma(reason="a column"):
                sp.dma_start(late_col.rearrange("(p o) -> p o", o=1), late_p[:, :]).then_inc(s_late, 16)
            sp.wait_ge(s_late, 16)
            sp.dma_start(late_row[:, :], late_col.rearrange("(o p) -> o p", o=1)).then_inc(s_late, 16)

            for k, w in enumerate((W_ih, W_hh)):
                sp.dma_start(w_raw[:, 3 * k:3 * k + 3, :], w.rearrange("(g o) i -> o g i", g=3)).then_inc(s_set, 16)
            sp.dma_start(w_lin[:, :], W_lin).then_inc(s_set, 16)
            sp.dma_start(mw0[:, :], mlp_w0).then_inc(s_set, 16)
            sp.dma_start(mw2[:, :], mlp_w2).then_inc(s_set, 16)
            with nc.allow_non_contiguous_dma(reason="short columns"):
                for k, b in enumerate((b_ih, b_hh)):
                    sp.dma_start(bias[:, 3 * k:3 * k + 3], b.rearrange("(g p) -> p g", g=3)).then_inc(s_set, 16)
                for k, b in enumerate((mlp_b0, mlp_b1)):
                    sp.dma_start(mb[:, k:k + 1], b.rearrange("(p o) -> p o", o=1)).then_inc(s_set, 16)
                sp.wait_ge(s_cst, 1)
                for k, blocks in enumerate(((0, 2, 2, 2), (1, 1, 1), (3, 3, 3))):
                    for q, b in enumerate(blocks):
                        sp.dma_start(mb2[q * MUL:(q + 1) * MUL, k:k + 1],
                                     mlp_b2[b * MUL:(b + 1) * MUL].rearrange("(p o) -> p o", o=1)).then_inc(s_set, 16)
                sp.dma_start(mw1[:, 0:HID], mlp_w1).then_inc(s_set, 16)
                sp.dma_start(up[0:MUL, 0:MUL], W_up0).then_inc(s_set, 16)
                for c in range(3):
                    sp.dma_start(upss[0:MUL, c * MUL:(c + 1) * MUL], W_up0).then_inc(s_set, 16)
                    sp.dma_start(up[MUL + c:MUL + c + 3 * (MUL - 1) + 1:3, MUL + c * MUL:MUL + (c + 1) * MUL],
                                 W_up1).then_inc(s_set, 16)
                sp.dma_start(wo[0:MUL, 0, 0:MUL], W_out0[0:MUL, :]).then_inc(s_set, 16)
                for c in range(3):
                    cols = slice(MUL + c, MUL + c + 3 * (MUL - 1) + 1, 3)
                    sp.dma_start(wo[MUL + c * MUL:2 * MUL + c * MUL, 0, cols], W_out1[MUL:2 * MUL, :]).then_inc(s_set, 16)
                    sp.dma_start(wo[c * MUL:(c + 1) * MUL, 1, cols], W_out1[0:MUL, :]).then_inc(s_set, 16)
                    sp.dma_start(wo[c * MUL:(c + 1) * MUL, 2, 0:MUL], W_out0[MUL:2 * MUL, :]).then_inc(s_set, 16)

            sp.wait_ge(s_order, 1)
            with nc.allow_non_contiguous_dma(reason="index columns"):
                for k, a in enumerate((src_s, dst_s, dst_pad[0:E])):
                    sp.dma_start(ic[k][:, :], a.rearrange("(t p) -> p t", p=TP)).then_inc(s_idx, 16)
            sp.dma_start(drow_i[:, :], dst_s.rearrange("(t p) -> t p", p=TP)).then_inc(s_idx, 16)
            for q in range(NCH):
                sp.dma_start(wbc[q * NB:(q + 1) * NB, :],
                             weight_s[q * CH:(q + 1) * CH].partition_broadcast(NB)).then_inc(s_idx, 16)
            sp.dma_start(attr_t[:, :], attr_s.rearrange("(p q) c -> p (q c)", p=TP)).then_inc(s_idx, 16)

            sp.wait_ge(s_prep, 1)
            tabs = [(idx_src, ic[0]), (idx_dst, ic[1]), (idx_first, ifirst), (edge_id, eid), (dst_col, dcf)]
            with nc.allow_non_contiguous_dma(reason="index columns"):
                for d, s_ in tabs:
                    sp.dma_start(d.rearrange("g p j -> p g j"), s_[:, :].rearrange("p (g j) -> p g j", j=TG)).then_inc(s_tab, 16)
            sp.dma_start(dst_rows.rearrange("g (j p) -> (g j) p", p=TP), drow[:, :]).then_inc(s_tab, 16)
            sp.dma_start(mask_keys.rearrange("g (j e) -> (g j) e", e=TE), ext[:, :]).then_inc(s_tab, 16)
            for c in range(3):
                sp.dma_start(rhat_d[c].rearrange("(p q) -> p q", p=TP), rh[:, c, :]).then_inc(s_tab, 16)
            sp.wait_ge(s_exp, 1)
            for q in range(NCH):
                sp.dma_start(emb_d[:, q * CH:(q + 1) * CH], emb_t[q * NB:(q + 1) * NB, :]).then_inc(s_tab, 16)
            sp.wait_ge(s_tab, 16 * N_TAB)

            with sp.Fori(0, TURNS) as i:
                for l in range(LANES):
                    g = i * LANES + l
                    sp.dma_start(pt[l][0:TP, :], mask_keys[g].partition_broadcast(TP)).then_inc(ld_w[l], 16)
                    sp.dma_start(pf[l][0:ET, :], dst_rows[g].partition_broadcast(ET)).then_inc(ld_w[l], 16)
                    sp.dma_start(dc[l][:, :], dst_col[g]).then_inc(ld_w[l], 16)
                    sp.dma_start(tT[l][0:NB, :], emb_d[:, bass.ds(g * G, G)]).then_inc(ld_w[l], 16)
                    sp.dma_start(hT[l][0:3, :], rhat_d[:, bass.ds(g * G, G)]).then_inc(ld_w[l], 16)
                    sp.dma_start(ix[l][:, :], idx_first[g]).then_inc(ld_i[l], 16)
                    sp.dma_start(jx[l][:, :], edge_id[g]).then_inc(ld_j[l], 16)
                for l in range(LANES):
                    g = i * LANES + l
                    sp.wait_ge(v_m, n_lane.at("W", i, l + 1))
                    sp.dma_start(tile_masks[g], mk[l][:, :]).then_inc(st_w[l], 16)
                    sp.dma_start(key_masks[g], rm[l][:, :]).then_inc(st_w[l], 16)
                    sp.wait_ge(vC, primed.at("W", i, l + 1))
                    sp.wait_ge(aC, primed.at("W", i, l + 1))
                    sp.dma_start(conv_d[g], cc[l][:, :]).then_inc(st_o[l], 16)
                for l in range(LANES):
                    sp.wait_ge(st_w[l], 16 * n_stw.at("W", i, 2))
                    sp.wait_ge(st_o[l], 16 * n_sto.at("W", i, 1))
                    sp.wait_ge(sc[l], 16 * n_scat.at("W", i, TG))
                settle(sp)

            def load_i(w, l):
                if not no_wave(w - 1):
                    sp.wait_ge(gj[l], 16 * n_gj.at("S", w))
                sp.dma_start(ix[l][:, :], idx_src[w * LANES + l]).then_inc(ld_i[l], 16)

            def store_j(w, l):
                sp.wait_ge(gj[l], 16 * n_gj.at("S", w, TG))
                sp.dma_start(idx_slot[w * LANES + l], jx[l][:, :]).then_inc(st_j[l], 16)

            def store_rows0(w, l):
                sp.wait_ge(s_h0, w * LANES + (l + 1))
                sp.dma_start(by_tile(src_rows[0])[w * LANES + l], on[l][:, :, :]).then_inc(st_o[l], 16)

            def store_step(w, c):
                s, l = divmod(c, LANES)
                sp.wait_ge(s_tof, tout.at("S", w, c + 1))
                sp.dma_start(by_tile(src_rows[s + 1])[w * LANES + l], on[l][:, :, :]).then_inc(st_o[l], 16)

            plans["S"].run(sp, {"load_i": load_i, "store_j": store_j, "rows0": store_rows0, "back": store_step})
            for l in range(LANES):
                sp.wait_ge(st_j[l], 16 * n_stj.total)
                sp.wait_ge(st_o[l], 16 * n_sto.start["M0"])
                rows_in(xa[l], x_dense, l, ld_x[l])

            for r in range(ROUNDS):
                M, D = f"M{r}", f"D{r}"

                def load_x(w, l):
                    sp.wait_ge(s_ln, norm_at(M, "norm", w - 1, l, 1))
                    settle(sp)
                    sp.wait_ge(s_cp, n_cp.at(M, w - 1, l + 1))
                    settle(sp)
                    rows_in(xa[l], x_dense, w * LANES + (r * TURNS * LANES + l), ld_x[l])

                def load_m(w, l):
                    g = sp.snap(w * LANES + l) if not isinstance(w, int) else w * LANES + l
                    if not no_wave(w - 1):
                        sp.wait_ge(st_p[l], 16 * n_stp.at(M, w))
                        settle(sp)
                        if r == STEPS:
                            sp.wait_ge(s_pr, n_cv.at(M, w))
                        settle(sp)
                    sp.dma_start(mm[l][:, :, :], by_tile(src_rows[r])[g]).then_inc(ld_m[l], 16)
                    sp.dma_start(mk[l][:, :], tile_masks[g]).then_inc(ld_k[l], 16)
                    if r:
                        sp.dma_start(jx[l][:, :], idx_slot[g]).then_inc(ld_j[l], 16)
                    if r == STEPS:
                        sp.dma_start(cc[l][:, :], conv_d[g]).then_inc(ld_c[l], 16)

                def store_out(w, l):
                    g = w * LANES + (r * TURNS * LANES + l)
                    if not isinstance(w, int):
                        g = sp.snap(g)
                    sp.wait_ge(s_tof, tout.at(M, w, l + 1))
                    settle(sp)
                    sp.dma_start(out_dense[g, 0:SPLIT], on[l][0:SPLIT]).then_inc(st_o[l], 16)
                    sp.dma_start(out_dense[g, SPLIT:TP], on[l][SPLIT:TP]).then_inc(st_o[l], 16)

                def store_sum(w, l):
                    sp.wait_ge(s_tif, ti_at(M, "conv", w, 0, LANES + l + 1) if r == STEPS else ti_at(M, "sum", w, l, 1))
                    sp.dma_start(sums_d[w * LANES + l], pt[l][:, :]).then_inc(st_p[l], 16)

                plans[M].run(sp, {"load_x": load_x, "load_m": load_m, "back": store_out, "store_sum": store_sum})
                for l in range(LANES):
                    sp.wait_ge(st_p[l], 16 * n_stp.at(M, TURNS))
                    if r == STEPS:
                        sp.wait_ge(st_o[l], 16 * n_sto.at(M, TURNS))

                def load_d(w, l):
                    if not no_wave(w - 1):
                        sp.wait_ge(s_tif, ti_at(D, "first", w - 1, l, 1))
                        settle(sp)
                        if r == 0:
                            sp.wait_ge(gx[l], 16 * n_gx.at(D, w))
                            settle(sp)
                            sp.wait_ge(s_tif, ti_at(D, "spread", w - 1, l, 1))
                            settle(sp)
                    g = w * LANES + l
                    sp.dma_start(pt[l][:, :], sums_d[g]).then_inc(ld_p[l], 16)
                    sp.dma_start(rm[l][:, :], key_masks[g]).then_inc(ld_r[l], 16)
                    if r == 0:
                        sp.dma_start(ix[l][:, :], idx_dst[g]).then_inc(ld_i[l], 16)
                    else:
                        sp.dma_start(mm[l][:, :, :], by_tile(slot_rows[r])[g]).then_inc(ld_m[l], 16)

                def load_dst_x(w, l):
                    if not no_wave(w - 1):
                        sp.wait_ge(s_tof, tout.at(D, w - 1, l + 1))
                        settle(sp)
                    sp.dma_start(xn[l][:, :, :], by_tile(dst_x)[w * LANES + l]).then_inc(ld_b[l], 16)

                def store_dst_x(w, l):
                    sp.wait_ge(gx[l], 16 * n_gx.at(D, w, TG))
                    sp.dma_start(by_tile(dst_x)[w * LANES + l], mm[l][:, :, :]).then_inc(st_x[l], 16)

                def store_slot(w, l):
                    sp.wait_ge(s_tof, tout.at(D, w, l + 1))
                    sp.dma_start(by_tile(slot_rows[r + 1])[w * LANES + l], on[l][:, :, :]).then_inc(st_o[l], 16)

                if r < STEPS:
                    plans[D].run(sp, {"load": load_d, "load_x": load_dst_x, "store_x": store_dst_x, "back": store_slot})
                else:
                    with sp.Fori(0, TURNS) as i:
                        for l in range(LANES):
                            g = i * LANES + l
                            sp.wait_ge(s_tof, tout.at(D, i))
                            settle(sp)
                            sp.wait_ge(s_tif, tin.at(D, i))
                            sp.dma_start(pt[l][:, :], sums_d[g]).then_inc(ld_p[l], 16)
                            sp.dma_start(rm[l][:, :], key_masks[g]).then_inc(ld_r[l], 16)
                            sp.dma_start(mm[l][:, :, :], by_tile(slot_rows[r])[g]).then_inc(ld_m[l], 16)
                            sp.dma_start(ix[l][:, :], idx_first[g]).then_inc(ld_i[l], 16)
                        for l in range(LANES):
                            sp.wait_ge(sc[l], 16 * n_scat.at(D, i, TG))
                        settle(sp)
                if r < STEPS:
                    for l in range(LANES):
                        sp.wait_ge(st_o[l], 16 * n_sto.at(D, TURNS))
                        if r == 0:
                            sp.wait_ge(st_x[l], 16 * TURNS)
            for l in range(LANES):
                sp.wait_ge(sc[l], 16 * n_scat.total)

        @block.gpsimd
        def _(pool):
            steps = [0]

            def link(ins):
                steps[0] += 1
                ins.then_inc(pchain, 1)
                pool.wait_ge(pchain, steps[0])

            pool.memset(seq_i[1][:, :], NONE)
            pool.memset(up[:, :], 0.0)
            pool.memset(mw1[:, :], 0.0)
            pool.memset(upss[:, :], 0.0)
            pool.memset(wo[:, :, :], 0.0)
            pool.memset(mb2[:, :], 0.0)
            pool.memset(minus1[:, :], -1)
            pool.memset(minus_half[:, :], -0.5)
            pool.memset(half[:, :], 0.5)
            pool.memset(none_t[:, :], NONE).then_inc(s_cst, 1)
            pool.iota(eid[:, :], pattern=[[TP, ET]], base=0, channel_multiplier=1).then_inc(s_id, 1)
            pool.iota(cen_i[:, :], pattern=[[1, 1]], base=0, channel_multiplier=1).then_inc(s_id, 1)
            link(pool.memset(ident[:, :], 0.0))
            pool.affine_select(out=ident[:, :], in_=ident[:, :], compare_op=ALU.not_equal, fill=1.0,
                               base=0, pattern=[[-1, C]], channel_multiplier=1).then_inc(s_id, 1)
            link(pool.memset(sel3[:, :], 1.0))
            link(pool.affine_select(out=sel3[:, :], in_=sel3[:, :], compare_op=ALU.is_ge, fill=0.0,
                                    base=0, pattern=[[1, 96]], channel_multiplier=-MUL))
            pool.affine_select(out=sel3[:, :], in_=sel3[:, :], compare_op=ALU.is_ge, fill=0.0,
                               base=MUL - 1, pattern=[[-1, 96]], channel_multiplier=MUL).then_inc(s_id, 1)

            last_node, last_slot = N - 1, E - 1

            def sort_edges():
                steps[0] = 0
                pool.sem_clear(pchain)
                link(pool.tensor_copy(dst_f[:, :], seq_i[0][:, :]))
                link(pool.tensor_tensor(dst_f[:, :], dst_f[:, :], dst_f[:, :], ALU.add))
                link(pool.iota(seq_i[1][:, :], pattern=[[1, ET]], base=0, channel_multiplier=ET))
                link(pool.tensor_copy(edge_f[:, :], seq_i[1][:, :]))
                link(pool.iota(other_i[:, :], pattern=[[1, RCH]], base=0, channel_multiplier=0))
                link(pool.tensor_copy(other[:, :], other_i[:, :]))
                link(pool.memset(counted, 0.0))
                whole = [TP, ET, RCH]
                by_edge = [t[:, :].unsqueeze(2).broadcast_to(whole) for t in (edge_f, dst_f)]
                by_other = [t[:, :].unsqueeze(1).broadcast_to(whole) for t in (other, other_d)]
                with pool.Fori(0, E // RCH) as q:
                    steps[0] = 0
                    pool.sem_clear(pchain)
                    pool.dma_start(other_i[:, :], dst[bass.ds(q * RCH, RCH)].partition_broadcast(TP)).then_inc(s_other, 16)
                    pool.wait_ge(s_other, 16 * (q + 1))
                    settle(pool)
                    link(pool.tensor_copy(other_d[:, :], other_i[:, :]))
                    link(pool.tensor_tensor(other_d[:, :], other_d[:, :], other_d[:, :], ALU.add))
                    link(pool.tensor_tensor(compared, by_edge[0], by_other[0], ALU.subtract))
                    link(pool.tensor_scalar(compared, compared, 0.0, 1.0, ALU.max, ALU.min))
                    link(pool.tensor_tensor(compared, by_other[1], compared, ALU.subtract))
                    link(pool.tensor_tensor(compared, by_edge[1], compared, ALU.subtract))
                    link(pool.tensor_scalar(compared, compared, 0.0, 1.0, ALU.max, ALU.min))
                    link(pool.tensor_tensor(counted, counted, compared, ALU.add))
                    link(pool.tensor_scalar(other[:, :], other[:, :], float(RCH), None, ALU.add))
                w = RCH
                while w > 1:
                    half_w = w // 2
                    link(pool.tensor_tensor(counted[:, :, 0:half_w], counted[:, :, 0:half_w],
                                            counted[:, :, w - half_w:w], ALU.add))
                    w -= half_w
                for k in range(2):
                    link(pool.tensor_scalar(seq[:, :], counted[:, :, 0], float(k), None, ALU.add))
                    link(pool.tensor_copy(rank_i[:, :], seq[:, :]))
                    pool.dma_start(ranks[k], rank_i[:, :]).then_inc(s_ranks, 16)
                    pool.wait_ge(s_ranks, 16 * (k + 1))
                with pool.Fori(0, EG) as g:
                    def part_of(a):
                        return a.rearrange("(p g j) -> g p j", p=TP, j=TG)[g]

                    for k in range(2):
                        pool.dma_start(move_rank[:, k, :], ranks[k].rearrange("p (g j) -> g p j", j=TG)[g]).then_inc(s_move, 16)
                    with nc.allow_non_contiguous_dma(reason="index columns"):
                        pool.dma_start(move_src[:, :], part_of(src)).then_inc(s_move, 16)
                        pool.dma_start(move_dst[:, :], part_of(dst)).then_inc(s_move, 16)
                        pool.dma_start(move_w[:, :], part_of(edge_weight)).then_inc(s_move, 16)
                        pool.dma_start(move_attr[:, :, :], edge_attr.rearrange("(p g j) c -> g p j c", p=TP, j=TG)[g]).then_inc(s_move, 16)
                    pool.wait_ge(s_move, 16 * 6 * (g + 1))
                    settle(pool)
                    for j in range(TG):
                        places = [move_rank[:, k, j:j + 1] for k in range(2)]
                        for sorted_, edges, k in ((src_s, move_src, 0), (dst_pad, move_dst, 1), (weight_s, move_w, 0)):
                            scatter(sorted_.rearrange("(e o) -> e o", o=1), edges[:, j:j + 1], places[k], s_moved,
                                    last_slot + k)
                        scatter(attr_s, move_attr[:, j, :], places[0], s_moved, last_slot)
                    pool.wait_ge(s_moved, 16 * 4 * TG * (g + 1))
                    settle(pool)

            def gather(rows, table, index, s, bound):
                pool.indirect_dma_start(
                    out=rows, out_offset=None, in_=table,
                    in_offset=bass.IndirectOffsetOnAxis(ap=index, axis=0),
                    bounds_check=bound, oob_is_err=False).then_inc(s, 16)

            def scatter(table, rows, index, s, bound):
                pool.indirect_dma_start(
                    out=table, out_offset=bass.IndirectOffsetOnAxis(ap=index, axis=0),
                    in_=rows, in_offset=None, bounds_check=bound, oob_is_err=False).then_inc(s, 16)

            pool.wait_ge(v_late, 2)
            pool.wait_ge(s_copied, 16 * 6)
            unsorted = pool.value_load(late_i[0:1, 0:1], min_val=0, max_val=1)
            with pool.If(unsorted != 0):
                sort_edges()
            pool.sem_inc(s_order, 1)

            pool.wait_ge(v_sq, 1)
            pool.tensor_tensor(nrm[:, :], nrm[:, :], half[:, :], ALU.pow).then_inc(p_nrm, 1)

            def rstds(l, count):
                pool.wait_ge(v_var, count)
                pool.tensor_tensor(rstd[l][:, :], veps[l][:, :], minus_half[:, :], ALU.pow).then_inc(p_rs, 1)

            with pool.Fori(0, TURNS) as i:
                for l in range(LANES):
                    pool.wait_ge(ld_i[l], 16 * n_i.at("W", i, 1))
                    pool.wait_ge(ld_j[l], 16 * n_j.at("W", i, 1))
                    settle(pool)
                    for j in range(TG):
                        scatter(slot_of_node, jx[l][:, j:j + 1], ix[l][:, j:j + 1], sc[l], last_node)

            def gather_source(w, l):
                pool.wait_ge(ld_i[l], 16 * n_i.at("S", w, 1))
                settle(pool)
                if not no_wave(w - 1):
                    pool.wait_ge(s_cp, n_cp.at("S", w - 1, l + 1))
                    settle(pool)
                for j in range(TG):
                    gather(mm[l][:, j, :], x, ix[l][:, j:j + 1], gx[l], last_node)

            def gather_slots(w, l):
                if not no_wave(w - 1):
                    pool.wait_ge(st_j[l], 16 * n_stj.at("S", w))
                    settle(pool)
                for j in range(TG):
                    gather(jx[l][:, j:j + 1], slot_of_node, ix[l][:, j:j + 1], gj[l], last_node)

            plans["S"].run(pool, {"gather_x": gather_source, "gather_j": gather_slots,
                                  "variance": lambda w, l: rstds(l, norm_at("S", "norm", w, l, 1))})

            for r in range(ROUNDS):
                M, D = f"M{r}", f"D{r}"

                def keep_x(w, l):
                    pool.wait_ge(ld_x[l], 16 * (n_x.at(M, w) + 2))
                    settle(pool)
                    pool.wait_ge(st_o[l], 16 * n_sto.at(M, w))
                    settle(pool)
                    pool.tensor_copy(flat(on[l])[:, :], flat(xa[l])[:, :]).then_inc(s_cp, 1)

                def gather_m(w, l):
                    if r == 0:
                        return
                    pool.wait_ge(ld_m[l], 16 * n_m.at(M, w, 1))
                    pool.wait_ge(ld_j[l], 16 * n_j.at(M, w, 1))
                    settle(pool)
                    for j in range(TG):
                        gather(mm[l][:, j, :], slot_rows[r], jx[l][:, j:j + 1], gm[l], last_slot)

                def conv_rstds(w, _):
                    for l in range(LANES):
                        rstds(l, norm_at(M, "conv", w, 0, l + 1))

                plans[M].run(pool, {"copy_x": keep_x, "gather_m": gather_m, "conv": conv_rstds,
                                    "variance": lambda w, l: rstds(l, norm_at(M, "norm", w, l, 1))})

                def gather_dst(w, l):
                    pool.wait_ge(ld_i[l], 16 * n_i.at(D, w, 1))
                    settle(pool)
                    if not no_wave(w - 1):
                        pool.wait_ge(st_x[l], 16 * w)
                        settle(pool)
                        pool.wait_ge(s_ln, norm_at(D, "norm", w - 1, l, 1))
                        settle(pool)
                    for j in range(TG):
                        gather(mm[l][:, j, :], x, ix[l][:, j:j + 1], gx[l], last_node)

                if r == 0:
                    plans[D].run(pool, {"gather_x": gather_dst,
                                        "variance": lambda w, l: rstds(l, norm_at(D, "norm", w, l, 1))})
                if r == STEPS:
                    with pool.Fori(0, TURNS) as i:
                        for l in range(LANES):
                            pool.wait_ge(ld_i[l], 16 * n_i.at(D, i, 1))
                            pool.wait_ge(s_tof, tout.at(D, i, l + 1))
                            settle(pool)
                            for j in range(TG):
                                scatter(out, on[l][:, j, :], ix[l][:, j:j + 1], sc[l], last_node)

        @block.scalar
        def _(act):
            act.sem_inc(a_r, 1)
            act.sem_inc(a_n, 1)
            act.sem_inc(a_z, 1)
            act.sem_inc(aC, 1)
            act.wait_ge(s_vs, 1)
            nc.scalar.activation(emb_t, etmp, ACT.Exp, scale=-0.5 * (NB - 1) ** 2).then_inc(s_exp_a, 1)

            with act.Fori(0, TURNS) as i:
                for q in range(LANES + 2):
                    if q < LANES:
                        act.wait_ge(pA, n_lane.at("W", i, q + 1))
                        nc.scalar.activation(rT[q][0:HID, :], gate[0][0][0:HID, 0:G], ACT.Sigmoid,
                                             bias=mb[:, 0:1]).then_inc(aA, 1)
                    l = q - 1
                    if 0 <= l < LANES:
                        act.wait_ge(pB, n_lane.at("W", i, l + 1))
                        nc.scalar.activation(flat(mm[l])[0:HID, 0:G], gate[0][1][0:HID, 0:G], ACT.Sigmoid,
                                             bias=mb[:, 1:2]).then_inc(aB, 1)
                    l = q - 2
                    if 0 <= l < LANES:
                        act.wait_ge(pC, n_lane.at("W", i, l + 1))
                        nc.scalar.activation(flat(xn[l])[0:96, 0:G], gate[1][2][0:96, 0:G], ACT.Copy)
                        nc.scalar.activation(cc[l][:, 0:G], gate[0][2][:, 0:G], ACT.Identity,
                                             bias=mb2[:, 0:1]).then_inc(aC, 1)

            def first_state(ph, func):
                def step(w, l):
                    act.wait_ge(s_ti, ti_at(ph, "first", w, l))
                    nc.scalar.activation(hT[l][:, :], ti[:, 0:G], func).then_inc(s_tif, 1)
                    if ph == "S":
                        if not no_wave(w - 1):
                            act.wait_ge(s_tof, tout.at("S", w - 1, CELLS - LANES + l + 1))
                        nc.scalar.activation(flat(xa[l])[:, :], flat(mm[l])[:, :], ACT.Copy).then_inc(s_cp, 1)
                return step

            def cell_r(ph):
                def step(w, k):
                    act.wait_ge(g_r, cell.at(ph, w, k + 1) - 1)
                    nc.scalar.activation(rT[k % LANES][:, :], gate[k % 2][0][:, 0:G], ACT.Sigmoid,
                                         bias=bias[:, 6:7]).then_inc(a_r, 1)
                return step

            def cell_z(ph):
                def step(w, k):
                    act.wait_ge(g_z, cell.at(ph, w, k + 1) - 1)
                    nc.scalar.activation(zT[k % LANES][:, :], gate[k % 2][2][:, 0:G], ACT.Sigmoid,
                                         bias=bias[:, 7:8]).then_inc(a_z, 1)
                return step

            def cell_n(ph):
                def step(w, k):
                    if ph in slot:
                        act.wait_ge(s_tif, ti_at(ph, "cell", w, k, 1))
                    else:
                        act.wait_ge(v_t, cell.at(ph, w, k + 1))
                    nc.scalar.activation(nT[k % LANES][:, :], tT[k % LANES][:, :], ACT.Tanh,
                                         bias=bias[:, 2:3]).then_inc(a_n, 1)
                return step

            def cell_steps_of(ph):
                return {"cell": cell_r(ph), "late": cell_n(ph), "z": cell_z(ph)}

            def rows_copy(ph, w, c, l, stored):
                act.wait_ge(s_to, tout.at(ph, w, c + 1) - 1)
                act.wait_ge(st_o[l], 16 * stored)
                nc.scalar.activation(flat(on[l])[:, :], to[0:TP, :], ACT.Copy).then_inc(s_tof, 1)

            def sums_copy(w, l, use):
                act.wait_ge(s_ti, use)
                nc.scalar.activation(pt[l][:, :], ti[:, 0:TG * TE], ACT.Copy)
                nc.scalar.activation(part[:, bass.ds((w * LANES + l) * 2 * TG, 2 * TG)].rearrange("p (j b) -> p j b", b=2),
                                     ti[:, 0:TG * TE].rearrange("p (j e) -> p j e", e=TE)[:, :, TP:TE],
                                     ACT.Copy).then_inc(s_tif, 1)

            def step_rows(w, c):
                if c < CELLS - LANES:
                    rows_copy("S", w, c, c % LANES, n_sto.at("S", w, c // LANES + 1))

            plans["S"].run(act, {**cell_steps_of("S"), "first": first_state("S", ACT.Relu), "back": step_rows})

            for r in range(ROUNDS):
                M, D = f"M{r}", f"D{r}"

                def conv_copies(w, _):
                    act.wait_ge(v_h, cell.at(M, w, CELLS))
                    for q in range(LANES):
                        act.wait_ge(s_ti, ti_at(M, "conv", w, 0, q))
                        nc.scalar.activation(tT[q][:, :], ti[:, 0:G], ACT.Relu).then_inc(s_tif, 1)
                    for q in range(LANES + 2):
                        l = q - 1
                        if 0 <= l < LANES:
                            act.wait_ge(s_cn, n_cv.at(M, w, l + 1))
                            nc.scalar.activation(flat(mm[l])[:, :], gate[1][0][0:TP, :], ACT.Copy).then_inc(s_cf, 1)
                        l = q - 2
                        if 0 <= l < LANES:
                            sums_copy(w, l, ti_at(M, "conv", w, 0, LANES + l))

                plans[M].run(act, {**cell_steps_of(M), "first": first_state(M, ACT.Relu), "conv": conv_copies,
                                   "sum": lambda w, l: sums_copy(w, l, ti_at(M, "sum", w, l))})
                act.wait_ge(s_ti, tin.at(D, 0) - 1)
                nc.scalar.activation(bsum[:, 0, :], ti[0:ET, 0:2 * C], ACT.Copy).then_inc(s_bh, 1)
                act.wait_ge(s_tif, tin.at(D, 0))
                nc.scalar.activation(bsum[:, 1, :], brest[:, :], ACT.Copy).then_inc(s_bm, 1)
                if r < STEPS:
                    def slot_rows_copy(w, l):
                        if r < STEPS - 1:
                            rows_copy(D, w, l, l, n_sto.at(D, w))

                    plans[D].run(act, {**cell_steps_of(D), "first": first_state(D, ACT.Copy if r else ACT.Relu),
                                       "back": slot_rows_copy})

        @block.vector
        def _(dve):
            steps = [0]

            def link(ins):
                steps[0] += 1
                ins.then_inc(chain, 1)
                dve.wait_ge(chain, steps[0])

            def new_chain():
                dve.sem_clear(chain)
                steps[0] = 0

            V = nc.vector
            dve.sem_inc(v_t, 1)
            dve.sem_inc(v_h, 1)
            dve.sem_inc(s_tif, 1)
            dve.sem_inc(s_tof, 1)
            for s_ in (vA, vB, vC):
                dve.sem_inc(s_, 1)
            dve.wait_ge(s_seq, 48)
            V.tensor_copy(late[:, :], seq_i[0][:, :])
            link(V.tensor_copy(seq[:, :], seq_i[1][:, :]))
            link(V.tensor_tensor(late[:, :], late[:, :], seq[:, :], ALU.is_gt))
            V.tensor_reduce(late_p[:, :], late[:, :], AX.X, ALU.max).then_inc(v_late, 1)
            dve.wait_ge(s_late, 32)
            link(V.tensor_reduce(late_any[:, :], late_row[:, :], AX.X, ALU.max))
            V.tensor_copy(late_i[:, :], late_any[:, :]).then_inc(v_late, 1)
            for l in range(LANES):
                V.memset(cc[l][96:C, G:3 * G], 0.0)
            dve.wait_ge(s_id, 4)
            dve.wait_ge(s_idx, 16 * N_IDX)
            link(V.tensor_scalar(cen_i[:, :], cen_i[:, :], NB - 1, None, ALU.bitwise_and))
            link(V.tensor_copy(cen[:, :], cen_i[:, :]))
            link(V.tensor_scalar(cen[:, :], cen[:, :], 1.0 / (NB - 1), None, ALU.mult))
            link(V.tensor_scalar(etmp, wbc, 0.0, 1.0, ALU.max, ALU.min))
            link(V.tensor_scalar(etmp, etmp, cen[:, 0:1], None, ALU.subtract))
            V.tensor_tensor(etmp, etmp, etmp, ALU.mult).then_inc(s_vs, 1)
            V.tensor_copy(dcf[:, :], ic[1][:, :])
            link(V.tensor_copy(dpf[:, :], ic[2][:, :]))
            V.tensor_tensor(deq[:, :], dcf[:, :], dpf[:, :], ALU.is_equal)
            link(V.tensor_scalar(dfi[:, :], dcf[:, :], -1.0, float(NONE), ALU.mult, ALU.add))
            link(V.tensor_tensor(dfi[:, :], dfi[:, :], deq[:, :], ALU.mult))
            link(V.tensor_tensor(dfi[:, :], dfi[:, :], dcf[:, :], ALU.add))
            V.tensor_copy(ifirst[:, :], dfi[:, :])
            link(V.tensor_copy(drow[:, :], drow_i[:, :]))
            V.tensor_scalar(eqf[:, :], drow[:, :], drow[:, 0:1], None, ALU.is_equal)
            link(V.tensor_scalar(eql[:, :], drow[:, :], drow[:, TP - 1:TP], None, ALU.is_equal))
            link(V.tensor_tensor(eql[:, :], eqf[:, :], eql[:, :], ALU.max))
            link(V.scalar_tensor_tensor(eql[:, :], drow[:, :], 1.0, eql[:, :], ALU.add, ALU.mult))
            V.tensor_tensor(ext[:, 0:TP], drow[:, :], eql[:, :], ALU.subtract)
            V.tensor_copy(ext[:, TP:TP + 1], drow[:, 0:1])
            link(V.scalar_tensor_tensor(ext[:, TP + 1:TE], drow[:, TP - 1:TP], 1.0, eqf[:, TP - 1:TP],
                                        ALU.add, ALU.mult))
            link(V.tensor_tensor(ext[:, TP + 1:TE], drow[:, TP - 1:TP], ext[:, TP + 1:TE], ALU.subtract))
            V.tensor_copy(keys[:, :], ext[:, TP:TE])
            link(V.tensor_tensor(asq[:, :], attr_t[:, :], attr_t[:, :], ALU.mult))
            V.tensor_reduce(nrm[:, :], asq[:, :].rearrange("p (q c) -> p q c", c=3), AX.X, ALU.add).then_inc(v_sq, 1)
            dve.wait_ge(p_nrm, 1)
            link(V.tensor_scalar(nrm[:, :], nrm[:, :], 1e-12, None, ALU.add))
            link(V.reciprocal(inv[:, :], nrm[:, :]))
            for c in range(3):
                last = V.tensor_tensor(rh[:, c, :], attr_t[:, :].rearrange("p (q c) -> p c q", c=3)[:, c, :],
                                       inv[:, :], ALU.mult)
            last.then_inc(s_prep, 1)
            link(V.tensor_scalar(etmp2, wbc, 1.0, float(NB) ** 0.5, ALU.is_le, ALU.mult))
            dve.wait_ge(s_exp_a, 1)
            V.tensor_tensor(emb_t, emb_t, etmp2, ALU.mult).then_inc(s_exp, 1)

            dve.wait_ge(s_set, 16 * N_SET)
            V.tensor_tensor(bias[:, 6:9], bias[:, 0:3], bias[:, 3:6], ALU.add)
            for k, blocks in enumerate(((0, 2, 2, 2), (1, 1, 1), (3, 3, 3))):
                for q, b in enumerate(blocks):
                    V.tensor_copy(mw2x[:, k, q * MUL:(q + 1) * MUL], mw2[:, b * MUL:(b + 1) * MUL])
            V.tensor_scalar(up[:, :], up[:, :], float(MUL) ** -0.5, None, ALU.mult)
            V.tensor_scalar(upss[:, :], upss[:, :], float(MUL) ** -0.5, None, ALU.mult)
            for k, f in enumerate((1.0, 3.0 ** 0.5, 1.0)):
                V.tensor_scalar(wo[:, k, :], wo[:, k, :], f / (float(2 * MUL) ** 0.5 * 16.0), None, ALU.mult)
            dve.wait_ge(s_wt, 1)
            V.tensor_copy(flat(w_ihT)[:, :], ti[:, 0:3 * C])
            V.tensor_copy(flat(w_hT)[:, :], to[:, 0:3 * C]).then_inc(s_wc, 1)
            dve.wait_ge(s_wt, 2)
            V.tensor_copy(flat(w_pT)[:, :], gate[0][0][:, 0:3 * C]).then_inc(s_wc, 1)

            with dve.Fori(0, TURNS) as i:
                for l in range(LANES):
                    dve.wait_ge(ld_w[l], 16 * n_w.at("W", i, 5))
                    for j in range(TG):
                        V.tensor_scalar(mk[l][:, j * TE:(j + 1) * TE], pt[l][0:TP, j * TE:(j + 1) * TE],
                                        dc[l][:, j:j + 1], None, ALU.is_equal)
                    for b in range(2):
                        last = V.tensor_scalar(rm[l][:, b * G:(b + 1) * G], pf[l][0:ET, :], keys[:, b:b + 1],
                                               None, ALU.is_equal)
                    last.then_inc(v_m, 1)
                for q in range(LANES + 2):
                    if q < LANES:
                        dve.wait_ge(aA, n_lane.at("W", i, q + 1))
                        V.scalar_tensor_tensor(nT[q][0:HID, :], gate[0][0][0:HID, 0:G], mb[:, 0:1], rT[q][0:HID, :],
                                               ALU.add, ALU.mult).then_inc(vA, 1)
                    l = q - 1
                    if 0 <= l < LANES:
                        dve.wait_ge(aB, n_lane.at("W", i, l + 1))
                        V.scalar_tensor_tensor(zT[l][0:HID, :], gate[0][1][0:HID, 0:G], mb[:, 1:2],
                                               flat(mm[l])[0:HID, 0:G], ALU.add, ALU.mult).then_inc(vB, 1)
                    l = q - 2
                    if 0 <= l < LANES:
                        dve.wait_ge(aC, primed.at("W", i, l + 1))
                        for k in range(2):
                            last = V.scalar_tensor_tensor(
                                cc[l][0:96, (k + 1) * G:(k + 2) * G], gate[1][k][0:96, 0:G], mb2[0:96, k + 1:k + 2],
                                flat(xn[l])[0:96, 0:G], ALU.add, ALU.mult)
                        last.then_inc(vC, 1)

            def variance(l, rows):
                for j in range(TG):
                    last = V.bn_stats(stats[l][:, j, :], rows[:, j, :])
                link(last)
                for j in range(TG):
                    last = V.bn_aggr(mv[l][:, j, :], stats[l][:, j, :])
                link(last)
                V.tensor_scalar(veps[l][:, :], mv[l][:, :, 1], EPS, None, ALU.add).then_inc(v_var, 1)

            def norm(l, rows, out_rows, count):
                dve.wait_ge(p_rs, count)
                for j in range(TG):
                    last = V.tensor_scalar(out_rows[:, j, :], rows[:, j, :], mv[l][:, j, 0:1], rstd[l][:, j:j + 1],
                                           ALU.subtract, ALU.mult)
                last.then_inc(s_ln, 1)

            def cell_t(ph):
                def step(w, k):
                    l = k % LANES
                    dve.wait_ge(a_r, cell.at(ph, w, k + 1))
                    dve.wait_ge(g_n, cell.at(ph, w, k + 1) - 1)
                    V.scalar_tensor_tensor(tT[l][:, :], gate[k % 2][1][:, 0:G], bias[:, 5:6], rT[l][:, :],
                                           ALU.add, ALU.mult).then_inc(v_t, 1)
                    if ph in slot:
                        dve.wait_ge(v_t, cell.at(ph, w, k + 1))
                        dve.wait_ge(s_ti, ti_at(ph, "cell", w, k))
                        V.tensor_tensor(tT[l][:, :], tT[l][:, :], ti[:, 0:G], ALU.add).then_inc(s_tif, 1)
                return step

            def cell_h(ph):
                def step(w, k):
                    l = k % LANES
                    dve.wait_ge(a_n, cell.at(ph, w, k + 1))
                    link(V.tensor_tensor(tT[l][:, :], hT[l][:, :], nT[l][:, :], ALU.subtract))
                    dve.wait_ge(a_z, cell.at(ph, w, k + 1))
                    link(V.tensor_tensor(tT[l][:, :], zT[l][:, :], tT[l][:, :], ALU.mult))
                    V.tensor_tensor(hT[l][:, :], nT[l][:, :], tT[l][:, :], ALU.add).then_inc(v_h, 1)
                return step

            def rows_add(ph, w, c, l, rows):
                dve.wait_ge(s_to, tout.at(ph, w, c + 1) - 1)
                V.tensor_tensor(flat(on[l])[:, :], to[0:TP, :], flat(rows)[:, :], ALU.add).then_inc(s_tof, 1)

            def source_variance(w, l):
                dve.wait_ge(gx[l], 16 * n_gx.at("S", w, TG))
                variance(l, mm[l])

            def source_rows0(w, l):
                dve.wait_ge(s_ln, norm_at("S", "norm", w, l, 1))
                dve.wait_ge(st_o[l], 16 * n_sto.at("S", w))
                V.tensor_scalar(flat(on[l])[:, :], flat(xn[l])[:, :], 0.0, None, ALU.max).then_inc(s_h0, 1)

            def source_rows3(w, c):
                if c >= CELLS - LANES:
                    l = c % LANES
                    dve.wait_ge(s_cp, n_cp.at("S", w, l + 1))
                    dve.wait_ge(st_o[l], 16 * n_sto.at("S", w, STEPS))
                    rows_add("S", w, c, l, xa[l])

            plans["S"].run(dve, {"cell": cell_t("S"), "late": cell_h("S"), "back": source_rows3, "rows0": source_rows0,
                                 "variance": source_variance,
                                 "norm": lambda w, l: norm(l, mm[l], xn[l], norm_at("S", "norm", w, l, 1))}, new_chain)

            for r in range(ROUNDS):
                M, D = f"M{r}", f"D{r}"

                def x_variance(w, l):
                    dve.wait_ge(ld_x[l], 16 * (n_x.at(M, w) + 2))
                    variance(l, xa[l])

                def x_add(w, l):
                    dve.wait_ge(s_cp, n_cp.at(M, w, l + 1))
                    rows_add(M, w, l, l, on[l])

                def conv_messages(w, _):
                    for q in range(LANES):
                        dve.wait_ge(gm[q], 16 * n_gm.at(M, w, TG))
                        variance(q, mm[q])
                    for q in range(LANES):
                        norm(q, mm[q], mm[q], norm_at(M, "conv", w, 0, q + 1))
                    for q in range(LANES):
                        dve.wait_ge(s_up, n_cv.at(M, w, q + 1))
                        dve.wait_ge(ld_c[q], 16 * n_c.at(M, w, 1))
                        V.tensor_tensor(rT[q][:, :], gate[0][0][:, 0:G], cc[q][:, 0:G], ALU.mult)
                        V.tensor_tensor(zT[q][0:96, :], gate[0][1][0:96, 0:G], cc[q][0:96, G:2 * G], ALU.mult)
                        V.tensor_tensor(nT[q][0:96, :], gate[0][2][0:96, 0:G], cc[q][0:96, 2 * G:3 * G],
                                        ALU.mult).then_inc(s_pr, 1)

                plans[M].run(dve, {"cell": cell_t(M), "late": cell_h(M), "back": x_add, "variance": x_variance,
                                   "norm": lambda w, l: norm(l, xa[l], xn[l], norm_at(M, "norm", w, l, 1)),
                                   "conv": conv_messages}, new_chain)
                dve.wait_ge(s_bh, r + 1)
                V.tensor_tensor(brest[:, :], ti[0:ET, 0:2 * C], bsum[:, 0, :], ALU.subtract).then_inc(s_tif, 1)
                dve.wait_ge(s_bm, r + 1)
                V.tensor_tensor(bsum[:, 2, :], brest[:, :], bsum[:, 1, :], ALU.subtract).then_inc(s_bl, 1)

                def whole_sums(w, l, use):
                    dve.wait_ge(s_ti, use)
                    dve.wait_ge(ld_p[l], 16 * n_p.at(D, w, 1))
                    V.tensor_tensor(pf[l][:, :].rearrange("p (j e) -> p j e", e=TP),
                                    ti[:, 0:G].rearrange("p (j e) -> p j e", e=TP),
                                    pt[l][:, :].rearrange("p (j e) -> p j e", e=TE)[:, :, 0:TP],
                                    ALU.add).then_inc(s_tif, 1)

                def dst_variance(w, l):
                    dve.wait_ge(gx[l], 16 * n_gx.at(D, w, TG))
                    variance(l, mm[l])

                def slot_add(w, l):
                    if r == STEPS - 1:
                        dve.wait_ge(ld_b[l], 16 * n_b.at(D, w, 1))
                        dve.wait_ge(st_o[l], 16 * n_sto.at(D, w))
                        rows_add(D, w, l, l, xn[l])

                if r < STEPS:
                    plans[D].run(dve, {"cell": cell_t(D), "late": cell_h(D), "back": slot_add,
                                       "spread": lambda w, l: whole_sums(w, l, ti_at(D, "spread", w, l)),
                                       "variance": dst_variance,
                                       "norm": lambda w, l: norm(l, mm[l], xn[l], norm_at(D, "norm", w, l, 1))},
                                 new_chain)
                else:
                    with dve.Fori(0, TURNS) as i:
                        for l in range(LANES):
                            whole_sums(i, l, tin.at(D, i, l + 1) - 1)
                            dve.wait_ge(sc[l], 16 * n_scat.at(D, i))
                            dve.wait_ge(ld_m[l], 16 * n_m.at(D, i, 1))
                            dve.wait_ge(st_o[l], 16 * n_sto.at(D, i))
                            rows_add(D, i, l, l, mm[l])

        @block.tensor
        def _(pe):
            T = nc.tensor
            pe.wait_ge(s_id, 4)
            pe.wait_ge(s_set, 16 * N_SET)
            for k in range(6):
                last = T.transpose((ti, to)[k // 3][:, (k % 3) * C:(k % 3 + 1) * C], w_raw[:, k, :], ident[:, :])
            last.then_inc(s_wt, 1)
            pe.wait_ge(s_wc, 1)
            T.matmul(gate[0][0][:, 0:3 * C], w_lin[:, :], flat(w_ihT)[:, :], start=True, stop=True).then_inc(s_wt, 1)
            pe.wait_ge(s_wc, 2)

            with pe.Fori(0, TURNS) as i:
                for q in range(LANES + 2):
                    if q < LANES:
                        pe.wait_ge(ld_w[q], 16 * n_w.at("W", i, 5))
                        pe.wait_ge(vA, primed.at("W", i, q))
                        T.matmul(gate[0][0][0:HID, 0:G], mw0[:, :], tT[q][0:NB, :], start=True, stop=True).then_inc(pA, 1)
                    l = q - 1
                    if 0 <= l < LANES:
                        pe.wait_ge(vA, primed.at("W", i, l + 1))
                        pe.wait_ge(vB, primed.at("W", i, l))
                        T.matmul(gate[0][1][:, 0:G], mw1[:, :], nT[l][0:HID, :], start=True, stop=True).then_inc(pB, 1)
                    l = q - 2
                    if 0 <= l < LANES:
                        pe.wait_ge(vB, primed.at("W", i, l + 1))
                        pe.wait_ge(vC, primed.at("W", i, l))
                        pe.wait_ge(aC, primed.at("W", i, l))
                        T.matmul(gate[0][2][:, 0:G], mw2x[:, 0, :], zT[l][0:HID, :], start=True, stop=True)
                        for k in range(2):
                            T.matmul(gate[1][k][0:96, 0:G], mw2x[:, k + 1, 0:96], zT[l][0:HID, :], start=True, stop=True)
                        T.matmul(gate[1][2][0:96, 0:G], sel3[:, :], hT[l][0:3, :], start=True, stop=True).then_inc(pC, 1)
            pe.wait_ge(vC, primed.total)
            pe.wait_ge(aC, primed.total)

            def rows_to_cols(rows, use):
                pe.wait_ge(s_tif, use)
                for j in range(TG):
                    last = T.transpose(ti[:, j * TP:(j + 1) * TP], rows[:, j, :], ident[0:TP, 0:TP])
                last.then_inc(s_ti, 1)

            def cols_to_rows(ph, i, u, cols):
                pe.wait_ge(s_tof, tout.at(ph, i, u))
                for j in range(TG):
                    last = T.transpose(to[0:TP, j * C:(j + 1) * C], cols[:, j * TP:(j + 1) * TP], ident[:, :])
                last.then_inc(s_to, 1)

            def cell_gates(ph):
                def step(w, k):
                    l, st = k % LANES, gate[k % 2]
                    if k < LANES:
                        pe.wait_ge(s_tif, ti_at(ph, "first", w, l, 1))
                    else:
                        pe.wait_ge(v_h, cell.at(ph, w, k - LANES + 1))
                    before = cell.at(ph, w, max(k - 1, 0))
                    for b, (g, full, read) in enumerate(((0, g_r, a_r), (2, g_n, v_t), (1, g_z, a_z))):
                        pe.wait_ge(read, before)
                        both = ph in slot and g != 2
                        last = T.matmul(st[b][:, 0:G], w_hT[:, g, :], hT[l][:, :], start=True, stop=not both)
                        if both:
                            last = T.matmul(st[b][:, 0:G], w_pT[:, g, :], pf[l][:, :], start=False, stop=True)
                        last.then_inc(full, 1)
                        if ph in slot and g == 2:
                            pe.wait_ge(s_tif, ti_at(ph, "cell", w, k))
                            T.matmul(ti[:, 0:G], w_pT[:, 2, :], pf[l][:, :], start=True, stop=True).then_inc(s_ti, 1)
                return step

            def sum_tiles(ph, w, l, use):
                pe.wait_ge(ld_k[l], 16 * n_k.at(ph, w, 1))
                pe.wait_ge(s_tif, use)
                for j in range(TG):
                    last = T.matmul(ti[:, j * TE:(j + 1) * TE], mm[l][:, j, :], mk[l][:, j * TE:(j + 1) * TE],
                                    start=True, stop=True)
                last.then_inc(s_ti, 1)

            def normed_to_cols(ph):
                def step(w, l):
                    pe.wait_ge(s_ln, norm_at(ph, "norm", w, l, 1))
                    rows_to_cols(xn[l], ti_at(ph, "first", w, l))
                return step

            def back(ph):
                def step(w, part):
                    c = part if ph == "S" else part + (0 if ph in slot else CELLS - LANES)
                    pe.wait_ge(v_h, cell.at(ph, w, c + 1))
                    cols_to_rows(ph, w, part, hT[c % LANES])
                return step

            plans["S"].run(pe, {"cell": cell_gates("S"), "first": normed_to_cols("S"), "back": back("S")})

            for r in range(ROUNDS):
                M, D = f"M{r}", f"D{r}"

                def message_sums(w, l):
                    if r:
                        pe.wait_ge(gm[l], 16 * n_gm.at(M, w, TG))
                    else:
                        pe.wait_ge(ld_m[l], 16 * n_m.at(M, w, 1))
                    sum_tiles(M, w, l, ti_at(M, "sum", w, l))

                def conv_messages(w, _):
                    for q in range(LANES):
                        pe.wait_ge(s_ln, norm_at(M, "conv", w, 0, q + 1))
                        rows_to_cols(mm[q], ti_at(M, "conv", w, 0, q))
                    for read in (a_r, v_t, a_z):
                        pe.wait_ge(read, cell.at(M, w, CELLS))
                    for q in range(LANES + 2):
                        if q < LANES:
                            pe.wait_ge(s_tif, ti_at(M, "conv", w, 0, q + 1))
                            if q:
                                pe.wait_ge(s_pr, n_cv.at(M, w, q))
                            T.matmul(gate[0][0][:, 0:G], up[:, :], tT[q][:, :], start=True, stop=True)
                            T.matmul(gate[0][1][0:96, 0:G], upss[:, :], tT[q][:, :], start=True, stop=True)
                            T.matmul(gate[0][2][0:96, 0:G], up[:, MUL:C], tT[q][:, :], start=True,
                                     stop=True).then_inc(s_up, 1)
                        l = q - 1
                        if 0 <= l < LANES:
                            pe.wait_ge(s_pr, n_cv.at(M, w, l + 1))
                            if l:
                                pe.wait_ge(s_cf, n_cv.at(M, w, l))
                            for j in range(TG):
                                cols = slice(j * TP, (j + 1) * TP)
                                o = gate[1][0][0:TP, j * C:(j + 1) * C]
                                T.matmul(o, rT[l][:, cols], wo[:, 0, :], start=True, stop=False)
                                T.matmul(o, zT[l][0:96, cols], wo[0:96, 1, :], start=False, stop=False)
                                last = T.matmul(o, nT[l][0:96, cols], wo[0:96, 2, :], start=False, stop=True)
                            last.then_inc(s_cn, 1)
                        l = q - 2
                        if 0 <= l < LANES:
                            pe.wait_ge(s_cf, n_cv.at(M, w, l + 1))
                            sum_tiles(M, w, l, ti_at(M, "conv", w, 0, LANES + l))

                plans[M].run(pe, {"cell": cell_gates(M), "first": normed_to_cols(M), "back": back(M),
                                  "sum": message_sums, "conv": conv_messages})
                pe.wait_ge(s_tif, tin.at(M, TURNS))
                for b in range(2):
                    last = T.transpose(ti[0:ET, b * C:(b + 1) * C],
                                       part[:, :].rearrange("p (t b) -> p b t", b=2)[:, b, :], ident[:, :])
                last.then_inc(s_ti, 1)
                pe.wait_ge(s_bl, r + 1)

                def spread(w, l, use):
                    pe.wait_ge(ld_r[l], 16 * n_p.at(D, w, 1))
                    pe.wait_ge(s_tif, use)
                    for b in range(2):
                        for m in range(3):
                            last = T.matmul(ti[:, 0:G], bsum[:, m, b * C:(b + 1) * C], rm[l][:, b * G:(b + 1) * G],
                                            start=b == m == 0, stop=b == 1 and m == 2)
                    last.then_inc(s_ti, 1)

                def slot_states(w, l):
                    pe.wait_ge(ld_m[l], 16 * n_m.at(D, w, 1))
                    rows_to_cols(mm[l], ti_at(D, "first", w, l))

                if r < STEPS:
                    plans[D].run(pe, {"spread": lambda w, l: spread(w, l, ti_at(D, "spread", w, l)),
                                      "cell": cell_gates(D), "back": back(D),
                                      "first": slot_states if r else normed_to_cols(D)})
                else:
                    with pe.Fori(0, TURNS) as i:
                        for l in range(LANES):
                            spread(i, l, tin.at(D, i, l))
                            pe.wait_ge(s_tif, tin.at(D, i, l + 1))
                            cols_to_rows(D, i, l, pf[l])


_INS = ["x", "src", "dst", "edge_attr_3", "edge_weight", "L0_gnn_W_lin", "L0_gnn_W_ih", "L0_gnn_W_hh",
        "L0_gnn_b_ih", "L0_gnn_b_hh", "L1_gnn_W_up0", "L1_gnn_W_up1", "L1_gnn_mlp_w0", "L1_gnn_mlp_b0",
        "L1_gnn_mlp_w1", "L1_gnn_mlp_b1", "L1_gnn_mlp_w2", "L1_gnn_mlp_b2", "L1_gnn_W_out0", "L1_gnn_W_out1"]


def kernel(**inputs):
    import numpy as _np
    import concourse.bacc as _bacc
    from concourse import mybir as _mybir
    from concourse.bass_utils import run_bass_kernel_spmd as _run

    nc = _bacc.Bacc("TRN2", target_bir_lowering=False, num_devices=1)
    arrays, args = {}, []
    for name in _INS:
        a = _np.ascontiguousarray(inputs[name])
        arrays[f"in_{name}"] = a
        args.append(nc.dram_tensor(f"in_{name}", a.shape, _mybir.dt.from_np(a.dtype), kind="ExternalInput").ap())
    shape = inputs["x"].shape
    args.append(nc.dram_tensor("out_0", shape, _mybir.dt.float32, kind="ExternalOutput").ap())
    gnn_kernel(nc, *args)
    r = _run(nc, [arrays], core_ids=[0])
    return r.results[0]["out_0"]
```

```python
from contextlib import ExitStack

import numpy as np

import concourse.bass as bass
from concourse import mybir

F32 = mybir.dt.float32
BF16 = mybir.dt.bfloat16
I32 = mybir.dt.int32
ALU = mybir.AluOpType
ACT = mybir.ActivationFunctionType
AX = mybir.AxisListType

C = 128
TP = 125
TG = 4
G = TP * TG
LANES = 5
STEPS = 3
TE = TP + 2
NONE = 1 << 20
NB = 8
MUL = 32
HID = 64
EPS = 1e-5
LAG = 4
SLOT_LAG = 3
SPLIT = 112


class Plan:

    def __init__(self, turns, period, steps, waves=None):
        self.turns, self.period, self.steps, self.waves = turns, period, steps, waves or {}

    def in_slot(self, g):
        for name, ahead, slots in self.steps:
            for part, slot in enumerate(slots):
                if (g - slot) % self.period == 0:
                    yield name, part, (g - slot) // self.period + ahead

    def exists(self, name, wave):
        return wave in self.waves.get(name, range(self.turns))

    def order(self, uses):
        place, at = {}, 0
        for g in range(-2 * self.period, (self.turns + 2) * self.period):
            for name, part, wave in self.in_slot(g):
                if name in uses and self.exists(name, wave):
                    place[name, part, wave] = at
                    at += uses[name]
        per = at // self.turns

        def at_step(name, wave, part=0):
            if isinstance(wave, int):
                return place[name, part, wave]
            return wave * per + (place[name, part, 2] - 2 * per)

        return at_step

    def run(self, eng, does, head=None):
        def slots(first, last, turn=None):
            for g in range(first, last):
                for name, part, wave in self.in_slot(g):
                    if name not in does:
                        continue
                    if turn is not None:
                        does[name](turn + wave if wave else turn, part)
                    elif self.exists(name, wave):
                        does[name](wave, part)

        if head:
            head()
        slots(-2 * self.period, self.period)
        with eng.Fori(1, self.turns - 1) as i:
            if head:
                head()
            slots(0, self.period, i)
        if head:
            head()
        slots((self.turns - 1) * self.period, (self.turns + 2) * self.period)


class Ledger:

    def __init__(self, phases, turns, per, start=0):
        self.start, self.per = {}, per
        at = start
        for p in phases:
            self.start[p] = at
            at += turns * per.get(p, 0)
        self.total = at

    def at(self, phase, i, k=0):
        return i * self.per.get(phase, 0) + (self.start[phase] + k)


def gnn_kernel(nc, x, src, dst, edge_attr, edge_weight, W_lin, W_ih, W_hh, b_ih, b_hh, W_up0, W_up1,
               mlp_w0, mlp_b0, mlp_w1, mlp_b1, mlp_w2, mlp_b2, W_out0, W_out1, out):
    N = x.shape[0]
    E = src.shape[0]
    NG, EG, ET = N // G, E // G, E // TP
    assert x.shape[1] == C and N % G == 0 and E % G == 0 and EG % LANES == 0
    TURNS = EG // LANES
    assert NG == 4 * TURNS * LANES
    ROUNDS = STEPS + 1
    PHASES = ["W", "S"] + [f"{a}{r}" for r in range(ROUNDS) for a in "MD"]
    CELLS = STEPS * LANES
    free = ["S"] + [f"M{r}" for r in range(ROUNDS)]
    slot = [f"D{r}" for r in range(STEPS)]

    def ledger(start=0, **per):
        return Ledger(PHASES, TURNS, per, start)

    cell = ledger(1, **{p: CELLS for p in free}, **{p: LANES for p in slot})
    tin_per = {"S": LANES, "D3": LANES, "M3": 3 * LANES}
    tin_per |= {f"M{r}": 2 * LANES for r in range(STEPS)} | {p: 3 * LANES for p in slot}
    tin = ledger(1, **tin_per)
    for r in range(ROUNDS):
        for p in PHASES[PHASES.index(f"D{r}"):]:
            tin.start[p] += 1
    tout = ledger(1, S=CELLS, M0=LANES, M1=LANES, M2=LANES, M3=LANES, **{p: LANES for p in slot}, D3=LANES)

    LN = (4, 6, 8, 10, 11)
    BACK = CELLS - LANES + LAG
    cell_steps = [("cell", 0, range(CELLS)), ("tanh", 0, range(1, CELLS + 1)), ("z", 0, range(CELLS)),
                  ("late", 0, range(2, CELLS + 2))]
    FIRST = (9, 11, 13, 15, 16)
    SHARED = range(1, CELLS, 2)
    pairs = [3 + p // 2 for p in range(TG * LANES)]
    plans = {"W": Plan(TURNS, LANES, [
        ("mlp1", 0, range(LANES)),
        ("mlp2", 0, range(1, LANES + 1)),
        ("fac", 0, range(2, LANES + 2)),
        ("store_c", 0, range(3, LANES + 3)),
        ("load_e", 1, range(3, LANES + 3))])}
    plans |= {"S": Plan(TURNS, CELLS, [
        *cell_steps,
        ("back", 0, range(LAG, CELLS + LAG)),
        ("first", 1, FIRST),
        ("keep_x", 1, range(BACK, BACK + LANES)),
        ("rows0", 1, range(BACK + 2, BACK + 2 + LANES)),
        ("load_i", 1, range(LANES)),
        ("load_w", 0, (0, 1, 2, 4, 5)),
        ("gather_x", 1, [1 + p // 3 for p in range(TG * LANES)]),
        ("variance", 1, LN),
        ("scatter_j", 0, [8 + p // 3 for p in range(TG * LANES)]),
        ("norm", 1, [k + 2 for k in LN]),
        ("masks", 0, (5, 7, 9, 14, 15)),
        ("store_w", 0, (7, 9, 11, 16, 17))],
        waves={"load_i": range(1, TURNS)})}
    for r in range(ROUNDS):
        conv = r == STEPS
        plans[f"M{r}"] = Plan(TURNS, CELLS + LANES + 1 if conv else CELLS, [
            *([("conv_sum", 0, range(CELLS + 3, CELLS + LANES + 3))] if conv else []),
            *cell_steps,
            *([] if conv else [("sum", 0, [k + (4 if r else 3) for k in LN])]),
            ("back", 0, range(BACK, BACK + LANES)),
            ("first", 1, range(BACK, BACK + LANES) if conv else FIRST),
            ("copy_x", 1, range(BACK + 2, BACK + 2 + LANES)),
            ("load_x", 1, range(2, LANES + 2)),
            ("load_m", 0, range(LANES)),
            ("variance", 1, LN),
            ("gather_m", 0, pairs),
            *([] if r else [("load_i", 0, range(LANES)), ("gather_j", 0, pairs), ("store_j", 0, [k + 4 for k in LN])]),
            ("norm", 1, [k + 2 for k in LN]),
            *([("conv_variance", 0, (8, 10, 12, 13, 14)), ("conv_norm", 0, (10, 12, 14, 15, 16)),
               ("conv_cols", 0, (12, 14, 16, 17, 18)),
               ("conv_up", 0, range(CELLS, CELLS + LANES)),
               ("conv_rows", 0, range(CELLS + 1, CELLS + LANES + 1))] if conv else []),
            ("store_sum", 0, range(CELLS + 4, CELLS + LANES + 4) if conv else [k + (5 if r else 4) for k in LN])],
            waves={"load_x": range(1, TURNS if conv else TURNS + 1)})
    for r in range(STEPS):
        d = SLOT_LAG if r else SLOT_LAG + 1
        plans[f"D{r}"] = Plan(TURNS, LANES, [
            ("spread", 1, range(d, d + LANES)),
            ("cell", 0, range(LANES)), ("tanh", 0, range(1, LANES + 1)), ("late", 0, range(1, LANES + 1)),
            ("z", 0, range(LANES)),
            ("back", 0, range(SLOT_LAG, LANES + SLOT_LAG)),
            ("first", 1, range(d, d + LANES)),
            ("load", 1, range(LANES)),
            *([("load_x", 0, range(LANES))] if r == STEPS - 1 else []),
            *([] if r else [
                ("gather_x", 1, range(LANES)),
                ("store_x", 1, range(1, LANES + 1)),
                ("variance", 1, range(2, LANES + 2)),
                ("norm", 1, range(3, LANES + 3))])])
    plans[f"D{STEPS}"] = Plan(TURNS, LANES, [
        ("spread", 0, range(LANES)),
        ("back", 0, range(1, LANES + 1)),
        ("load", 1, range(3, LANES + 3)),
        ("scatter", 0, range(1, LANES + 1))])
    ti_use, to_use, norm_use = {}, {}, {}
    for ph, plan in plans.items():
        uses = {"first": 1, "sum": 1, "spread": 1, "conv_cols": 1, "conv_sum": 1} | ({"cell": 1} if ph in slot else {})
        ti_use[ph] = plan.order(uses)
        to_use[ph] = plan.order({"back": 1})
        norm_use[ph] = plan.order({"norm": 1, "conv_norm": 1})

    with ExitStack() as ctx:
        def sb(name, shape, dt=F32):
            return ctx.enter_context(nc.sbuf_tensor(name, shape, dt))

        def lanes(name, shape, dt=F32):
            return [sb(f"{name}{l}", shape, dt) for l in range(LANES)]

        def bank(name):
            return ctx.enter_context(nc.psum_tensor(name, [C, 512], F32))

        def sem(name):
            return ctx.enter_context(nc.semaphore(name))

        def sems(name):
            return [sem(f"{name}{l}") for l in range(LANES)]

        def dram(name, shape, dt=F32):
            return nc.dram_tensor(name, shape, dt).ap()

        src_s = dram("src_sorted", [E], I32)
        dst_pad = dram("dst_sorted", [E + 1], I32)
        dst_s = dst_pad[1:E + 1]
        weight_s = dram("weight_sorted", [E])
        attr_s = dram("attr_sorted", [E, 3])
        late_col = dram("late_col", [TP])
        ranks = dram("ranks", [2, TP, ET], I32)
        slot_of_node = dram("slot_of_node", [N, 1], I32)
        idx_src = dram("idx_src", [EG, TP, TG], I32)
        idx_dst = dram("idx_dst", [EG, TP, TG], I32)
        idx_first = dram("idx_first", [EG, TP, TG], I32)
        idx_slot = dram("idx_slot", [EG, TP, TG], I32)
        edge_id = dram("edge_id", [EG, TP, TG], I32)
        dst_col = dram("dst_col", [EG, TP, TG])
        dst_rows = dram("dst_rows", [EG, G])
        mask_keys = dram("mask_keys", [EG, TG * TE])
        tile_masks = dram("tile_masks", [EG, TP, TG * TE])
        key_masks = dram("key_masks", [EG, ET, 2 * G], BF16)
        emb_d = dram("emb", [NB, E])
        rhat_d = dram("rhat", [3, E])
        conv_d = dram("conv_factors", [EG, C, 3 * G])
        src_rows = [dram(f"src_rows{r}", [E, C]) for r in range(ROUNDS)]
        slot_rows = [None] + [dram(f"slot_rows{r}", [E, C]) for r in range(1, ROUNDS)]
        dst_x = dram("dst_x", [E, C])
        sums_d = dram("sums", [EG, C, TG * TE])

        x_dense = x.rearrange("(g p j) c -> g p j c", p=TP, j=TG)
        out_dense = out.rearrange("(g p j) c -> g p j c", p=TP, j=TG)

        def by_tile(rows):
            return rows.rearrange("(g j p) c -> g p j c", p=TP, j=TG)

        ident = sb("ident", [C, C])
        w_raw = sb("w_raw", [C, 6, C])
        w_lin = sb("w_lin", [C, C])
        w_ihT = sb("w_ihT", [C, 3, C])
        w_hT = sb("w_hT", [C, 3, C])
        w_pT = sb("w_pT", [C, 3, C])
        bias = sb("bias", [C, 9])
        up = sb("up", [C, C])
        upss = sb("upss", [C, 96])
        mw0 = sb("mw0", [NB, C])
        mw1 = sb("mw1", [C, C])
        mw2 = sb("mw2", [C, 4 * MUL])
        mw2x = sb("mw2x", [C, 3, C])
        mb = sb("mb", [C, 2])
        mb2 = sb("mb2", [C, 3])
        wo = sb("wo", [C, 3, C])
        part = sb("part", [C, ET * 2])
        keys = sb("keys", [ET, 2])
        bsum = sb("bsum", [ET, 3, 2 * C], BF16)
        brest = sb("brest", [ET, 2 * C])
        xa_xn = sb("xa_xn", [TP, 2 * LANES, TG, C])
        mm_on = sb("mm_on", [TP, 2 * LANES, TG, C])
        xa, xn, mm, on = ([t[:, k * LANES + l] for l in range(LANES)] for t in (xa_xn, mm_on) for k in range(2))
        hT = lanes("hT", [C, G])
        rT = lanes("rT", [C, G])
        zT = lanes("zT", [C, G])
        nT = lanes("nT", [C, G])
        tT = lanes("tT", [C, G])
        pt = lanes("pt", [C, TG * TE])
        pf = lanes("pf", [C, G])
        mk = lanes("mk", [TP, TG * TE])
        rm = lanes("rm", [ET, 2 * G], BF16)
        cc = lanes("cc", [C, 3 * G])
        ix = lanes("ix", [TP, TG], I32)
        jx = lanes("jx", [TP, TG], I32)
        fx = lanes("fx", [TP, TG], I32)
        dc = lanes("dc", [TP, TG])
        stats = lanes("stats", [TP, TG, 6])
        mv = lanes("mv", [TP, TG, 2])
        veps = lanes("veps", [TP, TG])
        minus_half = sb("minus_half", [TP, TG])
        half = sb("half", [TP, ET])
        rstd = lanes("rstd", [TP, TG])

        def third(l, k, rows=C):
            return cc[l][0:rows, k * G:(k + 1) * G]

        sig1, act1, sig2, act2 = third(1, 0), third(1, 1), third(2, 0), third(2, 1)
        emb_in = [third(1, 2, NB), third(2, 2, NB)] + [third(3, k, NB) for k in range(3)]
        rhat_in = [pf[l][0:96, :] for l in range(LANES)]
        factors = [cc[0], cc[4]]

        NCH = 10
        CH = E // NCH
        assert E % NCH == 0 and NB * NCH <= C and CH <= 3 * G
        wbc, emb_t, etmp = (cc[k][0:NB * NCH, 0:CH] for k in range(3))
        first_h = {ph: hT if ph == "M3" else [third(l, 0) for l in range(LANES)] for ph in plans if ph != "W"}
        ic = [sb(f"ic{k}", [TP, ET], I32) for k in range(3)]
        ifirst, eid = sb("ifirst", [TP, ET], I32), sb("eid", [TP, ET], I32)
        dcf, dpf, deq, dfi = (sb(n, [TP, ET]) for n in ("dcf", "dpf", "deq", "dfi"))
        drow_i = sb("drow_i", [ET, TP], I32)
        drow, eqf, eql = (sb(n, [ET, TP]) for n in ("drow", "eqf", "eql"))
        ext = sb("ext", [ET, TE])
        none_t = sb("none_t", [TP, N // TP], I32)
        minus1 = sb("minus1", [1, 1], I32)
        attr_t = sb("attr_t", [TP, 3 * ET])
        asq = sb("asq", [TP, 3 * ET])
        rh = sb("rh", [TP, 3, ET])
        nrm, inv = sb("nrm", [TP, ET]), sb("inv", [TP, ET])
        etmp2 = cc[3][0:NB * NCH, 0:CH]
        cen_i, cen = sb("cen_i", [NB * NCH, 1], I32), sb("cen", [NB * NCH, 1])
        seq_i = [sb(f"seq_i{k}", [TP, ET], I32) for k in range(2)]
        seq, late, edge_f, dst_f = (sb(n, [TP, ET]) for n in ("seq", "late", "edge_f", "dst_f"))
        late_p, late_row, late_any = sb("late_p", [TP, 1]), sb("late_row", [1, TP]), sb("late_any", [1, 1])
        late_i, rank_i = sb("late_i", [1, 1], I32), sb("rank_i", [TP, ET], I32)
        RCH = 50
        assert E % RCH == 0 and ET * RCH <= 2 * LANES * TG * C
        other_i, other, other_d = sb("other_i", [TP, RCH], I32), sb("other", [TP, RCH]), sb("other_d", [TP, RCH])
        compared, counted = (t[:, :, :, :].rearrange("p a j c -> p (a j c)")[:, 0:ET * RCH].rearrange(
            "p (t f) -> p t f", f=RCH) for t in (xa_xn, mm_on))
        move_rank = sb("move_rank", [TP, 2, TG], I32)
        move_src, move_dst = (sb(n, [TP, TG], I32) for n in ("move_src", "move_dst"))
        move_w, move_attr = sb("move_w", [TP, TG]), sb("move_attr", [TP, TG, 3])
        N_SET = 3 + 3 + 4 + 10 + 1 + 6 + 1 + 9
        N_IDX = 4 + NCH + 1
        N_TAB = 5 + 2 + 3 + NCH

        gate = [[bank(f"{g}{s}") for g in "rnz"] for s in range(2)]
        ti, to = bank("ti"), bank("to")

        s_settle = sem("settled")
        s_seq = sem("edge_order_loaded")
        s_late = sem("edge_order_moved")
        v_late = sem("edge_order_found")
        s_copied = sem("edges_copied")
        s_order = sem("edges_sorted")
        s_ranks = sem("ranks_stored")
        s_other, s_move, s_moved = sem("others_loaded"), sem("unsorted_loaded"), sem("edges_moved")
        s_set = sem("setup_loaded")
        s_id = sem("ident_steps")
        s_cst = sem("pool_constants")
        s_wt = sem("weights_transposed")
        s_wc = sem("weights_copied")
        s_idx = sem("index_steps_loaded")
        s_prep = sem("tables_ready")
        s_tab = sem("tables_stored")
        s_exp_a, s_exp = sem("exp_done"), sem("radial_ready")
        s_vs = sem("vector_setup")
        chain = sem("vector_chain")
        pchain = sem("pool_chain")
        g_r, g_n, g_z = sem("gate_r_summed"), sem("gate_n_summed"), sem("gate_z_summed")
        a_r, a_n, a_z = sem("r_ready"), sem("n_ready"), sem("z_ready")
        v_t, v_h = sem("t_ready"), sem("state_ready")
        s_ti, s_tif = sem("ti_full"), sem("ti_free")
        s_to, s_tof = sem("to_full"), sem("to_free")
        s_ln = sem("normed")
        v_var, p_rs = sem("variances"), sem("rstd_ready")
        v_sq, p_nrm = sem("edge_squares"), sem("edge_norms")
        s_h0 = sem("first_rows_ready")
        s_cp = sem("rows_kept")
        p_d = sem("differences")
        s_pf = sem("pf_ready")
        ld_x, ld_m, ld_k, ld_i, ld_j = sems("ld_x"), sems("ld_m"), sems("ld_k"), sems("ld_i"), sems("ld_j")
        ld_p, ld_b, ld_c, ld_w = sems("ld_p"), sems("ld_b"), sems("ld_c"), sems("ld_w")
        gx, gj, gm = sems("gather_x"), sems("gather_slot"), sems("gather_rows")
        st_o, st_j, st_p, st_x, st_w = sems("st_o"), sems("st_j"), sems("st_p"), sems("st_x"), sems("st_w")
        sc = sems("scattered")
        pA, pB, pC = sem("mlp1_summed"), sem("mlp2_summed"), sem("factors_summed")
        aA, aB, aC = sem("mlp1_sigmoid"), sem("mlp2_sigmoid"), sem("factor0_ready")
        vA, vB, vC = sem("mlp1_ready"), sem("mlp2_ready"), sem("factors_ready")
        st_c = [sem("st_c0"), sem("st_c1")]
        ld_e, ld_f = ld_b, ld_c
        v_m = sem("masks_ready")
        s_bt, s_bh, s_br, s_bm, s_bl = (sem("bnd_T"), sem("bnd_hi"), sem("bnd_rest"), sem("bnd_mid"),
                                        sem("bnd_lo"))
        s_up = sem("conv_up")
        s_pr = sem("conv_products")
        s_cn = sem("conv_rows")
        s_cf = sem("conv_rows_copied")

        Ms = [f"M{r}" for r in range(ROUNDS)]
        Ds = [f"D{r}" for r in range(ROUNDS)]
        n_x = ledger(**{"S": 0}, **{p: 2 for p in Ms})
        n_m = ledger(**{p: 1 for p in Ms}, **{p: 1 for p in Ds[1:]})
        n_k = ledger(**{p: 1 for p in Ms})
        n_i = ledger(S=1, M0=1, D0=1, D3=1)
        n_j = ledger(S=1, **{p: 1 for p in Ms[1:]})
        n_p = ledger(**{p: 2 for p in Ds})
        n_b = ledger(W=4, D2=1)
        n_c = ledger(S=1, M3=1)
        n_gx = ledger(S=TG, D0=TG)
        n_gj = ledger(M0=TG)
        n_gm = ledger(**{p: TG for p in Ms[1:]})
        n_sto = ledger(S=4, **{p: 2 for p in Ms}, D0=1, D1=1, D2=1)
        n_stj = ledger(M0=1)
        n_stp = ledger(**{p: 1 for p in Ms})
        n_ln = ledger(S=LANES, **{p: LANES for p in Ms[:3]}, M3=2 * LANES, D0=LANES)
        n_w = ledger(S=3)
        n_stw = ledger(S=2)
        n_masks = ledger(S=LANES)
        n_pf = ledger(**{p: LANES for p in Ds})
        n_cv = ledger(M3=LANES)
        n_scat = ledger(S=TG, D3=TG)

        n_d = ledger(**{p: len(SHARED) for p in free})
        n_cp = ledger(S=LANES, **{p: LANES for p in Ms})

        def wait_earlier(eng, s, w, l):
            if not (isinstance(w, int) and w == l == 0):
                eng.wait_ge(s, w * LANES + l)

        def ti_at(ph, name, wave, part=0, more=0):
            return ti_use[ph](name, wave, part) + (tin.start[ph] + more)

        def to_at(ph, name, wave, part=0, more=0):
            return to_use[ph](name, wave, part) + (tout.start[ph] + more)

        def norm_at(ph, name, wave, part=0, more=0):
            return norm_use[ph](name, wave, part) + (n_ln.start[ph] + more)

        def no_wave(wave):
            return isinstance(wave, int) and wave < 0

        block = ctx.enter_context(nc.Block())

        def settle(eng):
            eng.sem_inc(s_settle, 1)

        def flat(rows):
            return rows[:, :, :].rearrange("p j c -> p (j c)")

        @block.sync
        def _(sp):
            def rows_in(buf, view, g, s):
                sp.dma_start(buf[0:SPLIT], view[g, 0:SPLIT]).then_inc(s, 16)
                sp.dma_start(buf[SPLIT:TP], view[g, SPLIT:TP]).then_inc(s, 16)

            with nc.allow_non_contiguous_dma(reason="short rows"):
                sp.dma_start(seq_i[0][:, :], dst.rearrange("(p q) -> p q", p=TP)).then_inc(s_seq, 16)
                sp.wait_ge(s_cst, 1)
                sp.dma_start(seq_i[1][0:TP - 1, :], dst[1:E - ET + 1].rearrange("(p q) -> p q", p=TP - 1)).then_inc(s_seq, 16)
                sp.dma_start(seq_i[1][TP - 1:TP, 0:ET - 1], dst[E - ET + 1:E].rearrange("(p q) -> p q", p=1)).then_inc(s_seq, 16)
            sp.dma_start(dst_pad[0:1].rearrange("(a b) -> a b", a=1), minus1[0:1, 0:1]).then_inc(s_copied, 16)
            sp.dma_start(dst_s, dst).then_inc(s_copied, 16)
            sp.dma_start(src_s, src).then_inc(s_copied, 16)
            sp.dma_start(weight_s, edge_weight).then_inc(s_copied, 16)
            sp.dma_start(attr_s, edge_attr).then_inc(s_copied, 16)
            sp.dma_start(slot_of_node.rearrange("(p q) o -> p (q o)", p=TP), none_t[:, :]).then_inc(s_copied, 16)

            sp.wait_ge(v_late, 1)
            with nc.allow_non_contiguous_dma(reason="a column"):
                sp.dma_start(late_col.rearrange("(p o) -> p o", o=1), late_p[:, :]).then_inc(s_late, 16)
            sp.wait_ge(s_late, 16)
            sp.dma_start(late_row[:, :], late_col.rearrange("(o p) -> o p", o=1)).then_inc(s_late, 16)

            sp.wait_ge(s_order, 1)
            with nc.allow_non_contiguous_dma(reason="index columns"):
                for k, a in enumerate((src_s, dst_s, dst_pad[0:E])):
                    sp.dma_start(ic[k][:, :], a.rearrange("(t p) -> p t", p=TP)).then_inc(s_idx, 16)
            sp.dma_start(drow_i[:, :], dst_s.rearrange("(t p) -> t p", p=TP)).then_inc(s_idx, 16)
            for q in range(NCH):
                sp.dma_start(wbc[q * NB:(q + 1) * NB, :],
                             weight_s[q * CH:(q + 1) * CH].partition_broadcast(NB)).then_inc(s_idx, 16)
            sp.dma_start(attr_t[:, :], attr_s.rearrange("(p q) c -> p (q c)", p=TP)).then_inc(s_idx, 16)

            for k, w in enumerate((W_ih, W_hh)):
                sp.dma_start(w_raw[:, 3 * k:3 * k + 3, :], w.rearrange("(g o) i -> o g i", g=3)).then_inc(s_set, 16)
            sp.dma_start(w_lin[:, :], W_lin).then_inc(s_set, 16)
            sp.dma_start(mw0[:, 0:HID], mlp_w0).then_inc(s_set, 16)
            sp.dma_start(mw2[0:HID, :], mlp_w2).then_inc(s_set, 16)
            with nc.allow_non_contiguous_dma(reason="short columns"):
                for k, b in enumerate((b_ih, b_hh)):
                    sp.dma_start(bias[:, 3 * k:3 * k + 3], b.rearrange("(g p) -> p g", g=3)).then_inc(s_set, 16)
                for k, b in enumerate((mlp_b0, mlp_b1)):
                    sp.dma_start(mb[0:HID, k:k + 1], b.rearrange("(p o) -> p o", o=1)).then_inc(s_set, 16)
                sp.wait_ge(s_cst, 1)
                for k, blocks in enumerate(((0, 2, 2, 2), (1, 1, 1), (3, 3, 3))):
                    for q, b in enumerate(blocks):
                        sp.dma_start(mb2[q * MUL:(q + 1) * MUL, k:k + 1],
                                     mlp_b2[b * MUL:(b + 1) * MUL].rearrange("(p o) -> p o", o=1)).then_inc(s_set, 16)
                sp.dma_start(mw1[0:HID, 0:HID], mlp_w1).then_inc(s_set, 16)
                sp.dma_start(up[0:MUL, 0:MUL], W_up0).then_inc(s_set, 16)
                for c in range(3):
                    sp.dma_start(upss[0:MUL, c * MUL:(c + 1) * MUL], W_up0).then_inc(s_set, 16)
                    sp.dma_start(up[MUL + c:MUL + c + 3 * (MUL - 1) + 1:3, MUL + c * MUL:MUL + (c + 1) * MUL],
                                 W_up1).then_inc(s_set, 16)
                sp.dma_start(wo[0:MUL, 0, 0:MUL], W_out0[0:MUL, :]).then_inc(s_set, 16)
                for c in range(3):
                    cols = slice(MUL + c, MUL + c + 3 * (MUL - 1) + 1, 3)
                    sp.dma_start(wo[MUL + c * MUL:2 * MUL + c * MUL, 0, cols], W_out1[MUL:2 * MUL, :]).then_inc(s_set, 16)
                    sp.dma_start(wo[c * MUL:(c + 1) * MUL, 1, cols], W_out1[0:MUL, :]).then_inc(s_set, 16)
                    sp.dma_start(wo[c * MUL:(c + 1) * MUL, 2, 0:MUL], W_out0[MUL:2 * MUL, :]).then_inc(s_set, 16)

            sp.wait_ge(s_prep, 1)
            tabs = [(idx_src, ic[0]), (idx_dst, ic[1]), (idx_first, ifirst), (edge_id, eid), (dst_col, dcf)]
            with nc.allow_non_contiguous_dma(reason="index columns"):
                for d, s_ in tabs:
                    sp.dma_start(d.rearrange("g p j -> p g j"), s_[:, :].rearrange("p (g j) -> p g j", j=TG)).then_inc(s_tab, 16)
            sp.dma_start(dst_rows.rearrange("g (j p) -> (g j) p", p=TP), drow[:, :]).then_inc(s_tab, 16)
            sp.dma_start(mask_keys.rearrange("g (j e) -> (g j) e", e=TE), ext[:, :]).then_inc(s_tab, 16)
            sp.wait_ge(s_exp, 1)
            for q in range(NCH):
                sp.dma_start(emb_d[:, q * CH:(q + 1) * CH], emb_t[q * NB:(q + 1) * NB, :]).then_inc(s_tab, 16)
            sp.wait_ge(s_prep, 2)
            for c in range(3):
                sp.dma_start(rhat_d[c].rearrange("(p q) -> p q", p=TP), rh[:, c, :]).then_inc(s_tab, 16)
            sp.wait_ge(s_tab, 16 * N_TAB)

            def load_e(w, l):
                g = sp.snap((w * LANES + l) * G) if not isinstance(w, int) else (w * LANES + l) * G
                if not no_wave(w - 1):
                    sp.wait_ge(vC, (w - 1) * LANES + (l + 1))
                    settle(sp)
                sp.dma_start(emb_in[l], emb_d[:, bass.ds(g, G)]).then_inc(ld_e[l], 16)
                for c in range(3):
                    sp.dma_start(rhat_in[l][c * MUL:(c + 1) * MUL, :],
                                 rhat_d[c, bass.ds(g, G)].partition_broadcast(MUL)).then_inc(ld_e[l], 16)

            def store_c(w, l):
                sp.wait_ge(vC, w * LANES + (l + 1))
                settle(sp)
                sp.wait_ge(aC, w * LANES + (l + 1))
                settle(sp)
                sp.dma_start(conv_d[w * LANES + l], factors[l % 2][:, :]).then_inc(st_c[l % 2], 16)

            for l in range(LANES):
                sp.dma_start(ix[l][:, :], idx_src[l]).then_inc(ld_i[l], 16)
            plans["W"].run(sp, {"load_e": load_e, "store_c": store_c})
            sp.wait_ge(st_c[0], 16 * 3 * TURNS)
            sp.wait_ge(st_c[1], 16 * 2 * TURNS)

            def load_i(w, l):
                if not no_wave(w - 1):
                    sp.wait_ge(gx[l], 16 * n_gx.at("S", w))
                    settle(sp)
                sp.dma_start(ix[l][:, :], idx_src[w * LANES + l]).then_inc(ld_i[l], 16)

            def load_w(w, l):
                g = sp.snap(w * LANES + l) if not isinstance(w, int) else w * LANES + l
                if not no_wave(w - 1):
                    sp.wait_ge(st_w[l], 16 * n_stw.at("S", w))
                    settle(sp)
                    sp.wait_ge(sc[l], 16 * n_scat.at("S", w))
                    settle(sp)
                sp.dma_start(pt[l][0:TP, :], mask_keys[g].partition_broadcast(TP)).then_inc(ld_w[l], 16)
                sp.dma_start(pf[l][0:ET, :], dst_rows[g].partition_broadcast(ET)).then_inc(ld_w[l], 16)
                sp.dma_start(dc[l][:, :], dst_col[g]).then_inc(ld_w[l], 16)
                sp.dma_start(fx[l][:, :], idx_first[g]).then_inc(ld_f[l], 16)
                sp.dma_start(jx[l][:, :], edge_id[g]).then_inc(ld_j[l], 16)

            def store_w(w, l):
                g = sp.snap(w * LANES + l) if not isinstance(w, int) else w * LANES + l
                sp.wait_ge(v_m, n_masks.at("S", w, l + 1))
                settle(sp)
                sp.dma_start(tile_masks[g], mk[l][:, :]).then_inc(st_w[l], 16)
                sp.dma_start(key_masks[g], rm[l][:, :]).then_inc(st_w[l], 16)

            def store_rows0(w, l):
                sp.wait_ge(s_h0, w * LANES + (l + 1))
                sp.dma_start(by_tile(src_rows[0])[w * LANES + l], on[l][:, :, :]).then_inc(st_o[l], 16)

            def store_step(w, c):
                s, l = divmod(c, LANES)
                sp.wait_ge(s_tof, to_at("S", "back", w, c, 1))
                sp.dma_start(by_tile(src_rows[s + 1])[w * LANES + l], on[l][:, :, :]).then_inc(st_o[l], 16)

            plans["S"].run(sp, {"load_i": load_i, "load_w": load_w, "store_w": store_w, "rows0": store_rows0,
                                "back": store_step})
            for l in range(LANES):
                sp.wait_ge(st_w[l], 16 * n_stw.total)
                sp.wait_ge(sc[l], 16 * n_scat.at("S", TURNS))
                sp.wait_ge(st_o[l], 16 * n_sto.start["M0"])
                rows_in(xa[l], x_dense, l, ld_x[l])

            for r in range(ROUNDS):
                M, D = f"M{r}", f"D{r}"

                def load_x(w, l):
                    sp.wait_ge(s_ln, norm_at(M, "norm", w - 1, l, 1))
                    settle(sp)
                    sp.wait_ge(s_cp, n_cp.at(M, w - 1, l + 1))
                    settle(sp)
                    rows_in(xa[l], x_dense, w * LANES + (r * TURNS * LANES + l), ld_x[l])

                def load_m(w, l):
                    g = sp.snap(w * LANES + l) if not isinstance(w, int) else w * LANES + l
                    if not no_wave(w - 1):
                        sp.wait_ge(st_p[l], 16 * n_stp.at(M, w))
                        settle(sp)
                        if r == STEPS:
                            sp.wait_ge(s_pr, n_cv.at(M, w))
                        settle(sp)
                    sp.dma_start(mm[l][:, :, :], by_tile(src_rows[r])[g]).then_inc(ld_m[l], 16)
                    sp.dma_start(mk[l][:, :], tile_masks[g]).then_inc(ld_k[l], 16)
                    if r:
                        sp.dma_start(jx[l][:, :], idx_slot[g]).then_inc(ld_j[l], 16)
                    if r == STEPS:
                        sp.dma_start(cc[l][:, :], conv_d[g]).then_inc(ld_c[l], 16)

                def load_i(w, l):
                    sp.wait_ge(gx[l], 16 * n_gx.at("S", TURNS))
                    if not no_wave(w - 1):
                        sp.wait_ge(gj[l], 16 * n_gj.at(M, w))
                        settle(sp)
                    sp.dma_start(ix[l][:, :], idx_src[w * LANES + l]).then_inc(ld_i[l], 16)

                def store_j(w, l):
                    sp.wait_ge(gj[l], 16 * n_gj.at(M, w, TG))
                    sp.dma_start(idx_slot[w * LANES + l], jx[l][:, :]).then_inc(st_j[l], 16)

                def store_out(w, l):
                    g = w * LANES + (r * TURNS * LANES + l)
                    if not isinstance(w, int):
                        g = sp.snap(g)
                    sp.wait_ge(s_tof, to_at(M, "back", w, l, 1))
                    settle(sp)
                    sp.dma_start(out_dense[g, 0:SPLIT], on[l][0:SPLIT]).then_inc(st_o[l], 16)
                    sp.dma_start(out_dense[g, SPLIT:TP], on[l][SPLIT:TP]).then_inc(st_o[l], 16)

                def store_sum(w, l):
                    sp.wait_ge(s_tif, ti_at(M, "conv_sum", w, l, 1) if r == STEPS else ti_at(M, "sum", w, l, 1))
                    sp.dma_start(sums_d[w * LANES + l], pt[l][:, :]).then_inc(st_p[l], 16)

                plans[M].run(sp, {"load_x": load_x, "load_m": load_m, "back": store_out, "store_sum": store_sum,
                                  "load_i": load_i, "store_j": store_j})
                if r == 0:
                    for l in range(LANES):
                        sp.wait_ge(st_j[l], 16 * n_stj.total)
                for l in range(LANES):
                    sp.wait_ge(st_p[l], 16 * n_stp.at(M, TURNS))
                    if r == STEPS:
                        sp.wait_ge(st_o[l], 16 * n_sto.at(M, TURNS))

                def load_d(w, l):
                    if not no_wave(w - 1):
                        sp.wait_ge(s_tif, ti_at(D, "first", w - 1, l, 1))
                        settle(sp)
                        if r == 0:
                            sp.wait_ge(gx[l], 16 * n_gx.at(D, w))
                            settle(sp)
                            sp.wait_ge(s_tif, ti_at(D, "spread", w - 1, l, 1))
                            settle(sp)
                    g = w * LANES + l
                    sp.dma_start(pt[l][:, :], sums_d[g]).then_inc(ld_p[l], 16)
                    sp.dma_start(rm[l][:, :], key_masks[g]).then_inc(ld_p[l], 16)
                    if r == 0:
                        sp.dma_start(ix[l][:, :], idx_dst[g]).then_inc(ld_i[l], 16)
                    else:
                        sp.dma_start(mm[l][:, :, :], by_tile(slot_rows[r])[g]).then_inc(ld_m[l], 16)

                def load_dst_x(w, l):
                    if not no_wave(w - 1):
                        sp.wait_ge(s_tof, to_at(D, "back", w - 1, l, 1))
                        settle(sp)
                    sp.dma_start(xn[l][:, :, :], by_tile(dst_x)[w * LANES + l]).then_inc(ld_b[l], 16)

                def store_dst_x(w, l):
                    sp.wait_ge(gx[l], 16 * n_gx.at(D, w, TG))
                    sp.dma_start(by_tile(dst_x)[w * LANES + l], mm[l][:, :, :]).then_inc(st_x[l], 16)

                def store_slot(w, l):
                    sp.wait_ge(s_tof, to_at(D, "back", w, l, 1))
                    sp.dma_start(by_tile(slot_rows[r + 1])[w * LANES + l], on[l][:, :, :]).then_inc(st_o[l], 16)

                if r < STEPS:
                    plans[D].run(sp, {"load": load_d, "load_x": load_dst_x, "store_x": store_dst_x, "back": store_slot})
                else:
                    def load_last(w, l):
                        if not no_wave(w - 1):
                            sp.wait_ge(sc[l], 16 * n_scat.at(D, w))
                            settle(sp)
                        g = w * LANES + l
                        sp.dma_start(pt[l][:, :], sums_d[g]).then_inc(ld_p[l], 16)
                        sp.dma_start(rm[l][:, :], key_masks[g]).then_inc(ld_p[l], 16)
                        sp.dma_start(mm[l][:, :, :], by_tile(slot_rows[r])[g]).then_inc(ld_m[l], 16)
                        sp.dma_start(ix[l][:, :], idx_first[g]).then_inc(ld_i[l], 16)

                    plans[D].run(sp, {"load": load_last})
                if r < STEPS:
                    for l in range(LANES):
                        sp.wait_ge(st_o[l], 16 * n_sto.at(D, TURNS))
                        if r == 0:
                            sp.wait_ge(st_x[l], 16 * TURNS)
            for l in range(LANES):
                sp.wait_ge(sc[l], 16 * n_scat.total)

        @block.gpsimd
        def _(pool):
            steps = [0]

            def link(ins):
                steps[0] += 1
                ins.then_inc(pchain, 1)
                pool.wait_ge(pchain, steps[0])

            pool.memset(seq_i[1][:, :], NONE)
            pool.memset(up[:, :], 0.0)
            for t in (mw0, mw1, mw2, mb):
                pool.memset(t[:, :], 0.0)
            pool.memset(upss[:, :], 0.0)
            pool.memset(wo[:, :, :], 0.0)
            pool.memset(mb2[:, :], 0.0)
            pool.memset(minus1[:, :], -1)
            pool.memset(minus_half[:, :], -0.5)
            pool.memset(half[:, :], 0.5)
            pool.memset(none_t[:, :], NONE).then_inc(s_cst, 1)
            pool.iota(eid[:, :], pattern=[[TP, ET]], base=0, channel_multiplier=1).then_inc(s_id, 1)
            pool.iota(cen_i[:, :], pattern=[[1, 1]], base=0, channel_multiplier=1).then_inc(s_id, 1)
            link(pool.memset(ident[:, :], 0.0))
            pool.affine_select(out=ident[:, :], in_=ident[:, :], compare_op=ALU.not_equal, fill=1.0,
                               base=0, pattern=[[-1, C]], channel_multiplier=1).then_inc(s_id, 1)
            last_node, last_slot = N - 1, E - 1

            def sort_edges():
                steps[0] = 0
                pool.sem_clear(pchain)
                link(pool.tensor_copy(dst_f[:, :], seq_i[0][:, :]))
                link(pool.tensor_tensor(dst_f[:, :], dst_f[:, :], dst_f[:, :], ALU.add))
                link(pool.iota(seq_i[1][:, :], pattern=[[1, ET]], base=0, channel_multiplier=ET))
                link(pool.tensor_copy(edge_f[:, :], seq_i[1][:, :]))
                link(pool.iota(other_i[:, :], pattern=[[1, RCH]], base=0, channel_multiplier=0))
                link(pool.tensor_copy(other[:, :], other_i[:, :]))
                link(pool.memset(counted, 0.0))
                whole = [TP, ET, RCH]
                by_edge = [t[:, :].unsqueeze(2).broadcast_to(whole) for t in (edge_f, dst_f)]
                by_other = [t[:, :].unsqueeze(1).broadcast_to(whole) for t in (other, other_d)]
                with pool.Fori(0, E // RCH) as q:
                    steps[0] = 0
                    pool.sem_clear(pchain)
                    pool.dma_start(other_i[:, :], dst[bass.ds(q * RCH, RCH)].partition_broadcast(TP)).then_inc(s_other, 16)
                    pool.wait_ge(s_other, 16 * (q + 1))
                    settle(pool)
                    link(pool.tensor_copy(other_d[:, :], other_i[:, :]))
                    link(pool.tensor_tensor(other_d[:, :], other_d[:, :], other_d[:, :], ALU.add))
                    link(pool.tensor_tensor(compared, by_edge[0], by_other[0], ALU.subtract))
                    link(pool.tensor_scalar(compared, compared, 0.0, 1.0, ALU.max, ALU.min))
                    link(pool.tensor_tensor(compared, by_other[1], compared, ALU.subtract))
                    link(pool.tensor_tensor(compared, by_edge[1], compared, ALU.subtract))
                    link(pool.tensor_scalar(compared, compared, 0.0, 1.0, ALU.max, ALU.min))
                    link(pool.tensor_tensor(counted, counted, compared, ALU.add))
                    link(pool.tensor_scalar(other[:, :], other[:, :], float(RCH), None, ALU.add))
                w = RCH
                while w > 1:
                    half_w = w // 2
                    link(pool.tensor_tensor(counted[:, :, 0:half_w], counted[:, :, 0:half_w],
                                            counted[:, :, w - half_w:w], ALU.add))
                    w -= half_w
                for k in range(2):
                    link(pool.tensor_scalar(seq[:, :], counted[:, :, 0], float(k), None, ALU.add))
                    link(pool.tensor_copy(rank_i[:, :], seq[:, :]))
                    pool.dma_start(ranks[k], rank_i[:, :]).then_inc(s_ranks, 16)
                    pool.wait_ge(s_ranks, 16 * (k + 1))
                with pool.Fori(0, EG) as g:
                    def part_of(a):
                        return a.rearrange("(p g j) -> g p j", p=TP, j=TG)[g]

                    for k in range(2):
                        pool.dma_start(move_rank[:, k, :], ranks[k].rearrange("p (g j) -> g p j", j=TG)[g]).then_inc(s_move, 16)
                    with nc.allow_non_contiguous_dma(reason="index columns"):
                        pool.dma_start(move_src[:, :], part_of(src)).then_inc(s_move, 16)
                        pool.dma_start(move_dst[:, :], part_of(dst)).then_inc(s_move, 16)
                        pool.dma_start(move_w[:, :], part_of(edge_weight)).then_inc(s_move, 16)
                        pool.dma_start(move_attr[:, :, :], edge_attr.rearrange("(p g j) c -> g p j c", p=TP, j=TG)[g]).then_inc(s_move, 16)
                    pool.wait_ge(s_move, 16 * 6 * (g + 1))
                    settle(pool)
                    for j in range(TG):
                        places = [move_rank[:, k, j:j + 1] for k in range(2)]
                        for sorted_, edges, k in ((src_s, move_src, 0), (dst_pad, move_dst, 1), (weight_s, move_w, 0)):
                            scatter(sorted_.rearrange("(e o) -> e o", o=1), edges[:, j:j + 1], places[k], s_moved,
                                    last_slot + k)
                        scatter(attr_s, move_attr[:, j, :], places[0], s_moved, last_slot)
                    pool.wait_ge(s_moved, 16 * 4 * TG * (g + 1))
                    settle(pool)

            def gather(rows, table, index, s, bound):
                pool.indirect_dma_start(
                    out=rows, out_offset=None, in_=table,
                    in_offset=bass.IndirectOffsetOnAxis(ap=index, axis=0),
                    bounds_check=bound, oob_is_err=False).then_inc(s, 16)

            def scatter(table, rows, index, s, bound):
                pool.indirect_dma_start(
                    out=table, out_offset=bass.IndirectOffsetOnAxis(ap=index, axis=0),
                    in_=rows, in_offset=None, bounds_check=bound, oob_is_err=False).then_inc(s, 16)

            pool.wait_ge(v_late, 2)
            pool.wait_ge(s_copied, 16 * 6)
            unsorted = pool.value_load(late_i[0:1, 0:1], min_val=0, max_val=1)
            with pool.If(unsorted != 0):
                sort_edges()
            pool.sem_inc(s_order, 1)

            pool.wait_ge(v_sq, 1)
            pool.tensor_tensor(nrm[:, :], nrm[:, :], half[:, :], ALU.pow).then_inc(p_nrm, 1)

            def rstds(l, count):
                pool.wait_ge(v_var, count)
                pool.tensor_tensor(rstd[l][:, :], veps[l][:, :], minus_half[:, :], ALU.pow).then_inc(p_rs, 1)

            def difference(ph):
                def step(w, k):
                    l = k % LANES
                    if k not in SHARED:
                        return
                    pool.wait_ge(a_n, cell.at(ph, w, k + 1))
                    h = first_h[ph][l] if k < LANES else hT[l]
                    pool.tensor_tensor(tT[l][:, :], h[:, :], nT[l][:, :], ALU.subtract).then_inc(p_d, 1)
                return step

            def gather_source(w, p):
                l, j = divmod(p, TG)
                if j == 0:
                    pool.wait_ge(ld_i[l], 16 * n_i.at("S", w, 1))
                    settle(pool)
                    if not no_wave(w - 1):
                        pool.wait_ge(s_cp, n_cp.at("S", w - 1, l + 1))
                        settle(pool)
                gather(mm[l][:, j, :], x, ix[l][:, j:j + 1], gx[l], last_node)

            def scatter_first(w, p):
                l, j = divmod(p, TG)
                if j == 0:
                    pool.wait_ge(ld_f[l], 16 * n_c.at("S", w, 1))
                    pool.wait_ge(ld_j[l], 16 * n_j.at("S", w, 1))
                    settle(pool)
                scatter(slot_of_node, jx[l][:, j:j + 1], fx[l][:, j:j + 1], sc[l], last_node)

            plans["S"].run(pool, {"tanh": difference("S"),
                                  "gather_x": gather_source, "scatter_j": scatter_first,
                                  "variance": lambda w, l: rstds(l, norm_at("S", "norm", w, l, 1))})

            for r in range(ROUNDS):
                M, D = f"M{r}", f"D{r}"

                def gather_slots(w, p):
                    l, j = divmod(p, TG)
                    if j == 0:
                        pool.wait_ge(ld_i[l], 16 * n_i.at(M, w, 1))
                        settle(pool)
                        if not no_wave(w - 1):
                            pool.wait_ge(st_j[l], 16 * n_stj.at(M, w))
                            settle(pool)
                    gather(jx[l][:, j:j + 1], slot_of_node, ix[l][:, j:j + 1], gj[l], last_node)

                def gather_m(w, p):
                    l, j = divmod(p, TG)
                    if r and j == 0:
                        pool.wait_ge(ld_m[l], 16 * n_m.at(M, w, 1))
                        pool.wait_ge(ld_j[l], 16 * n_j.at(M, w, 1))
                        settle(pool)
                    if r:
                        gather(mm[l][:, j, :], slot_rows[r], jx[l][:, j:j + 1], gm[l], last_slot)

                def conv_rstds(w, l):
                    rstds(l, norm_at(M, "conv_norm", w, l, 1))

                plans[M].run(pool, {"tanh": difference(M),
                                    "gather_m": gather_m, "conv_variance": conv_rstds, "gather_j": gather_slots,
                                    "variance": lambda w, l: rstds(l, norm_at(M, "norm", w, l, 1))})

                def gather_dst(w, l):
                    pool.wait_ge(ld_i[l], 16 * n_i.at(D, w, 1))
                    settle(pool)
                    if not no_wave(w - 1):
                        pool.wait_ge(st_x[l], 16 * w)
                        settle(pool)
                        pool.wait_ge(s_ln, norm_at(D, "norm", w - 1, l, 1))
                        settle(pool)
                    for j in range(TG):
                        gather(mm[l][:, j, :], x, ix[l][:, j:j + 1], gx[l], last_node)

                if r == 0:
                    plans[D].run(pool, {"gather_x": gather_dst,
                                        "variance": lambda w, l: rstds(l, norm_at(D, "norm", w, l, 1))})
                def scatter_out(w, l):
                    pool.wait_ge(ld_i[l], 16 * n_i.at(D, w, 1))
                    pool.wait_ge(s_tof, to_at(D, "back", w, l, 1))
                    settle(pool)
                    for j in range(TG):
                        scatter(out, on[l][:, j, :], ix[l][:, j:j + 1], sc[l], last_node)

                if r == STEPS:
                    plans[D].run(pool, {"scatter": scatter_out})

        @block.scalar
        def _(act):
            act.sem_inc(a_r, 1)
            act.sem_inc(a_n, 1)
            act.sem_inc(a_z, 1)
            act.wait_ge(s_vs, 1)
            nc.scalar.activation(emb_t, etmp, ACT.Exp, scale=-0.5 * (NB - 1) ** 2).then_inc(s_exp_a, 1)

            def mlp1_sigmoid(w, l):
                act.wait_ge(pA, w * LANES + (l + 1))
                wait_earlier(act, vA, w, l)
                nc.scalar.activation(sig1, gate[0][0][:, 0:G], ACT.Sigmoid, bias=mb[:, 0:1]).then_inc(aA, 1)

            def mlp2_sigmoid(w, l):
                act.wait_ge(pB, w * LANES + (l + 1))
                wait_earlier(act, vB, w, l)
                nc.scalar.activation(sig2, gate[0][1][:, 0:G], ACT.Sigmoid, bias=mb[:, 1:2]).then_inc(aB, 1)

            def factor0(w, l):
                act.wait_ge(pC, w * LANES + (l + 1))
                if not (isinstance(w, int) and w == 0 and l < 2):
                    act.wait_ge(st_c[l % 2], 16 * (w * (3 - l % 2) + l // 2))
                nc.scalar.activation(factors[l % 2][:, 0:G], gate[0][2][:, 0:G], ACT.Identity,
                                     bias=mb2[:, 0:1]).then_inc(aC, 1)

            plans["W"].run(act, {"mlp1": mlp1_sigmoid, "mlp2": mlp2_sigmoid, "fac": factor0})

            def first_state(ph, func):
                def step(w, l):
                    act.wait_ge(s_ti, ti_at(ph, "first", w, l))
                    nc.scalar.activation(first_h[ph][l][:, :], ti[:, 0:G], func).then_inc(s_tif, 1)
                return step

            def keep_source(w, l):
                act.wait_ge(s_ln, norm_at("S", "norm", w, l, 1))
                if not no_wave(w - 1):
                    act.wait_ge(s_tof, to_at("S", "back", w - 1, CELLS - LANES + l, 1))
                nc.scalar.activation(flat(xa[l])[:, :], flat(mm[l])[:, :], ACT.Copy).then_inc(s_cp, 1)

            def cell_r(ph):
                def step(w, k):
                    act.wait_ge(g_r, cell.at(ph, w, k + 1) - 1)
                    nc.scalar.activation(rT[k % LANES][:, :], gate[k % 2][0][:, 0:G], ACT.Sigmoid,
                                         bias=bias[:, 6:7]).then_inc(a_r, 1)
                return step

            def cell_z(ph):
                def step(w, k):
                    act.wait_ge(g_z, cell.at(ph, w, k + 1) - 1)
                    nc.scalar.activation(zT[k % LANES][:, :], gate[k % 2][2][:, 0:G], ACT.Sigmoid,
                                         bias=bias[:, 7:8]).then_inc(a_z, 1)
                return step

            def cell_n(ph):
                def step(w, k):
                    if ph in slot:
                        act.wait_ge(s_tif, ti_at(ph, "cell", w, k, 1))
                    else:
                        act.wait_ge(v_t, cell.at(ph, w, k + 1))
                    nc.scalar.activation(nT[k % LANES][:, :], tT[k % LANES][:, :], ACT.Tanh,
                                         bias=bias[:, 2:3]).then_inc(a_n, 1)
                return step

            def cell_steps_of(ph):
                return {"cell": cell_r(ph), "tanh": cell_n(ph), "z": cell_z(ph)}

            def rows_copy(ph, w, c, l, stored):
                act.wait_ge(s_to, to_at(ph, "back", w, c))
                act.wait_ge(st_o[l], 16 * stored)
                nc.scalar.activation(flat(on[l])[:, :], to[0:TP, :], ACT.Copy).then_inc(s_tof, 1)

            def sums_copy(w, l, use):
                act.wait_ge(s_ti, use)
                nc.scalar.activation(pt[l][:, :], ti[:, 0:TG * TE], ACT.Copy)
                nc.scalar.activation(part[:, bass.ds((w * LANES + l) * 2 * TG, 2 * TG)].rearrange("p (j b) -> p j b", b=2),
                                     ti[:, 0:TG * TE].rearrange("p (j e) -> p j e", e=TE)[:, :, TP:TE],
                                     ACT.Copy).then_inc(s_tif, 1)

            def step_rows(w, c):
                if c < CELLS - LANES:
                    rows_copy("S", w, c, c % LANES, n_sto.at("S", w, c // LANES + 1))

            act.wait_ge(st_c[0], 16 * 3 * TURNS)
            act.wait_ge(st_c[1], 16 * 2 * TURNS)
            plans["S"].run(act, {**cell_steps_of("S"), "first": first_state("S", ACT.Relu), "keep_x": keep_source,
                                 "back": step_rows})

            for r in range(ROUNDS):
                M, D = f"M{r}", f"D{r}"

                def conv_states(w, l):
                    act.wait_ge(s_ti, ti_at(M, "conv_cols", w, l))
                    nc.scalar.activation(pf[l][:, :], ti[:, 0:G], ACT.Relu).then_inc(s_tif, 1)

                def conv_rows(w, l):
                    act.wait_ge(s_cn, n_cv.at(M, w, l + 1))
                    nc.scalar.activation(flat(mm[l])[:, :], gate[1][0][0:TP, :], ACT.Copy).then_inc(s_cf, 1)

                def keep_x(w, l):
                    act.wait_ge(ld_x[l], 16 * (n_x.at(M, w) + 2))
                    act.wait_ge(st_o[l], 16 * n_sto.at(M, w))
                    nc.scalar.activation(flat(on[l])[:, :], flat(xa[l])[:, :], ACT.Copy).then_inc(s_cp, 1)

                plans[M].run(act, {"copy_x": keep_x, **cell_steps_of(M),  "first": first_state(M, ACT.Relu), "conv_cols": conv_states, "conv_rows": conv_rows,
                                   "conv_sum": lambda w, l: sums_copy(w, l, ti_at(M, "conv_sum", w, l)),
                                   "sum": lambda w, l: sums_copy(w, l, ti_at(M, "sum", w, l))})
                act.wait_ge(s_ti, tin.at(D, 0) - 1)
                nc.scalar.activation(bsum[:, 0, :], ti[0:ET, 0:2 * C], ACT.Copy).then_inc(s_bh, 1)
                act.wait_ge(s_tif, tin.at(D, 0))
                nc.scalar.activation(bsum[:, 1, :], brest[:, :], ACT.Copy).then_inc(s_bm, 1)
                if r < STEPS:
                    def slot_rows_copy(w, l):
                        if r < STEPS - 1:
                            rows_copy(D, w, l, l, n_sto.at(D, w))

                    plans[D].run(act, {**cell_steps_of(D), "first": first_state(D, ACT.Copy if r else ACT.Relu),
                                       "back": slot_rows_copy})

        @block.vector
        def _(dve):
            steps = [0]

            def link(ins):
                steps[0] += 1
                ins.then_inc(chain, 1)
                dve.wait_ge(chain, steps[0])

            def new_chain():
                dve.sem_clear(chain)
                steps[0] = 0

            V = nc.vector
            dve.sem_inc(v_t, 1)
            dve.sem_inc(v_h, 1)
            dve.sem_inc(s_tif, 1)
            dve.sem_inc(s_tof, 1)
            dve.wait_ge(s_seq, 48)
            V.tensor_copy(late[:, :], seq_i[0][:, :])
            link(V.tensor_copy(seq[:, :], seq_i[1][:, :]))
            link(V.tensor_tensor(late[:, :], late[:, :], seq[:, :], ALU.is_gt))
            V.tensor_reduce(late_p[:, :], late[:, :], AX.X, ALU.max).then_inc(v_late, 1)
            dve.wait_ge(s_late, 32)
            link(V.tensor_reduce(late_any[:, :], late_row[:, :], AX.X, ALU.max))
            V.tensor_copy(late_i[:, :], late_any[:, :]).then_inc(v_late, 1)
            for l in (0, 4):
                V.memset(cc[l][96:C, G:3 * G], 0.0)
            dve.wait_ge(s_id, 3)
            dve.wait_ge(s_idx, 16 * N_IDX)
            link(V.tensor_tensor(asq[:, :], attr_t[:, :], attr_t[:, :], ALU.mult))
            V.tensor_reduce(nrm[:, :], asq[:, :].rearrange("p (q c) -> p q c", c=3), AX.X, ALU.add).then_inc(v_sq, 1)
            link(V.tensor_scalar(cen_i[:, :], cen_i[:, :], NB - 1, None, ALU.bitwise_and))
            link(V.tensor_copy(cen[:, :], cen_i[:, :]))
            link(V.tensor_scalar(cen[:, :], cen[:, :], 1.0 / (NB - 1), None, ALU.mult))
            link(V.tensor_scalar(etmp, wbc, 0.0, 1.0, ALU.max, ALU.min))
            link(V.tensor_scalar(etmp, etmp, cen[:, 0:1], None, ALU.subtract))
            V.tensor_tensor(etmp, etmp, etmp, ALU.mult).then_inc(s_vs, 1)
            V.tensor_copy(dcf[:, :], ic[1][:, :])
            link(V.tensor_copy(dpf[:, :], ic[2][:, :]))
            V.tensor_tensor(deq[:, :], dcf[:, :], dpf[:, :], ALU.is_equal)
            link(V.tensor_scalar(dfi[:, :], dcf[:, :], -1.0, float(NONE), ALU.mult, ALU.add))
            link(V.tensor_tensor(dfi[:, :], dfi[:, :], deq[:, :], ALU.mult))
            link(V.tensor_tensor(dfi[:, :], dfi[:, :], dcf[:, :], ALU.add))
            V.tensor_copy(ifirst[:, :], dfi[:, :])
            link(V.tensor_copy(drow[:, :], drow_i[:, :]))
            V.tensor_scalar(eqf[:, :], drow[:, :], drow[:, 0:1], None, ALU.is_equal)
            link(V.tensor_scalar(eql[:, :], drow[:, :], drow[:, TP - 1:TP], None, ALU.is_equal))
            link(V.tensor_tensor(eql[:, :], eqf[:, :], eql[:, :], ALU.max))
            link(V.scalar_tensor_tensor(eql[:, :], drow[:, :], 1.0, eql[:, :], ALU.add, ALU.mult))
            V.tensor_tensor(ext[:, 0:TP], drow[:, :], eql[:, :], ALU.subtract)
            V.tensor_copy(ext[:, TP:TP + 1], drow[:, 0:1])
            link(V.scalar_tensor_tensor(ext[:, TP + 1:TE], drow[:, TP - 1:TP], 1.0, eqf[:, TP - 1:TP],
                                        ALU.add, ALU.mult))
            link(V.tensor_tensor(ext[:, TP + 1:TE], drow[:, TP - 1:TP], ext[:, TP + 1:TE], ALU.subtract))
            V.tensor_copy(keys[:, :], ext[:, TP:TE]).then_inc(s_prep, 1)
            link(V.tensor_scalar(etmp2, wbc, 1.0, float(NB) ** 0.5, ALU.is_le, ALU.mult))
            dve.wait_ge(s_exp_a, 1)
            V.tensor_tensor(emb_t, emb_t, etmp2, ALU.mult).then_inc(s_exp, 1)
            dve.wait_ge(p_nrm, 1)
            link(V.tensor_scalar(nrm[:, :], nrm[:, :], 1e-12, None, ALU.add))
            link(V.reciprocal(inv[:, :], nrm[:, :]))
            for c in range(3):
                last = V.tensor_tensor(rh[:, c, :], attr_t[:, :].rearrange("p (q c) -> p c q", c=3)[:, c, :],
                                       inv[:, :], ALU.mult)
            last.then_inc(s_prep, 1)

            dve.wait_ge(s_set, 16 * N_SET)
            V.tensor_tensor(bias[:, 6:9], bias[:, 0:3], bias[:, 3:6], ALU.add)
            for k, blocks in enumerate(((0, 2, 2, 2), (1, 1, 1), (3, 3, 3))):
                for q, b in enumerate(blocks):
                    V.tensor_copy(mw2x[:, k, q * MUL:(q + 1) * MUL], mw2[:, b * MUL:(b + 1) * MUL])
            V.tensor_scalar(up[:, :], up[:, :], float(MUL) ** -0.5, None, ALU.mult)
            V.tensor_scalar(upss[:, :], upss[:, :], float(MUL) ** -0.5, None, ALU.mult)
            for k, f in enumerate((1.0, 3.0 ** 0.5, 1.0)):
                V.tensor_scalar(wo[:, k, :], wo[:, k, :], f / (float(2 * MUL) ** 0.5 * 16.0), None, ALU.mult)
            dve.wait_ge(s_wt, 1)
            V.tensor_copy(flat(w_ihT)[:, :], ti[:, 0:3 * C])
            V.tensor_copy(flat(w_hT)[:, :], to[:, 0:3 * C]).then_inc(s_wc, 1)
            dve.wait_ge(s_wt, 2)
            V.tensor_copy(flat(w_pT)[:, :], gate[0][0][:, 0:3 * C]).then_inc(s_wc, 1)

            def variance(l, rows):
                for j in range(TG):
                    last = V.bn_stats(stats[l][:, j, :], rows[:, j, :])
                link(last)
                for j in range(TG):
                    last = V.bn_aggr(mv[l][:, j, :], stats[l][:, j, :])
                link(last)
                V.tensor_scalar(veps[l][:, :], mv[l][:, :, 1], EPS, None, ALU.add).then_inc(v_var, 1)

            def norm(l, rows, out_rows, count):
                dve.wait_ge(p_rs, count)
                for j in range(TG):
                    last = V.tensor_scalar(out_rows[:, j, :], rows[:, j, :], mv[l][:, j, 0:1], rstd[l][:, j:j + 1],
                                           ALU.subtract, ALU.mult)
                last.then_inc(s_ln, 1)

            def cell_t(ph):
                def step(w, k):
                    l = k % LANES
                    dve.wait_ge(a_r, cell.at(ph, w, k + 1))
                    dve.wait_ge(g_n, cell.at(ph, w, k + 1) - 1)
                    V.scalar_tensor_tensor(tT[l][:, :], gate[k % 2][1][:, 0:G], bias[:, 5:6], rT[l][:, :],
                                           ALU.add, ALU.mult).then_inc(v_t, 1)
                    if ph in slot:
                        dve.wait_ge(v_t, cell.at(ph, w, k + 1))
                        dve.wait_ge(s_ti, ti_at(ph, "cell", w, k))
                        V.tensor_tensor(tT[l][:, :], tT[l][:, :], ti[:, 0:G], ALU.add).then_inc(s_tif, 1)
                return step

            def cell_h(ph):
                def step(w, k):
                    l = k % LANES
                    if ph in slot or k not in SHARED:
                        dve.wait_ge(a_n, cell.at(ph, w, k + 1))
                        h = first_h[ph][l] if k < LANES else hT[l]
                        link(V.tensor_tensor(tT[l][:, :], h[:, :], nT[l][:, :], ALU.subtract))
                    else:
                        dve.wait_ge(p_d, n_d.at(ph, w, SHARED.index(k) + 1))
                    dve.wait_ge(a_z, cell.at(ph, w, k + 1))
                    link(V.tensor_tensor(tT[l][:, :], zT[l][:, :], tT[l][:, :], ALU.mult))
                    V.tensor_tensor(hT[l][:, :], nT[l][:, :], tT[l][:, :], ALU.add).then_inc(v_h, 1)
                return step

            def rows_add(ph, w, c, l, rows):
                dve.wait_ge(s_to, to_at(ph, "back", w, c))
                V.tensor_tensor(flat(on[l])[:, :], to[0:TP, :], flat(rows)[:, :], ALU.add).then_inc(s_tof, 1)

            def source_variance(w, l):
                dve.wait_ge(gx[l], 16 * n_gx.at("S", w, TG))
                variance(l, mm[l])

            def mlp1(w, l):
                dve.wait_ge(aA, w * LANES + (l + 1))
                wait_earlier(dve, pB, w, l)
                V.scalar_tensor_tensor(act1, gate[0][0][:, 0:G], mb[:, 0:1], sig1, ALU.add, ALU.mult).then_inc(vA, 1)

            def mlp2(w, l):
                dve.wait_ge(aB, w * LANES + (l + 1))
                wait_earlier(dve, pC, w, l)
                V.scalar_tensor_tensor(act2, gate[0][1][:, 0:G], mb[:, 1:2], sig2, ALU.add, ALU.mult).then_inc(vB, 1)

            def vector_factors(w, l):
                dve.wait_ge(pC, w * LANES + (l + 1))
                if not (isinstance(w, int) and w == 0 and l < 2):
                    dve.wait_ge(st_c[l % 2], 16 * (w * (3 - l % 2) + l // 2))
                for k in (1, 2):
                    last = V.scalar_tensor_tensor(factors[l % 2][0:96, k * G:(k + 1) * G], gate[1][k - 1][0:96, 0:G],
                                                  mb2[0:96, k:k + 1], rhat_in[l], ALU.add, ALU.mult)
                last.then_inc(vC, 1)

            plans["W"].run(dve, {"mlp1": mlp1, "mlp2": mlp2, "fac": vector_factors})

            def masks(w, l):
                dve.wait_ge(ld_w[l], 16 * n_w.at("S", w, 3))
                for j in range(TG):
                    V.tensor_scalar(mk[l][:, j * TE:(j + 1) * TE], pt[l][0:TP, j * TE:(j + 1) * TE],
                                    dc[l][:, j:j + 1], None, ALU.is_equal)
                for b in range(2):
                    last = V.tensor_scalar(rm[l][:, b * G:(b + 1) * G], pf[l][0:ET, :], keys[:, b:b + 1],
                                           None, ALU.is_equal)
                last.then_inc(v_m, 1)

            def source_rows0(w, l):
                dve.wait_ge(s_ln, norm_at("S", "norm", w, l, 1))
                dve.wait_ge(st_o[l], 16 * n_sto.at("S", w))
                V.tensor_scalar(flat(on[l])[:, :], flat(xn[l])[:, :], 0.0, None, ALU.max).then_inc(s_h0, 1)

            def source_rows3(w, c):
                if c >= CELLS - LANES:
                    l = c % LANES
                    dve.wait_ge(s_cp, n_cp.at("S", w, l + 1))
                    dve.wait_ge(st_o[l], 16 * n_sto.at("S", w, STEPS))
                    rows_add("S", w, c, l, xa[l])

            plans["S"].run(dve, {"cell": cell_t("S"), "late": cell_h("S"), "back": source_rows3, "rows0": source_rows0,
                                 "masks": masks,
                                 "variance": source_variance,
                                 "norm": lambda w, l: norm(l, mm[l], xn[l], norm_at("S", "norm", w, l, 1))}, new_chain)

            for r in range(ROUNDS):
                M, D = f"M{r}", f"D{r}"

                def x_variance(w, l):
                    dve.wait_ge(ld_x[l], 16 * (n_x.at(M, w) + 2))
                    variance(l, xa[l])

                def x_add(w, l):
                    dve.wait_ge(s_cp, n_cp.at(M, w, l + 1))
                    rows_add(M, w, l, l, on[l])

                def conv_variance(w, l):
                    dve.wait_ge(gm[l], 16 * n_gm.at(M, w, TG))
                    variance(l, mm[l])

                def conv_products(w, l):
                    dve.wait_ge(s_up, n_cv.at(M, w, l + 1))
                    dve.wait_ge(ld_c[l], 16 * n_c.at(M, w, 1))
                    V.tensor_tensor(rT[l][:, :], gate[0][0][:, 0:G], cc[l][:, 0:G], ALU.mult)
                    V.tensor_tensor(zT[l][0:96, :], gate[0][1][0:96, 0:G], cc[l][0:96, G:2 * G], ALU.mult)
                    V.tensor_tensor(nT[l][0:96, :], gate[0][2][0:96, 0:G], cc[l][0:96, 2 * G:3 * G],
                                    ALU.mult).then_inc(s_pr, 1)

                plans[M].run(dve, {"cell": cell_t(M), "late": cell_h(M), "back": x_add, "variance": x_variance,
                                   "norm": lambda w, l: norm(l, xa[l], xn[l], norm_at(M, "norm", w, l, 1)),
                                   "conv_variance": conv_variance,
                                   "conv_norm": lambda w, l: norm(l, mm[l], mm[l], norm_at(M, "conv_norm", w, l, 1)),
                                   "conv_up": conv_products}, new_chain)
                dve.wait_ge(s_bh, r + 1)
                V.tensor_tensor(brest[:, :], ti[0:ET, 0:2 * C], bsum[:, 0, :], ALU.subtract).then_inc(s_tif, 1)
                dve.wait_ge(s_bm, r + 1)
                V.tensor_tensor(bsum[:, 2, :], brest[:, :], bsum[:, 1, :], ALU.subtract).then_inc(s_bl, 1)

                def whole_sums(w, l, use):
                    dve.wait_ge(s_ti, use)
                    dve.wait_ge(ld_p[l], 16 * n_p.at(D, w, 2))
                    V.tensor_tensor(pf[l][:, :].rearrange("p (j e) -> p j e", e=TP),
                                    ti[:, 0:G].rearrange("p (j e) -> p j e", e=TP),
                                    pt[l][:, :].rearrange("p (j e) -> p j e", e=TE)[:, :, 0:TP],
                                    ALU.add).then_inc(s_tif, 1)

                def dst_variance(w, l):
                    dve.wait_ge(gx[l], 16 * n_gx.at(D, w, TG))
                    variance(l, mm[l])

                def slot_add(w, l):
                    if r == STEPS - 1:
                        dve.wait_ge(ld_b[l], 16 * n_b.at(D, w, 1))
                        dve.wait_ge(st_o[l], 16 * n_sto.at(D, w))
                        rows_add(D, w, l, l, xn[l])

                if r < STEPS:
                    plans[D].run(dve, {"cell": cell_t(D), "late": cell_h(D), "back": slot_add,
                                       "spread": lambda w, l: whole_sums(w, l, ti_at(D, "spread", w, l)),
                                       "variance": dst_variance,
                                       "norm": lambda w, l: norm(l, mm[l], xn[l], norm_at(D, "norm", w, l, 1))},
                                 new_chain)
                else:
                    def last_add(w, l):
                        dve.wait_ge(sc[l], 16 * n_scat.at(D, w))
                        dve.wait_ge(ld_m[l], 16 * n_m.at(D, w, 1))
                        dve.wait_ge(st_o[l], 16 * n_sto.at(D, w))
                        rows_add(D, w, l, l, mm[l])

                    plans[D].run(dve, {"spread": lambda w, l: whole_sums(w, l, ti_at(D, "spread", w, l)),
                                       "back": last_add})

        @block.tensor
        def _(pe):
            T = nc.tensor
            pe.wait_ge(s_id, 3)
            pe.wait_ge(s_set, 16 * N_SET)
            for k in range(6):
                last = T.transpose((ti, to)[k // 3][:, (k % 3) * C:(k % 3 + 1) * C], w_raw[:, k, :], ident[:, :])
            last.then_inc(s_wt, 1)
            pe.wait_ge(s_wc, 1)
            T.matmul(gate[0][0][:, 0:3 * C], w_lin[:, :], flat(w_ihT)[:, :], start=True, stop=True).then_inc(s_wt, 1)
            pe.wait_ge(s_wc, 2)

            def mlp1(w, l):
                pe.wait_ge(ld_e[l], 16 * n_b.at("W", w, 4))
                wait_earlier(pe, vA, w, l)
                T.matmul(gate[0][0][:, 0:G], mw0[:, :], emb_in[l], start=True, stop=True).then_inc(pA, 1)

            def mlp2(w, l):
                pe.wait_ge(vA, w * LANES + (l + 1))
                wait_earlier(pe, vB, w, l)
                T.matmul(gate[0][1][:, 0:G], mw1[:, :], act1, start=True, stop=True).then_inc(pB, 1)

            def all_factors(w, l):
                pe.wait_ge(vB, w * LANES + (l + 1))
                wait_earlier(pe, aC, w, l)
                wait_earlier(pe, vC, w, l)
                T.matmul(gate[0][2][:, 0:G], mw2x[:, 0, :], act2, start=True, stop=True)
                for k in (1, 2):
                    last = T.matmul(gate[1][k - 1][0:96, 0:G], mw2x[:, k, 0:96], act2, start=True, stop=True)
                last.then_inc(pC, 1)

            plans["W"].run(pe, {"mlp1": mlp1, "mlp2": mlp2, "fac": all_factors})
            pe.wait_ge(vC, TURNS * LANES)
            pe.wait_ge(aC, TURNS * LANES)

            def rows_to_cols(rows, use):
                pe.wait_ge(s_tif, use)
                for j in range(TG):
                    last = T.transpose(ti[:, j * TP:(j + 1) * TP], rows[:, j, :], ident[0:TP, 0:TP])
                last.then_inc(s_ti, 1)

            def cols_to_rows(cols, use):
                pe.wait_ge(s_tof, use)
                for j in range(TG):
                    last = T.transpose(to[0:TP, j * C:(j + 1) * C], cols[:, j * TP:(j + 1) * TP], ident[:, :])
                last.then_inc(s_to, 1)

            def cell_gates(ph):
                def step(w, k):
                    l, st = k % LANES, gate[k % 2]
                    if k < LANES:
                        pe.wait_ge(s_tif, ti_at(ph, "first", w, l, 1))
                    else:
                        pe.wait_ge(v_h, cell.at(ph, w, k - LANES + 1))
                    before = cell.at(ph, w, max(k - 1, 0))
                    h = first_h[ph][l] if k < LANES else hT[l]
                    for b, (g, full, read) in enumerate(((0, g_r, a_r), (2, g_n, v_t), (1, g_z, a_z))):
                        pe.wait_ge(read, before)
                        both = ph in slot and g != 2
                        last = T.matmul(st[b][:, 0:G], w_hT[:, g, :], h[:, :], start=True, stop=not both)
                        if both:
                            last = T.matmul(st[b][:, 0:G], w_pT[:, g, :], pf[l][:, :], start=False, stop=True)
                        last.then_inc(full, 1)
                        if ph in slot and g == 2:
                            pe.wait_ge(s_tif, ti_at(ph, "cell", w, k))
                            T.matmul(ti[:, 0:G], w_pT[:, 2, :], pf[l][:, :], start=True, stop=True).then_inc(s_ti, 1)
                return step

            def sum_tiles(ph, w, l, use):
                pe.wait_ge(ld_k[l], 16 * n_k.at(ph, w, 1))
                pe.wait_ge(s_tif, use)
                for j in range(TG):
                    last = T.matmul(ti[:, j * TE:(j + 1) * TE], mm[l][:, j, :], mk[l][:, j * TE:(j + 1) * TE],
                                    start=True, stop=True)
                last.then_inc(s_ti, 1)

            def normed_to_cols(ph):
                def step(w, l):
                    pe.wait_ge(s_ln, norm_at(ph, "norm", w, l, 1))
                    rows_to_cols(xn[l], ti_at(ph, "first", w, l))
                return step

            def back(ph):
                def step(w, part):
                    c = part if ph == "S" else part + (0 if ph in slot else CELLS - LANES)
                    pe.wait_ge(v_h, cell.at(ph, w, c + 1))
                    cols_to_rows(hT[c % LANES], to_at(ph, "back", w, part))
                return step

            plans["S"].run(pe, {"cell": cell_gates("S"), "first": normed_to_cols("S"), "back": back("S")})

            for r in range(ROUNDS):
                M, D = f"M{r}", f"D{r}"

                def message_sums(w, l):
                    if r:
                        pe.wait_ge(gm[l], 16 * n_gm.at(M, w, TG))
                    else:
                        pe.wait_ge(ld_m[l], 16 * n_m.at(M, w, 1))
                    sum_tiles(M, w, l, ti_at(M, "sum", w, l))

                def conv_cols(w, l):
                    pe.wait_ge(s_ln, norm_at(M, "conv_norm", w, l, 1))
                    rows_to_cols(mm[l], ti_at(M, "conv_cols", w, l))

                def conv_up(w, l):
                    pe.wait_ge(s_tif, ti_at(M, "conv_cols", w, l, 1))
                    if l:
                        pe.wait_ge(s_pr, n_cv.at(M, w, l))
                    else:
                        for read in (a_r, v_t, a_z):
                            pe.wait_ge(read, cell.at(M, w, CELLS))
                    T.matmul(gate[0][0][:, 0:G], up[:, :], pf[l][:, :], start=True, stop=True)
                    T.matmul(gate[0][1][0:96, 0:G], upss[:, :], pf[l][:, :], start=True, stop=True)
                    T.matmul(gate[0][2][0:96, 0:G], up[:, MUL:C], pf[l][:, :], start=True, stop=True).then_inc(s_up, 1)

                def conv_rows(w, l):
                    pe.wait_ge(s_pr, n_cv.at(M, w, l + 1))
                    if l:
                        pe.wait_ge(s_cf, n_cv.at(M, w, l))
                    for j in range(TG):
                        cols = slice(j * TP, (j + 1) * TP)
                        o = gate[1][0][0:TP, j * C:(j + 1) * C]
                        T.matmul(o, rT[l][:, cols], wo[:, 0, :], start=True, stop=False)
                        T.matmul(o, zT[l][0:96, cols], wo[0:96, 1, :], start=False, stop=False)
                        last = T.matmul(o, nT[l][0:96, cols], wo[0:96, 2, :], start=False, stop=True)
                    last.then_inc(s_cn, 1)

                def conv_sum(w, l):
                    pe.wait_ge(s_cf, n_cv.at(M, w, l + 1))
                    sum_tiles(M, w, l, ti_at(M, "conv_sum", w, l))

                plans[M].run(pe, {"cell": cell_gates(M), "first": normed_to_cols(M), "back": back(M),
                                  "sum": message_sums, "conv_cols": conv_cols,
                                  "conv_up": conv_up, "conv_rows": conv_rows, "conv_sum": conv_sum})
                pe.wait_ge(s_tif, tin.at(M, TURNS))
                for b in range(2):
                    last = T.transpose(ti[0:ET, b * C:(b + 1) * C],
                                       part[:, :].rearrange("p (t b) -> p b t", b=2)[:, b, :], ident[:, :])
                last.then_inc(s_ti, 1)
                pe.wait_ge(s_bl, r + 1)

                def spread(w, l, use):
                    pe.wait_ge(ld_p[l], 16 * n_p.at(D, w, 2))
                    pe.wait_ge(s_tif, use)
                    for b in range(2):
                        for m in range(3):
                            last = T.matmul(ti[:, 0:G], bsum[:, m, b * C:(b + 1) * C], rm[l][:, b * G:(b + 1) * G],
                                            start=b == m == 0, stop=b == 1 and m == 2)
                    last.then_inc(s_ti, 1)

                def slot_states(w, l):
                    pe.wait_ge(ld_m[l], 16 * n_m.at(D, w, 1))
                    rows_to_cols(mm[l], ti_at(D, "first", w, l))

                if r < STEPS:
                    plans[D].run(pe, {"spread": lambda w, l: spread(w, l, ti_at(D, "spread", w, l)),
                                      "cell": cell_gates(D), "back": back(D),
                                      "first": slot_states if r else normed_to_cols(D)})
                else:
                    def sums_back(w, l):
                        pe.wait_ge(s_tif, ti_at(D, "spread", w, l, 1))
                        cols_to_rows(pf[l], to_at(D, "back", w, l))

                    plans[D].run(pe, {"spread": lambda w, l: spread(w, l, ti_at(D, "spread", w, l)), "back": sums_back})


_INS = ["x", "src", "dst", "edge_attr_3", "edge_weight", "L0_gnn_W_lin", "L0_gnn_W_ih", "L0_gnn_W_hh",
        "L0_gnn_b_ih", "L0_gnn_b_hh", "L1_gnn_W_up0", "L1_gnn_W_up1", "L1_gnn_mlp_w0", "L1_gnn_mlp_b0",
        "L1_gnn_mlp_w1", "L1_gnn_mlp_b1", "L1_gnn_mlp_w2", "L1_gnn_mlp_b2", "L1_gnn_W_out0", "L1_gnn_W_out1"]


def kernel(**inputs):
    import numpy as _np
    import concourse.bacc as _bacc
    from concourse import mybir as _mybir
    from concourse.bass_utils import run_bass_kernel_spmd as _run

    nc = _bacc.Bacc("TRN2", target_bir_lowering=False, num_devices=1)
    arrays, args = {}, []
    for name in _INS:
        a = _np.ascontiguousarray(inputs[name])
        arrays[f"in_{name}"] = a
        args.append(nc.dram_tensor(f"in_{name}", a.shape, _mybir.dt.from_np(a.dtype), kind="ExternalInput").ap())
    shape = inputs["x"].shape
    args.append(nc.dram_tensor("out_0", shape, _mybir.dt.float32, kind="ExternalOutput").ap())
    gnn_kernel(nc, *args)
    r = _run(nc, [arrays], core_ids=[0])
    return r.results[0]["out_0"]
```
